# Optimizing a Trainium2 kernel written in Bass

```python
import numpy as np
import jax
import jax.numpy as jnp

def _softmax(x, axis=-1):
    return jax.nn.softmax(x, axis=axis)

def _gelu(x):
    return jax.nn.gelu(x, approximate=True)

def _silu(x):
    return jax.nn.silu(x)

def _sigmoid(x):
    return jax.nn.sigmoid(x)

def _layernorm(x, axis=-1, eps=1e-05):
    m = jnp.mean(x, axis=axis, keepdims=True)
    v = jnp.var(x, axis=axis, keepdims=True)
    return (x - m) / jnp.sqrt(v + eps)

def _scatter_add(tgt, idx, src, axis=0):
    return tgt.at[idx].add(src)

def _segment_sum(src, seg, n):
    return jax.ops.segment_sum(src, seg, n)
kernel_name = 'mk_gps_d1_gnn_r8_572509'

def setup_inputs(seed: int=0):
    np.random.seed(seed)
    _w = jnp.asarray

    def _rec_inputs():
        import jax
        import jax.numpy as jnp
        _gk = jax.random.key(seed)
        x = -0.0003713 + 1 * jax.random.normal(jax.random.fold_in(_gk, 1), (12500, 256), jnp.float32)
        src = jax.random.randint(jax.random.fold_in(_gk, 2), (200000,), 0, 12500, jnp.int32)
        dst = jnp.minimum((12500 * jax.random.uniform(jax.random.fold_in(_gk, 3), (200000,)) ** 2.0).astype(jnp.int32), 99999)
        _o = jnp.argsort(dst, stable=True)
        src = src[_o]
        dst = dst[_o]
        edge_attr_3 = -1.09012e-05 + 0.99985 * jax.random.normal(jax.random.fold_in(_gk, 11), (200000, 3), jnp.float32)
        return (x, src, dst, edge_attr_3)
    x, src, dst, edge_attr_3 = _rec_inputs()

    def _L0_gnn_setup():
        import jax, jax.numpy as jnp
        import numpy as np
        N = 6250
        E = 50000
        IN = 256
        H = 8
        D = 32
        EF = 3
        key = jax.random.key(seed)
        ks = jax.random.split(key, 8)
        x = jax.random.normal(ks[0], (N, IN), dtype=jnp.float32)
        edge_index = jax.random.randint(ks[1], (2, E), 0, N, dtype=jnp.int64)
        edge_attr = jax.random.normal(ks[2], (E, EF), dtype=jnp.float32)
        W = jax.random.normal(ks[3], (H * D, IN), dtype=jnp.float32) * np.float32(np.sqrt(2.0 / (IN + H * D)))
        a_src = jax.random.normal(ks[4], (H, D), dtype=jnp.float32) * np.float32(np.sqrt(2.0 / (H + D)))
        a_dst = jax.random.normal(ks[5], (H, D), dtype=jnp.float32) * np.float32(np.sqrt(2.0 / (H + D)))
        edge_W = jax.random.normal(ks[6], (H * D, EF), dtype=jnp.float32) * np.float32(np.sqrt(2.0 / (EF + H * D)))
        edge_b = jnp.zeros((H * D,), dtype=jnp.float32)
        bias = jnp.zeros((H * D,), dtype=jnp.float32)
        return {'x': x, 'W': W, 'a_src': a_src, 'a_dst': a_dst, 'edge_W': edge_W, 'edge_b': edge_b, 'bias': bias, 'edge_attr': edge_attr, 'edge_index': edge_index}
    _L0_gnn_all = _L0_gnn_setup()
    _L0_gnn_in = {k: v for k, v in _L0_gnn_all.items() if k in ('W', 'a_src', 'a_dst', 'edge_W', 'edge_b', 'bias')}
    del _L0_gnn_all

    def _L0_mix_setup():
        import jax, jax.numpy as jnp
        import numpy as np
        N, F, C, H = (32, 512, 256, 8)
        D = C // H
        EPS_ATTN = 1e-06
        EPS_LN = 1e-05

        def layer_norm(x, g, b):
            mu = jnp.mean(x, axis=-1, keepdims=True)
            var = jnp.var(x, axis=-1, keepdims=True)
            return (x - mu) * jax.lax.rsqrt(var + EPS_LN) * g + b
        key = jax.random.key(seed)
        ks = jax.random.split(key, 8)
        s = 1.0 / np.sqrt(C)
        return {'x': jax.random.normal(ks[0], (N, F, C), jnp.float32), 'Wqkv': jax.random.uniform(ks[1], (3 * C, C), jnp.float32, -s, s), 'ln1_g': jnp.ones((C,), jnp.float32), 'ln1_b': jnp.zeros((C,), jnp.float32), 'W1': jax.random.uniform(ks[2], (C, C), jnp.float32, -s, s), 'b1': jax.random.uniform(ks[3], (C,), jnp.float32, -s, s), 'W2': jax.random.uniform(ks[4], (C, C), jnp.float32, -s, s), 'b2': jax.random.uniform(ks[5], (C,), jnp.float32, -s, s), 'ln2_g': jnp.ones((C,), jnp.float32), 'ln2_b': jnp.zeros((C,), jnp.float32)}
    _L0_mix_all = _L0_mix_setup()
    _L0_mix_in = {k: v for k, v in _L0_mix_all.items() if k in ('Wqkv', 'ln1_g', 'ln1_b', 'W1', 'b1', 'W2', 'b2', 'ln2_g', 'ln2_b')}
    del _L0_mix_all

    def _L0_ffn_setup():
        import math
        import jax, jax.numpy as jnp
        import numpy as np
        CAPACITY_FACTOR = 1.25
        TOP_K = 2
        LN_EPS = 1e-05

        def _layer_norm(x, gamma, beta):
            mu = jnp.mean(x, axis=-1, keepdims=True)
            var = jnp.var(x, axis=-1, keepdims=True)
            return (x - mu) * jax.lax.rsqrt(var + LN_EPS) * gamma + beta
        key = jax.random.key(seed)
        ks = jax.random.split(key, 4)
        B, S, D, F, E = (8, 512, 256, 512, 8)
        x = jax.random.normal(ks[0], (B, S, D), dtype=jnp.float32)
        Wr = jax.random.normal(ks[1], (D, E), dtype=jnp.float32) / np.sqrt(D)
        br = jnp.zeros((E,), jnp.float32)
        W1 = jax.random.normal(ks[2], (E, D, F), dtype=jnp.float32) / np.sqrt(D)
        b1 = jnp.zeros((E, F), jnp.float32)
        W2 = jax.random.normal(ks[3], (E, F, D), dtype=jnp.float32) / np.sqrt(F)
        b2 = jnp.zeros((E, D), jnp.float32)
        gamma = jnp.ones((D,), jnp.float32)
        beta = jnp.zeros((D,), jnp.float32)
        return {'x': x, 'Wr': Wr, 'br': br, 'W1': W1, 'b1': b1, 'W2': W2, 'b2': b2, 'gamma': gamma, 'beta': beta}
    _L0_ffn_all = _L0_ffn_setup()
    _L0_ffn_in = {k: v for k, v in _L0_ffn_all.items() if k in ('Wr', 'br', 'W1', 'b1', 'W2', 'b2', 'gamma', 'beta')}
    del _L0_ffn_all
    return {'x': x, 'src': src, 'dst': dst, 'edge_attr_3': edge_attr_3, 'L0_gnn_W': _L0_gnn_in['W'], 'L0_gnn_a_src': _L0_gnn_in['a_src'], 'L0_gnn_a_dst': _L0_gnn_in['a_dst'], 'L0_gnn_edge_W': _L0_gnn_in['edge_W'], 'L0_gnn_edge_b': _L0_gnn_in['edge_b'], 'L0_gnn_bias': _L0_gnn_in['bias'], 'L0_mix_Wqkv': _L0_mix_in['Wqkv'], 'L0_mix_ln1_g': _L0_mix_in['ln1_g'], 'L0_mix_ln1_b': _L0_mix_in['ln1_b'], 'L0_mix_W1': _L0_mix_in['W1'], 'L0_mix_b1': _L0_mix_in['b1'], 'L0_mix_W2': _L0_mix_in['W2'], 'L0_mix_b2': _L0_mix_in['b2'], 'L0_mix_ln2_g': _L0_mix_in['ln2_g'], 'L0_mix_ln2_b': _L0_mix_in['ln2_b'], 'L0_ffn_Wr': _L0_ffn_in['Wr'], 'L0_ffn_br': _L0_ffn_in['br'], 'L0_ffn_W1': _L0_ffn_in['W1'], 'L0_ffn_b1': _L0_ffn_in['b1'], 'L0_ffn_W2': _L0_ffn_in['W2'], 'L0_ffn_b2': _L0_ffn_in['b2'], 'L0_ffn_gamma': _L0_ffn_in['gamma'], 'L0_ffn_beta': _L0_ffn_in['beta']}

def reference(x, src, dst, edge_attr_3, L0_gnn_W, L0_gnn_a_src, L0_gnn_a_dst, L0_gnn_edge_W, L0_gnn_edge_b, L0_gnn_bias, L0_mix_Wqkv, L0_mix_ln1_g, L0_mix_ln1_b, L0_mix_W1, L0_mix_b1, L0_mix_W2, L0_mix_b2, L0_mix_ln2_g, L0_mix_ln2_b, L0_ffn_Wr, L0_ffn_br, L0_ffn_W1, L0_ffn_b1, L0_ffn_W2, L0_ffn_b2, L0_ffn_gamma, L0_ffn_beta):
    import jax
    import jax.numpy as jnp

    def _L0_gnn_ref(x, W, a_src, a_dst, edge_W, edge_b, bias, edge_attr, edge_index):
        import jax, jax.numpy as jnp
        import numpy as np
        N = 6250
        E = 50000
        IN = 256
        H = 8
        D = 32
        EF = 3
        n = x.shape[0]
        h = (x @ W.T).reshape(n, H, D)
        src, dst = (edge_index[0], edge_index[1])
        h_src = h[src]
        h_dst = h[dst]
        alpha = jnp.einsum('ehd,hd->eh', h_src, a_src) + jnp.einsum('ehd,hd->eh', h_dst, a_dst)
        enc = jax.nn.relu(edge_attr @ edge_W.T + edge_b).reshape(-1, H, D)
        alpha = alpha + jnp.sum(enc * h_dst, axis=-1)
        alpha = jnp.where(alpha >= 0, alpha, 0.2 * alpha)
        amax = jax.ops.segment_max(alpha, dst, num_segments=n)
        ex = jnp.exp(alpha - amax[dst])
        denom = jax.ops.segment_sum(ex, dst, num_segments=n)
        attn = ex / jnp.maximum(denom[dst], 1e-10)
        out = jax.ops.segment_sum(h_src * attn[..., None], dst, num_segments=n)
        return out.reshape(n, H * D) + bias

    def _L0_mix_ref(x, Wqkv, ln1_g, ln1_b, W1, b1, W2, b2, ln2_g, ln2_b):
        import jax, jax.numpy as jnp
        import numpy as np
        N, F, C, H = (32, 512, 256, 8)
        D = C // H
        EPS_ATTN = 1e-06
        EPS_LN = 1e-05

        def layer_norm(x, g, b):
            mu = jnp.mean(x, axis=-1, keepdims=True)
            var = jnp.var(x, axis=-1, keepdims=True)
            return (x - mu) * jax.lax.rsqrt(var + EPS_LN) * g + b
        n, f, c = x.shape
        qkv = jnp.einsum('nfc,oc->nfo', x, Wqkv)
        q, k, v = jnp.split(qkv, 3, axis=-1)
        q = q.reshape(n, f, H, D)
        k = k.reshape(n, f, H, D)
        v = v.reshape(n, f, H, D)
        q = jax.nn.elu(q) + 1.0
        k = jax.nn.elu(k) + 1.0
        kv = jnp.einsum('nshd,nshm->nhmd', k, v)
        ksum = jnp.sum(k, axis=1)
        z = 1.0 / (jnp.einsum('nlhd,nhd->nlh', q, ksum) + EPS_ATTN)
        t = jnp.einsum('nlhd,nhmd,nlh->nlhm', q, kv, z)
        t = t.reshape(n, f, c)
        x1 = layer_norm(t + x, ln1_g, ln1_b)
        h = jax.nn.gelu(jnp.einsum('nfc,oc->nfo', x1, W1) + b1, approximate=False)
        y = jnp.einsum('nfc,oc->nfo', h, W2) + b2
        return layer_norm(y + x1, ln2_g, ln2_b)

    def _L0_ffn_ref(x, Wr, br, W1, b1, W2, b2, gamma, beta):
        import math
        import jax, jax.numpy as jnp
        import numpy as np
        CAPACITY_FACTOR = 1.25
        TOP_K = 2
        LN_EPS = 1e-05

        def _layer_norm(x, gamma, beta):
            mu = jnp.mean(x, axis=-1, keepdims=True)
            var = jnp.var(x, axis=-1, keepdims=True)
            return (x - mu) * jax.lax.rsqrt(var + LN_EPS) * gamma + beta
        B, S, D = x.shape
        E = Wr.shape[1]
        N = B * S
        K = TOP_K
        logits = jnp.mean(x, axis=1) @ Wr + br
        routing_weights = jax.nn.softmax(logits, axis=-1)
        capacity = float(math.ceil(N * CAPACITY_FACTOR / E))
        expected_loads = routing_weights.sum(axis=0) * (N / B)
        scale = jnp.where(expected_loads > capacity, capacity / expected_loads, 1.0)
        routing_weights = jax.nn.softmax(routing_weights * scale, axis=-1)
        rw_tok = jnp.broadcast_to(routing_weights[:, None, :], (B, S, E)).reshape(N, E)
        top_w, top_i = jax.lax.top_k(rw_tok, K)
        top_w = jax.nn.softmax(top_w, axis=-1)
        xf = x.reshape(N, D)
        h = jax.nn.gelu(jnp.einsum('nd,edf->enf', xf, W1) + b1[:, None, :], approximate=False)
        y = jnp.einsum('enf,efd->end', h, W2) + b2[:, None, :]
        w_dense = jnp.zeros((N, E), x.dtype).at[jnp.arange(N)[:, None], top_i].add(top_w)
        out = jnp.einsum('ne,end->nd', w_dense, y).reshape(B, S, D)
        out = _layer_norm(out + x, gamma, beta)
        return out
    edge_index = jnp.stack([src, dst])
    xn = _layernorm(x, axis=-1)
    x = x + _L0_gnn_ref(xn, L0_gnn_W, L0_gnn_a_src, L0_gnn_a_dst, L0_gnn_edge_W, L0_gnn_edge_b, L0_gnn_bias, edge_attr_3, edge_index) + _L0_mix_ref(xn[None], L0_mix_Wqkv, L0_mix_ln1_g, L0_mix_ln1_b, L0_mix_W1, L0_mix_b1, L0_mix_W2, L0_mix_b2, L0_mix_ln2_g, L0_mix_ln2_b)[0]
    x = x + _L0_ffn_ref(_layernorm(x, axis=-1)[None], L0_ffn_Wr, L0_ffn_br, L0_ffn_W1, L0_ffn_b1, L0_ffn_W2, L0_ffn_b2, L0_ffn_gamma, L0_ffn_beta)[0]
    return x

_drawn_inputs = setup_inputs


def setup_inputs(seed=0):
    import zlib

    import numpy as np

    out = dict(_drawn_inputs(seed))
    spreads = {'L0_gnn_edge_b': (0.0, 0.1),
     'L0_gnn_bias': (0.0, 0.1),
     'L0_mix_ln1_g': (1.0, 0.2),
     'L0_mix_ln1_b': (0.0, 0.1),
     'L0_mix_ln2_g': (1.0, 0.2),
     'L0_mix_ln2_b': (0.0, 0.1),
     'L0_ffn_br': (0.0, 0.1),
     'L0_ffn_b1': (0.0, 0.567),
     'L0_ffn_b2': (0.0, 0.383),
     'L0_ffn_gamma': (1.0, 0.2),
     'L0_ffn_beta': (0.0, 0.1)}
    factors = {'L0_mix_Wqkv': 8.0, 'L0_mix_b1': 8.0, 'L0_mix_b2': 3.288, 'L0_ffn_Wr': 8.0}
    for name, (base, spread) in spreads.items():
        noise = np.random.default_rng([zlib.crc32(name.encode()), seed]).standard_normal(out[name].shape)
        drawn = base * np.exp(spread * noise) if base else spread * noise
        out[name] = jnp.asarray(drawn.astype(out[name].dtype))
    for name, factor in factors.items():
        out[name] = (out[name] * factor).astype(out[name].dtype)
    return out
```

```python
import concourse.bass as bass
from concourse import mybir
from contextlib import ExitStack

F32 = mybir.dt.float32
I32 = mybir.dt.int32
U32 = mybir.dt.uint32
F32R = mybir.dt.float32r
ALU = mybir.AluOpType
ACT = mybir.ActivationFunctionType
AX = mybir.AxisListType

P = 128
N = 12500
C = 256
H = 8
D = C // H
KC = C // P
NW = -(-N // P)
NP = NW * P
E = 200000
EF = 4
CH = 16
TC = -(-E // (P * CH))
T = TC * CH
EP = T * P
CE = TC * P
GA = 4
GB = 2
BIG = 1.0e30
XP = 8
FF = 512
TOPW = N
CAPACITY = float(-(-N * 5 // (4 * XP)))
LN_EPS = 1e-5




def step_count(tiles):
    return -(-(T // tiles + NW - 1) // UE) * UE


UE = 4
UN = 2
SA = step_count(GA)
SB = step_count(GB)


def run(eng, count, unroll, body, tail=0):
    for s in range(unroll):
        body(s, s, 0)
    turns = (count - unroll - tail) // unroll
    with eng.Fori(0, turns) as it:
        for k in range(unroll):
            body(it * unroll + (unroll + k), k, it + 1)
    for s in range((turns + 1) * unroll, count):
        body(s, s % unroll, turns + 1)


def since(s, n):
    return not isinstance(s, int) or s >= n


class Link:

    def __init__(self, eng, sem, s=0, each=0):
        self.eng, self.sem, self.base, self.each, self.n = eng, sem, s * each, each, 0

    def __call__(self, ins):
        ins.then_inc(self.sem, 1)
        self.n += 1
        assert not self.each or self.n <= self.each, (self.n, self.each)
        self.eng.wait_ge(self.sem, self.base + self.n)


class Phase:

    def __init__(self, nc, name):
        self.nc, self.name, self.ctx = nc, name, ExitStack()

    def __enter__(self):
        self.ctx.__enter__()
        return self

    def __exit__(self, *a):
        return self.ctx.__exit__(*a)

    def sb(self, name, shape, dt=F32):
        return self.ctx.enter_context(self.nc.sbuf_tensor(f"{self.name}_{name}", shape, dt))

    def ps(self, name, shape, dt=F32):
        return self.ctx.enter_context(self.nc.psum_tensor(f"{self.name}_{name}", shape, dt))

    def sem(self, name):
        return self.ctx.enter_context(self.nc.semaphore(f"{self.name}_{name}"))

    def sems(self, name, n):
        return [self.sem(f"{name}{k}") for k in range(n)]


def pool_rstd(nc, link, var, const, rstd):
    link(nc.gpsimd.tensor_tensor(rstd, var, const[:, 1:2], ALU.add))
    return nc.gpsimd.tensor_tensor(rstd, rstd, const[:, 0:1], ALU.pow)


def rows(dram, i, n=P):
    return dram[bass.ds(i * n, n), :]


def fold_attention_weights(nc, t, r):
    with Phase(nc, "fold") as f:
        w_nat = f.sb("w_nat", [P, KC, C])
        a_col = f.sb("a_col", [P, KC, 2])
        a_diag = f.sb("a_diag", [P, KC, 2, H])
        wa = f.ps("wa", [P, KC, 2 * H])
        loaded, diag_ready, wa_ready, done = (f.sem(s) for s in ("loaded", "diag", "wa", "done"))
        block = f.ctx.enter_context(nc.Block())

        @block.sync
        def _(sp):
            sp.dma_start(r.ident[:, :], t["c_ident"]).then_inc(loaded, 16)
            sp.dma_start(r.jrow[:, :], t["c_jrow"]).then_inc(loaded, 16)
            sp.dma_start(r.jcol[:, :], t["c_jcol"]).then_inc(loaded, 16)
            sp.dma_start(r.headsel[:, :], t["c_headsel"]).then_inc(loaded, 16)
            sp.dma_start(r.valid[:, :], t["c_valid"]).then_inc(loaded, 16)
            sp.dma_start(r.wall[:, :, 0:C], t["wT"].rearrange("(k p) n -> p k n", p=P)).then_inc(loaded, 16)
            sp.dma_start(w_nat[:, :, :], t["w"].rearrange("(k p) n -> p k n", p=P)).then_inc(loaded, 16)
            sp.dma_start(a_col[:, :, :], t["a_col"].rearrange("(k p) n -> p k n", p=P)).then_inc(loaded, 16)
            sp.wait_ge(loaded, 8 * 16)

        @block.vector
        def _(dve):
            dve.wait_ge(loaded, 8 * 16)
            for k in range(KC):
                for side in range(2):
                    nc.vector.tensor_scalar(a_diag[:, k, side, :], r.headsel[:, k * H:(k + 1) * H],
                                            a_col[:, k, side:side + 1], None, ALU.mult).then_inc(diag_ready, 1)
            dve.wait_ge(wa_ready, 1)
            nc.vector.tensor_copy(r.wall[:, :, C:C + 2 * H], wa[:, :, :]).then_inc(done, 1)

        @block.tensor
        def _(pe):
            pe.wait_ge(diag_ready, 4)
            for k in range(KC):
                for j in range(KC):
                    last = nc.tensor.matmul(wa[:, k, :], w_nat[:, j, k * P:(k + 1) * P], a_diag[:, j, :, :],
                                            start=(j == 0), stop=(j == KC - 1))
            last.then_inc(wa_ready, 1)


def make_steps(nc, t, r, ph, tiles, count, last_dst, gcol_dram):
    groups = T // tiles
    chunks = groups // NW
    half = count // 2
    with Phase(nc, f"steps{tiles}") as f:
        raw = f.sb("raw", [NW, chunks], I32)
        win = f.sb("win", [NW, chunks], I32)
        winf = f.sb("winf", [NW, chunks])
        gcol = f.sb("gcol", [NW, chunks])
        start = f.sb("start", [NW, chunks])
        sidx = f.sb("sidx", [P, count])
        begun = f.sb("begun", [NW, chunks, count])
        ones = f.sb("ones", [NW, P])
        gs = f.sb("gs", [P, count])
        ws = f.sb("ws", [P, count])
        wc = f.sb("wc", [P, count])
        acc = f.ps("acc", [P, 2, 512])
        loaded, link_s, begun_s, acc_s = (f.sem(s) for s in ("loaded", "link", "begun", "acc"))
        block = f.ctx.enter_context(nc.Block())

        @block.sync
        def _(sp):
            sp.dma_start(raw[:, :], last_dst).then_inc(loaded, 16)
            sp.dma_start(sidx[:, :], t["c_sidx"][:, 0:count]).then_inc(loaded, 16)
            sp.dma_start(gcol[:, :], gcol_dram).then_inc(loaded, 16)
            sp.wait_ge(loaded, 48)

        @block.vector
        def _(dve):
            link = Link(dve, link_s)
            dve.wait_ge(loaded, 48)
            link(nc.vector.memset(ones[:, :], 1.0))
            link(nc.vector.tensor_scalar(win[:, :], raw[:, :], 7, None, ALU.arith_shift_right))
            link(nc.vector.tensor_copy(winf[:, :], win[:, :]))
            link(nc.vector.tensor_tensor(start[:, :], winf[:, :], gcol[:, :], ALU.add))
            for c in range(chunks):
                nc.vector.tensor_scalar(begun[:, c, :], sidx[0:NW, :], start[:, c:c + 1], None,
                                        ALU.is_ge).then_inc(begun_s, 1)
            dve.wait_ge(acc_s, 1)
            for a in range(2):
                link(nc.vector.tensor_scalar(gs[:, a * half:(a + 1) * half], acc[:, a, 0:half],
                                             float(groups - 1), None, ALU.min))
            link(nc.vector.tensor_tensor(ws[:, :], sidx[:, :], gs[:, :], ALU.subtract))
            link(nc.vector.tensor_scalar(wc[:, :], ws[:, :], float(NW - 1), None, ALU.min))
            link(nc.vector.tensor_copy(ph.g_int[:, :], gs[:, :]))
            link(nc.vector.tensor_copy(ph.w_int[:, :], wc[:, :]))
            link(nc.vector.tensor_scalar(ph.w_node[:, :], ws[:, :], float(P), None, ALU.mult))
            if ph.j_node is not None:
                link(nc.vector.tensor_scalar(ph.j_node[:, :], ph.w_node[:, :], r.jcol[:, 0:1], None, ALU.add))

        @block.tensor
        def _(pe):
            pe.wait_ge(begun_s, chunks)
            for a in range(2):
                for c in range(chunks):
                    last = nc.tensor.matmul(acc[:, a, 0:half], ones[:, :], begun[:, c, a * half:(a + 1) * half],
                                            start=(c == 0), stop=(c == chunks - 1))
            last.then_inc(acc_s, 1)


def node_pass(nc, t, r):
    with Phase(nc, "node") as f:
        wqkv = f.sb("wqkv", [P, KC, 3 * C])
        x = f.sb("x", [P, UN, C])
        st = f.sb("st", [P, UN, 6])
        mv = f.sb("mv", [P, UN, 2])
        rstd = f.sb("rstd", [P, UN])
        xn = f.sb("xn", [P, UN, C])
        xnT = f.sb("xnT", [P, UN, KC * P])
        h = f.sb("h", [P, UN, C + 2 * H])
        hsp = f.sb("hsp", [P, UN, 2, C + H], F32R)
        neg = f.sb("neg", [P, UN, 2, C])
        ex = f.sb("ex", [P, UN, 2, C])
        q = f.sb("q", [P, UN, C])
        k = f.sb("k", [P, UN, C])
        v = f.sb("v", [P, UN, KC, P + 1])
        zero = f.sb("zero", [P, P])
        p_tq = f.ps("p_tq", [P, UN, 2, C])
        p_h = f.ps("p_h", [P, UN, 512])
        p_kv = f.ps("p_kv", [P, UN, 2, C])
        p_sum = f.ps("p_sum", [P, KC, P + 1])
        x_in = f.sems("x_in", UN)
        stored = f.sems("stored", UN)
        (w_in, xn_ready, xT_ready, xT_sb, mm_ready, h_sb, neg_s, exp_s, q_sb, k_s, v_s, kv_used, link_s, zero_s,
         sum_s) = (f.sem(s) for s in (
             "w_in", "xn_ready", "xT_ready", "xT_sb", "mm_ready", "h_sb", "neg", "exp", "q_sb", "k", "v", "kv_used",
             "link", "zero", "sum"))
        hold_s = f.sem("hold")
        h_hi_s, h_lo_s = f.sem("h_hi"), f.sem("h_lo")
        pconst = f.sb("pconst", [P, 2])
        var_s, rstd_s, plink_s, half_s = (f.sem(s) for s in ("var", "rstd", "plink", "half"))
        block = f.ctx.enter_context(nc.Block())

        @block.sync
        def _(sp):
            sp.dma_start(wqkv[:, :, :], t["wqkvT"].rearrange("(k p) n -> p k n", p=P)).then_inc(w_in, 16)
            sp.dma_start(r.headmask[:, :], t["c_headmask"]).then_inc(w_in, 16)
            for u in range(UN):
                sp.dma_start(x[:, u, :], t["x"][u * P:(u + 1) * P, :]).then_inc(x_in[u], 16)

            def body(i, u, turn):
                sp.wait_ge(xn_ready, i + 1)
                sp.dma_start(x[:, u, :], t["x"][bass.ds((i + UN) * P, P), :]).then_inc(x_in[u], 16)
                sp.dma_start(rows(t["d_xn"], i), xn[:, u, :]).then_inc(stored[u], 16)
                sp.wait_ge(h_lo_s, i + 1)
                sp.dma_start(rows(t["d_hw"], i), hsp[:, u, :, :].rearrange("p a c -> p (a c)").bitcast(F32)).then_inc(stored[u], 16)
                sp.dma_start(rows(t["d_h"], i), h[:, u, 0:C]).then_inc(stored[u], 16)
                sp.dma_start(rows(t["d_as"], i), h[:, u, C + H:C + 2 * H]).then_inc(stored[u], 16)
                sp.wait_ge(q_sb, i + 1)
                sp.dma_start(t["d_q"][:, bass.ds(i * C, C)], q[:, u, :]).then_inc(stored[u], 16)

            run(sp, NW, UN, body)
            for u in range(UN):
                sp.wait_ge(x_in[u], 16 * (NW // UN + 1))
                sp.wait_ge(stored[u], 80 * (NW // UN))

        @block.vector
        def _(dve):
            nc.vector.memset(zero[:, :], 0.0).then_inc(zero_s, 1)

            def body(i, u, turn):
                link = Link(dve, link_s, i, 1)
                dve.wait_ge(x_in[u], turn * 16 + 16)
                link(nc.vector.bn_stats(st[:, u, :], x[:, u, :]))
                dve.sem_inc(hold_s, 1)
                nc.vector.bn_aggr(mv[:, u, :], st[:, u, :]).then_inc(var_s, 1)
                dve.wait_ge(rstd_s, i + 1)
                if since(i, UN):
                    dve.wait_ge(stored[u], turn * 80)
                nc.vector.tensor_scalar(xn[:, u, :], x[:, u, :], mv[:, u, 0:1], rstd[:, u:u + 1],
                                        ALU.subtract, ALU.mult).then_inc(xn_ready, 1)
                dve.wait_ge(mm_ready, i + 1)
                nc.vector.tensor_scalar(neg[:, u, 0, :], p_kv[:, u, 0, :], 0.0, None, ALU.min)
                nc.vector.tensor_scalar(neg[:, u, 1, :], p_tq[:, u, 1, :], 0.0, None, ALU.min).then_inc(neg_s, 1)
                nc.vector.tensor_copy(h[:, u, :], p_h[:, u, 0:C + 2 * H]).then_inc(h_sb, 1)
                dve.wait_ge(h_hi_s, i + 1)
                nc.vector.tensor_tensor(hsp[:, u, 1, :], h[:, u, 0:C + H], hsp[:, u, 0, :].bitcast(F32),
                                        ALU.subtract).then_inc(h_lo_s, 1)
                dve.wait_ge(exp_s, i + 1)
                nc.vector.scalar_tensor_tensor(q[:, u, :], p_tq[:, u, 1, :], 0.0, ex[:, u, 1, :],
                                               ALU.max, ALU.add).then_inc(q_sb, 1)
                if since(i, UN):
                    dve.wait_ge(kv_used, i - 1)
                nc.vector.tensor_copy(v[:, u, :, P], r.valid[:, bass.ds(i, 1)].broadcast_to([P, KC]))
                nc.vector.scalar_tensor_tensor(k[:, u, :], p_kv[:, u, 0, :], 0.0, ex[:, u, 0, :],
                                               ALU.max, ALU.add).then_inc(k_s, 1)

            run(dve, NW, UN, body)
            dve.wait_ge(sum_s, 1)
            for c in range(KC):
                nc.vector.tensor_tensor(r.kvbd[:, c, 0:P], p_sum[:, c, 0:P], r.headmask[:, :], ALU.mult).then_inc(link_s, 1)
                nc.vector.tensor_scalar(r.kvbd[:, c, P:P + 4], r.headsel[:, 0:4], p_sum[:, c, P:P + 1], None,
                                        ALU.mult).then_inc(link_s, 1)

        @block.gpsimd
        def _(pool):
            nc.gpsimd.memset(pconst[:, 0:1], -0.5).then_inc(half_s, 1)
            nc.gpsimd.memset(pconst[:, 1:2], LN_EPS).then_inc(half_s, 1)
            pool.wait_ge(half_s, 2)

            def body(i, u, turn):
                pool.wait_ge(var_s, i + 1)
                pool_rstd(nc, Link(pool, plink_s, i, 1), mv[:, u, 1:2], pconst, rstd[:, u:u + 1]).then_inc(rstd_s, 1)

            run(pool, NW, 2, body)

        @block.scalar
        def _(act):
            def body(i, u, turn):
                act.wait_ge(xT_ready, i + 1)
                nc.scalar.copy(xnT[:, u, :], p_tq[:, u, 0, :]).then_inc(xT_sb, 1)
                act.wait_ge(h_sb, i + 1)
                nc.scalar.copy(hsp[:, u, 0, :], h[:, u, 0:C + H]).then_inc(h_hi_s, 1)
                act.wait_ge(neg_s, i + 1)
                if since(i, UN):
                    act.wait_ge(kv_used, i - 1)
                nc.scalar.copy(v[:, u, :, 0:P], p_kv[:, u, 1, :].rearrange("p (c n) -> p c n", c=KC)).then_inc(v_s, 1)
                act.wait_ge(v_s, i + 1)
                nc.scalar.activation(ex[:, u, :, :], neg[:, u, :, :], ACT.Exp).then_inc(exp_s, 1)

            run(act, NW, UN, body)

        @block.tensor
        def _(pe):
            pe.wait_ge(w_in, 32)
            pe.wait_ge(zero_s, 1)
            for c in range(KC):
                nc.tensor.matmul(p_sum[:, c, :], zero[:, :], wqkv[:, 0, 0:P + 1], start=(c == 0), stop=False,
                                 skip_group_check=True)

            def body(i, u, turn):
                pe.wait_ge(xn_ready, i + 1)
                if since(i, UN):
                    pe.wait_ge(q_sb, i - 1)
                for c in range(KC):
                    last = nc.tensor.transpose(p_tq[:, u, 0, c * P:(c + 1) * P], xn[:, u, c * P:(c + 1) * P],
                                               r.ident[:, :])
                last.then_inc(xT_ready, 1)
                if since(i, 1):
                    sums(i - 1, (u - 1) % UN)
                pe.wait_ge(xT_sb, i + 1)
                if since(i, UN):
                    pe.wait_ge(h_sb, i - 1)
                    pe.wait_ge(v_s, i - 1)
                for c in range(KC):
                    nc.tensor.matmul(p_h[:, u, 0:C + 2 * H], xnT[:, u, c * P:(c + 1) * P], r.wall[:, c, :],
                                     start=(c == 0), stop=(c == KC - 1))
                for c in range(KC):
                    nc.tensor.matmul(p_kv[:, u, :, :], xnT[:, u, c * P:(c + 1) * P], wqkv[:, c, C:3 * C],
                                     start=(c == 0), stop=(c == KC - 1))
                for o in range(KC):
                    for c in range(KC):
                        last = nc.tensor.matmul(p_tq[:, u, 1, o * P:(o + 1) * P], wqkv[:, c, o * P:(o + 1) * P],
                                                xnT[:, u, c * P:(c + 1) * P], start=(c == 0), stop=(c == KC - 1))
                last.then_inc(mm_ready, 1)

            def sums(i, u):
                pe.wait_ge(k_s, i + 1)
                pe.wait_ge(v_s, i + 1)
                for c in range(KC):
                    last = nc.tensor.matmul(p_sum[:, c, :], k[:, u, c * P:(c + 1) * P], v[:, u, c, :],
                                            start=False, stop=False, skip_group_check=True)
                last.then_inc(kv_used, 1)

            run(pe, NW, UN, body)
            sums(NW - 1, (NW - 1) % UN)
            for c in range(KC):
                last = nc.tensor.matmul(p_sum[:, c, :], zero[:, :], wqkv[:, 0, 0:P + 1], start=False, stop=True,
                                        skip_group_check=True)
            last.then_inc(sum_s, 1)


def edge_scores(nc, t, r, ph):
    W = GA * P
    CX = C + H
    with Phase(nc, "score") as f:
        hw = f.sb("hw", [P, UE, 2, CX], F32R)
        dstb = f.sb("dstb", [P, UE, W], I32)
        ea = f.sb("ea", [3 * EF, UE, W], F32R)
        mt = f.sb("mt", [P, UE, W], F32R)
        rel = f.sb("rel", [P, 2, 2 * C])
        pr = f.sb("pr", [P, 2, 2 * C])
        red = f.sb("red", [P, 2, GA * H])
        ew = f.sb("ew", [3 * EF, C], F32R)
        sring = f.sb("sring", [P, 2, GA], U32)
        gring = f.sb("gring", [P, 2, GA, H])
        p_enc = f.ps("p_enc", [P, 2, 2 * C])
        p_hd = f.ps("p_hd", [P, 2, 2 * C])
        p_ad = f.ps("p_ad", [P, 2, 512])
        ins = f.sems("ins", UE)
        gat = f.sems("gat", 2)
        w_in, mt_s, enc_s, hd_s, rel_s, pr_s, red_s, add_s, turn_s, ring_s, out_s, link_s = (
            f.sem(s) for s in ("w_in", "mt", "enc", "hd", "rel", "pr", "red", "add", "turn", "ring", "out", "link"))
        block = f.ctx.enter_context(nc.Block())
        PAIRS = GA // 2

        @block.sync
        def _(sp):
            sp.dma_start(ew[:, :].bitcast(F32), t["d_ew"]).then_inc(w_in, 16)

            def body(s, u, turn):
                if since(s, UE):
                    sp.wait_ge(hd_s, (s - UE) * PAIRS + PAIRS)
                g = sp.value_load(ph.g_int[0:1, bass.ds(s, 1)], min_val=0, max_val=T // GA - 1)
                w = sp.value_load(ph.w_int[0:1, bass.ds(s, 1)], min_val=0, max_val=NW - 1)
                sp.dma_start(hw[:, u, :, :].bitcast(F32), rows(t["d_hw"], w).rearrange("p (a c) -> p a c", a=2)).then_inc(ins[u], 16)
                sp.dma_start(dstb[:, u, :], t["dst_row"][:, bass.ds(g * W, W)].broadcast_to([P, W])).then_inc(ins[u], 16)
                sp.dma_start(ea[:, u, :].bitcast(F32), t["d_ea"][:, bass.ds(g * W, W)]).then_inc(ins[u], 16)

            run(sp, SA, UE, body)
            for u in range(UE):
                sp.wait_ge(ins[u], 48 * (SA // UE))

        @block.gpsimd
        def _(pool):
            def take(i, u, turn):
                pool.wait_ge(gat[u], turn * (16 * GA) + 16 * GA)
                nc.gpsimd.tensor_copy(ph.asrc[:, bass.ds(i * (GA * H), GA * H)],
                                      gring[:, u, :, :].rearrange("p k h -> p (k h)")).then_inc(out_s, 1)

            def body(i, u, turn):
                if since(i, 2):
                    take(i - 2, u, turn - 1)
                    pool.wait_ge(out_s, i - 1)
                nc.gpsimd.tensor_copy(sring[:, u, :], r.src[:, bass.ds(i * GA, GA)]).then_inc(ring_s, 1)
                pool.wait_ge(ring_s, i + 1)
                pool.sem_inc(turn_s, 1)
                for k in range(GA):
                    nc.gpsimd.indirect_dma_start(gring[:, u, k, :], None, t["d_as"][:, :],
                                                 bass.IndirectOffsetOnAxis(sring[:, u, k:k + 1], 0)).then_inc(gat[u], 16)

            n = T // GA
            run(pool, n, 2, body)
            for i in (n - 2, n - 1):
                take(i, i % 2, i // 2)

        @block.vector
        def _(dve):
            nc.vector.memset(ph.al[:, :], 0.0).then_inc(add_s, 1)

            def onehot(s, u, turn):
                dve.wait_ge(ins[u], turn * 48 + 48)
                nc.vector.tensor_scalar(mt[:, u, :], dstb[:, u, :], ph.j_node[:, bass.ds(s, 1)], None,
                                        ALU.is_equal).then_inc(mt_s, 1)

            def body(s, u, turn):
                v = u % 2
                link = Link(dve, link_s, s, 1)
                g = dve.value_load(ph.g_int[0:1, bass.ds(s, 1)], min_val=0, max_val=T // GA - 1)
                if not isinstance(s, int) or s < SA - 1:
                    onehot(s + 1, (u + 1) % UE, turn + (u == UE - 1))
                for p in range(PAIRS):
                    m = s * PAIRS + p
                    dve.wait_ge(hd_s, m + 1)
                    dve.wait_ge(rel_s, m + 1)
                    if since(s, 1):
                        dve.wait_ge(red_s, m - 1)
                    nc.vector.tensor_tensor(pr[:, p, :], rel[:, p, :], p_hd[:, p, :], ALU.mult).then_inc(pr_s, 1)
                for p in range(PAIRS):
                    m = s * PAIRS + p
                    dve.wait_ge(pr_s, m + 1)
                    nc.vector.tensor_reduce(red[:, v, p * 2 * H:(p + 1) * 2 * H],
                                            pr[:, p, :].rearrange("p (h d) -> p h d", d=D), AX.X, ALU.add).then_inc(red_s, 1)
                dve.wait_ge(red_s, s * PAIRS + PAIRS)
                link(nc.vector.tensor_tensor(red[:, v, :], red[:, v, :], p_ad[:, v, 0:GA * H], ALU.add))
                dve.wait_ge(add_s, s + 1)
                sl = ph.al[:, bass.ds(g * (GA * H), GA * H)]
                nc.vector.tensor_tensor(sl, sl, red[:, v, :], ALU.add).then_inc(add_s, 1)

            onehot(0, 0, 0)
            run(dve, SA, UE, body, tail=1)

        @block.scalar
        def _(act):
            def body(s, u, turn):
                for p in range(PAIRS):
                    m = s * PAIRS + p
                    act.wait_ge(enc_s, m + 1)
                    if since(s, 1):
                        act.wait_ge(pr_s, m - 1)
                    nc.scalar.activation(rel[:, p, :], p_enc[:, p, :], ACT.Relu).then_inc(rel_s, 1)

            run(act, SA, UE, body)

        @block.tensor
        def _(pe):
            pe.wait_ge(w_in, 16)

            def body(s, u, turn):
                v = u % 2
                pe.wait_ge(ins[u], turn * 48 + 48)
                pe.wait_ge(mt_s, s + 1)
                for p in range(PAIRS):
                    m = s * PAIRS + p
                    if since(s, 1):
                        pe.wait_ge(rel_s, m - 1)
                    for k in range(2):
                        e = slice((2 * p + k) * P, (2 * p + k + 1) * P)
                        last = nc.tensor.matmul(p_enc[:, p, k * C:(k + 1) * C], ea[:, u, e], ew[:, :],
                                                start=True, stop=True)
                    last.then_inc(enc_s, 1)
                    if since(s, 1):
                        pe.wait_ge(pr_s, m - 1)
                    if p == 0 and since(s, 2):
                        pe.wait_ge(add_s, s)
                    for k in range(2):
                        e = slice((2 * p + k) * P, (2 * p + k + 1) * P)
                        for part in range(2):
                            nc.tensor.matmul(p_hd[:, p, k * C:(k + 1) * C], mt[:, u, e], hw[:, u, part, 0:C],
                                             start=(part == 0), stop=(part == 1))
                        for part in range(2):
                            last = nc.tensor.matmul(p_ad[:, v, (2 * p + k) * H:(2 * p + k + 1) * H], mt[:, u, e],
                                                    hw[:, u, part, C:CX], start=(part == 0), stop=(part == 1))
                    last.then_inc(hd_s, 1)

            run(pe, SA, UE, body)


def edge_softmax(nc, t, r, ph):
    by_block = lambda x, b: x[:, 0:T * H].rearrange("p (c b h) -> p c b h", c=CH, h=H)[:, :, bass.ds(b, 1), :] \
        .rearrange("p c b h -> p c (b h)")
    pen, db, ex = ph.al, ph.asrc, ph.al
    PIECE = CE // 8
    with Phase(nc, "soft") as f:
        a = f.sb("a", [P, CE])
        slot = f.sb("slot", [P, 2, P])
        back = f.sb("back", [P, 2, P])
        trash = f.sb("trash", [P, 2, PIECE])
        ends = f.sb("ends", [P, 2])
        srow = f.sb("srow", [1, 2, P])
        crow = f.sb("crow", [1, P + H])
        carry = f.sb("carry", [P, 1])
        one = f.sb("one", [1, 1])
        p_a = f.ps("p_a", [P, 2, 512])
        p_e = f.ps("p_e", [P, 2, 512])
        p_row = f.ps("p_row", [1, 2, P])
        p_c = f.ps("p_c", [P, 1])

        link_s, slot_s, turned, got = (f.sem(s) for s in ("t_link", "t_slot", "t_turned", "t_got"))
        with nc.Block() as block:
            @block.vector
            def _(dve):
                def body(b, u, turn):
                    link = Link(dve, link_s, b, 1)
                    o = slot[:, u, :].rearrange("p (c h) -> p c h", h=H)
                    if since(b, 2):
                        dve.wait_ge(turned, b - 1)
                    link(nc.vector.tensor_tensor(o, by_block(ph.al, b), by_block(ph.asrc, b), ALU.add))
                    nc.vector.scalar_tensor_tensor(slot[:, u, :], slot[:, u, :], 0.2, slot[:, u, :],
                                                   ALU.mult, ALU.max).then_inc(slot_s, 1)

                run(dve, TC, 2, body)

            @block.tensor
            def _(pe):
                def body(b, u, turn):
                    pe.wait_ge(slot_s, b + 1)
                    if since(b, 2):
                        pe.wait_ge(got, b - 1)
                    nc.tensor.transpose(p_a[:, u, 0:P], slot[:, u, :], r.ident[:, :]).then_inc(turned, 1)

                run(pe, TC, 2, body)

            @block.scalar
            def _(act):
                def body(b, u, turn):
                    act.wait_ge(turned, b + 1)
                    nc.scalar.copy(a[:, bass.ds(b * P, P)], p_a[:, u, 0:P]).then_inc(got, 1)

                run(act, TC, 2, body)

        dst_in, link_s, rows_s, row_ps, carry_ps, crow_s = (
            f.sem(s) for s in ("dst_in", "s_link", "s_rows", "s_row_ps", "s_carry_ps", "s_crow"))
        with nc.Block() as block:
            @block.sync
            def _(sp):
                for c in range(CH):
                    sp.dma_start(db[c * H:(c + 1) * H, 0:CE + 2].bitcast(I32),
                                 t["dst_ext"][0:1, c * CE:c * CE + CE + 2].broadcast_to([H, CE + 2])).then_inc(dst_in, 16)
                sp.wait_ge(dst_in, 16 * CH)

            @block.vector
            def _(dve):
                link = Link(dve, link_s)
                dve.wait_ge(dst_in, 16 * CH)
                di = db[:, :].bitcast(I32)
                link(nc.vector.memset(one[:, :], 1.0))
                link(nc.vector.tensor_tensor(pen[:, 0:CE + 1], di[:, 0:CE + 1], di[:, 1:CE + 2], ALU.not_equal))
                link(nc.vector.tensor_scalar(pen[:, 0:CE + 1], pen[:, 0:CE + 1], -BIG, None, ALU.mult))

                def sweep(data, out, shift, reverse, n):
                    step = slice(None, None, -1) if reverse else slice(None)
                    state = -BIG
                    for j in (range(7, -1, -1) if reverse else range(8)):
                        a0 = j * PIECE
                        o = trash[:, j % 2, :]
                        link(nc.vector.tensor_tensor_scan(o[:, step], pen[:, shift + a0:shift + a0 + PIECE][:, step],
                                                          data[:, a0:a0 + PIECE][:, step], state, ALU.add, ALU.max))
                        state = o[:, 0:1] if reverse else o[:, PIECE - 1:PIECE]
                    link(nc.vector.tensor_copy(ends[:, 0:1], state))
                    link(nc.vector.tensor_reduce(ends[:, 1:2], pen[:, shift:shift + CE], AX.X, ALU.min))
                    nc.vector.memset(crow[:, :], -BIG).then_inc(rows_s, 1)
                    dve.wait_ge(rows_s, n)
                    dve.wait_ge(row_ps, n)
                    link(nc.vector.tensor_copy(srow[:, :, :], p_row[:, :, :]))
                    for h in range(H):
                        own = srow[:, 0, h:P:H][:, step]
                        through = srow[:, 1, h:P:H][:, step]
                        o = (crow[:, h:P:H] if reverse else crow[:, h + H:P + H:H])[:, step]
                        link(nc.vector.tensor_tensor_scan(o, through, own, -BIG, ALU.add, ALU.max))
                    dve.sem_inc(crow_s, 1)
                    dve.wait_ge(carry_ps, n)
                    link(nc.vector.tensor_copy(carry[:, :], p_c[:, :]))
                    link(nc.vector.tensor_tensor_scan(out[:, 0:CE][:, step], pen[:, shift:shift + CE][:, step],
                                                      data[:, 0:CE][:, step], carry[:, 0:1], ALU.add, ALU.max))

                sweep(a, db, 0, False, 1)
                sweep(db, db, 1, True, 2)
                link(nc.vector.tensor_tensor(a[:, :], a[:, :], db[:, 0:CE], ALU.subtract))

            @block.tensor
            def _(pe):
                for n in (1, 2):
                    pe.wait_ge(rows_s, n)
                    for k in range(2):
                        last = nc.tensor.transpose(p_row[:, k, :], ends[:, k:k + 1], r.ident[:, :])
                    last.then_inc(row_ps, 1)
                    pe.wait_ge(crow_s, n)
                    off = 0 if n == 1 else H
                    nc.tensor.matmul(p_c[:, :], crow[:, off:off + P], one[:, :], start=True, stop=True).then_inc(carry_ps, 1)

        exp_s, turned, got = (f.sem(s) for s in ("e_exp", "e_turned", "e_got"))
        with nc.Block() as block:
            @block.scalar
            def _(act):
                def body(b, u, turn):
                    if since(b, 2):
                        act.wait_ge(turned, b - 1)
                    nc.scalar.activation(back[:, u, :], a[:, bass.ds(b * P, P)], ACT.Exp).then_inc(exp_s, 1)

                run(act, TC, 2, body)

            @block.tensor
            def _(pe):
                def body(b, u, turn):
                    pe.wait_ge(exp_s, b + 1)
                    if since(b, 2):
                        pe.wait_ge(got, b - 1)
                    nc.tensor.transpose(p_e[:, u, 0:P], back[:, u, :], r.ident[:, :]).then_inc(turned, 1)

                run(pe, TC, 2, body)

            @block.vector
            def _(dve):
                def body(b, u, turn):
                    dve.wait_ge(turned, b + 1)
                    nc.vector.tensor_copy(by_block(ex, b), p_e[:, u, 0:P].rearrange("p (c h) -> p c h", h=H)).then_inc(got, 1)

                run(dve, TC, 2, body)


def edge_sums(nc, t, r, ph, ex, acc):
    CX = C + H
    with Phase(nc, "sum") as f:
        sring = f.sb("sring", [P, UE, GB], U32)
        hg = f.sb("hg", [P, UE, GB, C])
        x = f.sb("x", [P, 2, GB, CX])
        dc = f.sb("dc", [P, 2, GB])
        mm = f.sb("mm", [P, 2, GB, P])
        p_o = f.ps("p_o", [P, 2, 512])
        gat = f.sems("gat", UE)
        ring_s, turn_s, x_s, m_s, o_s, acc_s, link_s = (
            f.sem(s) for s in ("ring", "turn", "x", "m", "o", "acc", "link"))
        block = f.ctx.enter_context(nc.Block())

        @block.gpsimd
        def _(pool):
            def body(s, u, turn):
                g = pool.value_load(ph.g_int[0:1, bass.ds(s, 1)], min_val=0, max_val=T // GB - 1)
                if since(s, UE):
                    pool.wait_ge(x_s, s - UE + 1)
                nc.gpsimd.tensor_copy(sring[:, u, :], r.src[:, bass.ds(g * GB, GB)]).then_inc(ring_s, 1)
                pool.wait_ge(ring_s, s + 1)
                pool.sem_inc(turn_s, 1)
                for k in range(GB):
                    nc.gpsimd.indirect_dma_start(hg[:, u, k, :], None, t["d_h"][:, :],
                                                 bass.IndirectOffsetOnAxis(sring[:, u, k:k + 1], 0)).then_inc(gat[u], 16)

            run(pool, SB, UE, body)

        @block.vector
        def _(dve):
            nc.vector.memset(acc[:, :, :], 0.0).then_inc(acc_s, 1)

            def add(s, v):
                w = dve.value_load(ph.w_int[0:1, bass.ds(s, 1)], min_val=0, max_val=NW - 1)
                dve.wait_ge(o_s, s + 1)
                dve.wait_ge(acc_s, s + 1)
                sl = acc[:, bass.ds(w, 1), :].rearrange("p a c -> p (a c)")
                nc.vector.tensor_tensor(sl, sl, p_o[:, v, 0:CX], ALU.add).then_inc(acc_s, 1)

            def body(s, u, turn):
                v = u % 2
                link = Link(dve, link_s, s, 1)
                g = dve.value_load(ph.g_int[0:1, bass.ds(s, 1)], min_val=0, max_val=T // GB - 1)
                if since(s, 2):
                    dve.wait_ge(o_s, s - 1)
                link(nc.vector.tensor_scalar(dc[:, v, :], r.dst[:, bass.ds(g * GB, GB)], ph.w_node[:, bass.ds(s, 1)],
                                             None, ALU.subtract))
                nc.vector.tensor_tensor(mm[:, v, :, :], r.jrow[:, None, :].broadcast_to([P, GB, P]),
                                        dc[:, v, :, None].broadcast_to([P, GB, P]), ALU.is_equal).then_inc(m_s, 1)
                eg = ex[:, bass.ds(g * (GB * H), GB * H)].rearrange("p (k h) -> p k h", h=H)
                nc.vector.tensor_copy(x[:, v, :, C:CX], eg)
                dve.wait_ge(gat[u], turn * (16 * GB) + 16 * GB)
                for k in range(GB):
                    last = nc.vector.tensor_tensor(x[:, v, k, 0:C].rearrange("p (h d) -> p h d", h=H),
                                                   hg[:, u, k, :].rearrange("p (h d) -> p h d", h=H),
                                                   eg[:, k, :, None].broadcast_to([P, H, D]), ALU.mult)
                last.then_inc(x_s, 1)
                if since(s, 1):
                    add(s - 1, 1 - v)

            run(dve, SB, UE, body)
            add(SB - 1, (SB - 1) % 2)

        @block.tensor
        def _(pe):
            def body(s, u, turn):
                v = u % 2
                pe.wait_ge(m_s, s + 1)
                pe.wait_ge(x_s, s + 1)
                if since(s, 2):
                    pe.wait_ge(acc_s, s)
                for k in range(GB):
                    last = nc.tensor.matmul(p_o[:, v, 0:CX], mm[:, v, k, :], x[:, v, k, :],
                                            start=(k == 0), stop=(k == GB - 1))
                last.then_inc(o_s, 1)

            run(pe, SB, UE, body)
def layer_norm(nc, dve, link, src, dst, st, mv, rstd, var_s, rstd_s, hold_s, n, g=None, b=None):
    link(nc.vector.bn_stats(st, src))
    dve.sem_inc(hold_s, 1)
    nc.vector.bn_aggr(mv, st).then_inc(var_s, 1)
    dve.wait_ge(rstd_s, n)
    if g is None:
        link(nc.vector.tensor_scalar(dst, src, mv[:, 0:1], rstd, ALU.subtract, ALU.mult))
    else:
        link(nc.vector.scalar_tensor_tensor(dst, src, mv[:, 0:1], g, ALU.subtract, ALU.mult))
        link(nc.vector.scalar_tensor_tensor(dst, dst, rstd, b, ALU.mult, ALU.add))


def mixer(nc, t, r):
    HC = H // KC
    with Phase(nc, "mix") as f:
        w1 = f.sb("w1", [P, KC, C])
        w2 = f.sb("w2", [P, KC, C])
        b1 = f.sb("b1", [P, KC])
        vec = f.sb("vec", [P, 5, C])
        q = f.sb("q", [P, UN, C])
        xn = f.sb("xn", [P, UN, C])
        x = f.sb("x", [P, UN, C])
        z = f.sb("z", [P, UN, KC, HC])
        y = f.sb("y", [P, UN, C])
        x1 = f.sb("x1", [P, UN, C])
        x1b = f.sb("x1b", [P, UN, C])
        x1T = f.sb("x1T", [P, UN, C])
        hT = f.sb("hT", [P, UN, KC, P])
        o = f.sb("o", [P, UN, C])
        st = f.sb("st", [P, UN, 2, 6])
        mv = f.sb("mv", [P, UN, 2, 2])
        rstd = f.sb("rstd", [P, UN, 2])
        p_t = f.ps("p_t", [P, UN, 512])
        p_x = f.ps("p_x", [P, UN, 512])
        p_h = f.ps("p_h", [P, UN, 512])
        p_y = f.ps("p_y", [P, UN, 512])
        ins = f.sems("ins", UN)
        stored = f.sems("stored", UN)
        w_in, t_s, x1_s, xT_s, xTc_s, h_s, hT_s, y_s, o_s, link_s, link2_s, x1b_s = (
            f.sem(s) for s in ("w_in", "t", "x1", "xT", "xTc", "h", "hT", "y", "o", "link", "link2", "x1b"))
        hold_s = f.sem("hold")
        pconst = f.sb("pconst", [P, 2])
        var1_s, rstd1_s, var2_s, rstd2_s, plink_s, plink2_s, half_s = (
            f.sem(s) for s in ("var1", "rstd1", "var2", "rstd2", "plink", "plink2", "half"))
        block = f.ctx.enter_context(nc.Block())

        @block.sync
        def _(sp):
            sp.dma_start(w1[:, :, :], t["w1T"].rearrange("(k p) n -> p k n", p=P)).then_inc(w_in, 16)
            sp.dma_start(w2[:, :, :], t["w2T"].rearrange("(k p) n -> p k n", p=P)).then_inc(w_in, 16)
            sp.dma_start(b1[:, :], t["b1_col"]).then_inc(w_in, 16)
            for k, v in enumerate((t["g1"], t["be1"], t["g2"], t["be2"], t["b2"])):
                sp.dma_start(vec[:, k, :], v.broadcast_to([P, C])).then_inc(w_in, 16)

            def body(i, u, turn):
                if since(i, UN):
                    sp.wait_ge(o_s, i - UN + 1)
                sp.dma_start(q[:, u, :], t["d_q"][:, bass.ds(i * C, C)]).then_inc(ins[u], 16)
                sp.dma_start(xn[:, u, :], rows(t["d_xn"], i)).then_inc(ins[u], 16)
                sp.dma_start(x[:, u, :], rows(t["x"], i)).then_inc(ins[u], 16)
                if since(i, UN):
                    sp.dma_start(rows(t["d_x1"], i - UN), o[:, u, :]).then_inc(stored[u], 16)

            run(sp, NW, UN, body)
            for i in range(NW - UN, NW):
                sp.wait_ge(o_s, i + 1)
                sp.dma_start(rows(t["d_x1"], i), o[:, i % UN, :]).then_inc(stored[i % UN], 16)
            for u in range(UN):
                sp.wait_ge(ins[u], 48 * (NW // UN))
                sp.wait_ge(stored[u], 16 * (NW // UN))

        @block.vector
        def _(dve):
            dve.wait_ge(w_in, 8 * 16)
            g1, be1, g2, be2, b2 = (vec[:, k, :] for k in range(5))

            def first(i, u, turn):
                link = Link(dve, link_s, i, 7)
                dve.wait_ge(ins[u], turn * 48 + 48)
                dve.wait_ge(t_s, i + 1)
                pt = p_t[:, u, 0:KC * (P + HC)].rearrange("p (c n) -> p c n", c=KC)
                link(nc.vector.tensor_scalar(z[:, u, :, :], pt[:, :, P:P + HC], 1e-6, None, ALU.add))
                link(nc.vector.reciprocal(z[:, u, :, :], z[:, u, :, :]))
                y4 = y[:, u, :].rearrange("p (c h d) -> p c h d", c=KC, h=HC)
                for c in range(KC):
                    last = nc.vector.tensor_tensor(y4[:, c, :, :], pt[:, c, 0:P].rearrange("p (h d) -> p h d", h=HC),
                                                   z[:, u, c, :, None].broadcast_to([P, HC, D]), ALU.mult)
                link(last)
                link(nc.vector.tensor_tensor(y[:, u, :], y[:, u, :], xn[:, u, :], ALU.add))
                layer_norm(nc, dve, link, y[:, u, :], x1[:, u, :], st[:, u, 0, :], mv[:, u, 0, :], rstd[:, u, 0:1],
                           var1_s, rstd1_s, hold_s, i + 1, g1, be1)
                dve.sem_inc(x1_s, 1)
                nc.vector.tensor_tensor(x1b[:, u, :], x1[:, u, :], b2, ALU.add).then_inc(x1b_s, 1)

            def second(i, u, turn):
                link = Link(dve, link2_s, i, 4)
                dve.wait_ge(y_s, i + 1)
                dve.wait_ge(x1b_s, i + 1)
                link(nc.vector.tensor_tensor(y[:, u, :], p_y[:, u, 0:C], x1b[:, u, :], ALU.add))
                if since(i, UN):
                    dve.wait_ge(stored[u], turn * 16)
                layer_norm(nc, dve, link, y[:, u, :], o[:, u, :], st[:, u, 1, :], mv[:, u, 1, :], rstd[:, u, 1:2],
                           var2_s, rstd2_s, hold_s, i + 1, g2, be2)
                nc.vector.tensor_tensor(o[:, u, :], o[:, u, :], x[:, u, :], ALU.add).then_inc(o_s, 1)

            def body(i, u, turn):
                first(i, u, turn)
                if since(i, 1):
                    second(i - 1, (u - 1) % UN, turn - 1 if u == 0 else turn)

            run(dve, NW, UN, body)
            second(NW - 1, (NW - 1) % UN, NW // UN - 1)

        @block.gpsimd
        def _(pool):
            nc.gpsimd.memset(pconst[:, 0:1], -0.5).then_inc(half_s, 1)
            nc.gpsimd.memset(pconst[:, 1:2], LN_EPS).then_inc(half_s, 1)
            pool.wait_ge(half_s, 2)

            def body(i, u, turn):
                pool.wait_ge(var1_s, i + 1)
                pool_rstd(nc, Link(pool, plink_s, i, 1), mv[:, u, 0, 1:2], pconst, rstd[:, u, 0:1]).then_inc(rstd1_s, 1)
                if since(i, 1):
                    second(i - 1, (u - 1) % UN)

            def second(i, u):
                pool.wait_ge(var2_s, i + 1)
                pool_rstd(nc, Link(pool, plink2_s, i, 1), mv[:, u, 1, 1:2], pconst, rstd[:, u, 1:2]).then_inc(rstd2_s, 1)

            run(pool, NW, 2, body)
            second(NW - 1, (NW - 1) % UN)

        @block.scalar
        def _(act):
            act.wait_ge(w_in, 8 * 16)

            def body(i, u, turn):
                act.wait_ge(xT_s, i + 1)
                nc.scalar.copy(x1T[:, u, :], p_x[:, u, 0:C]).then_inc(xTc_s, 1)
                act.wait_ge(h_s, i + 1)
                for c in range(KC):
                    last = nc.scalar.activation(hT[:, u, c, :], p_h[:, u, c * P:(c + 1) * P], ACT.Gelu,
                                                bias=b1[:, c:c + 1])
                last.then_inc(hT_s, 1)

            run(act, NW, UN, body)

        @block.tensor
        def _(pe):
            pe.wait_ge(w_in, 8 * 16)

            def read(i, u, turn):
                pe.wait_ge(ins[u], turn * 48 + 48)
                if since(i, UN):
                    pe.wait_ge(x1_s, i - 1)
                for c in range(KC):
                    last = nc.tensor.matmul(p_t[:, u, c * (P + HC):(c + 1) * (P + HC)], q[:, u, c * P:(c + 1) * P],
                                            r.kvbd[:, c, :], start=True, stop=True)
                last.then_inc(t_s, 1)

            def mlp(i, u):
                pe.wait_ge(x1_s, i + 1)
                for c in range(KC):
                    last = nc.tensor.transpose(p_x[:, u, c * P:(c + 1) * P], x1[:, u, c * P:(c + 1) * P], r.ident[:, :])
                last.then_inc(xT_s, 1)
                pe.wait_ge(xTc_s, i + 1)
                for c in range(KC):
                    for k in range(KC):
                        last = nc.tensor.matmul(p_h[:, u, c * P:(c + 1) * P], w1[:, k, c * P:(c + 1) * P],
                                                x1T[:, u, k * P:(k + 1) * P], start=(k == 0), stop=(k == KC - 1))
                last.then_inc(h_s, 1)
                pe.wait_ge(hT_s, i + 1)
                if since(i, UN):
                    pe.wait_ge(o_s, i - 1)
                for k in range(KC):
                    last = nc.tensor.matmul(p_y[:, u, 0:C], hT[:, u, k, :], w2[:, k, :],
                                            start=(k == 0), stop=(k == KC - 1))
                last.then_inc(y_s, 1)

            def body(i, u, turn):
                read(i, u, turn)
                if since(i, 1):
                    mlp(i - 1, (u - 1) % UN)

            run(pe, NW, UN, body)
            mlp(NW - 1, (NW - 1) % UN)


def node_update(nc, t, r, acc):
    with Phase(nc, "upd") as f:
        bias = f.sb("bias", [P, C])
        x1 = f.sb("x1", [P, UN, C])
        den = f.sb("den", [P, UN, H])
        x2 = f.sb("x2", [P, UN, C])
        xf = f.sb("xf", [P, UN, C])
        xfT = f.sb("xfT", [P, UN, C])
        st = f.sb("st", [P, UN, 6])
        mv = f.sb("mv", [P, UN, 2])
        rstd = f.sb("rstd", [P, UN])
        zero = f.sb("zero", [P, P])
        p_x = f.ps("p_x", [P, UN, 512])
        p_m = f.ps("p_m", [P, KC])
        ins = f.sems("ins", UN)
        stored = f.sems("stored", UN)
        w_in, x2_s, xf_s, xT_s, xTc_s, link_s, zero_s, mean_s = (
            f.sem(s) for s in ("w_in", "x2", "xf", "xT", "xTc", "link", "zero", "mean"))
        hold_s = f.sem("hold")
        pconst = f.sb("pconst", [P, 2])
        var_s, rstd_s, plink_s, half_s = (f.sem(s) for s in ("var", "rstd", "plink", "half"))
        block = f.ctx.enter_context(nc.Block())

        @block.sync
        def _(sp):
            sp.dma_start(bias[:, :], t["bias"].broadcast_to([P, C])).then_inc(w_in, 16)

            def store(i, u):
                sp.wait_ge(xf_s, i + 1)
                sp.dma_start(rows(t["d_x2"], i), x2[:, u, :]).then_inc(stored[u], 16)
                sp.dma_start(rows(t["d_xf"], i), xf[:, u, :]).then_inc(stored[u], 16)
                sp.wait_ge(xTc_s, i + 1)
                sp.sem_inc(hold_s, 1)
                sp.dma_start(t["d_xfT"][:, :, bass.ds(i * P, P)], xfT[:, u, :].rearrange("p (k n) -> p k n", k=KC)).then_inc(stored[u], 16)

            def body(i, u, turn):
                if since(i, UN):
                    store(i - UN, u)
                sp.dma_start(x1[:, u, :], rows(t["d_x1"], i)).then_inc(ins[u], 16)

            run(sp, NW, UN, body)
            for i in range(NW - UN, NW):
                store(i, i % UN)
            for u in range(UN):
                sp.wait_ge(ins[u], 16 * (NW // UN))
                sp.wait_ge(stored[u], 48 * (NW // UN))

        @block.vector
        def _(dve):
            nc.vector.memset(zero[:, :], 0.0).then_inc(zero_s, 1)
            dve.wait_ge(w_in, 16)

            def body(i, u, turn):
                link = Link(dve, link_s, i, 7)
                a = acc[:, bass.ds(i, 1), :].rearrange("p a c -> p (a c)")
                link(nc.vector.tensor_scalar(den[:, u, :], a[:, C:C + H], 1e-10, None, ALU.max))
                link(nc.vector.reciprocal(den[:, u, :], den[:, u, :]))
                if since(i, UN):
                    dve.wait_ge(stored[u], turn * 48)
                link(nc.vector.tensor_tensor(x2[:, u, :].rearrange("p (h d) -> p h d", h=H),
                                             a[:, 0:C].rearrange("p (h d) -> p h d", h=H),
                                             den[:, u, :, None].broadcast_to([P, H, D]), ALU.mult))
                link(nc.vector.tensor_tensor(x2[:, u, :], x2[:, u, :], bias[:, :], ALU.add))
                dve.wait_ge(ins[u], turn * 16 + 16)
                link(nc.vector.tensor_tensor(x2[:, u, :], x2[:, u, :], x1[:, u, :], ALU.add))
                layer_norm(nc, dve, link, x2[:, u, :], xf[:, u, :], st[:, u, :], mv[:, u, :], rstd[:, u:u + 1],
                           var_s, rstd_s, hold_s, i + 1)
                dve.sem_inc(xf_s, 1)

            run(dve, NW, UN, body)
            dve.wait_ge(mean_s, 1)
            nc.vector.tensor_scalar(r.mean[:, :], p_m[:, :], 1.0 / N, None, ALU.mult).then_inc(zero_s, 1)

        @block.gpsimd
        def _(pool):
            nc.gpsimd.memset(pconst[:, 0:1], -0.5).then_inc(half_s, 1)
            nc.gpsimd.memset(pconst[:, 1:2], LN_EPS).then_inc(half_s, 1)
            pool.wait_ge(half_s, 2)

            def body(i, u, turn):
                pool.wait_ge(var_s, i + 1)
                pool_rstd(nc, Link(pool, plink_s, i, 1), mv[:, u, 1:2], pconst, rstd[:, u:u + 1]).then_inc(rstd_s, 1)

            run(pool, NW, 2, body)

        @block.scalar
        def _(act):
            def body(i, u, turn):
                act.wait_ge(xT_s, i + 1)
                if since(i, UN):
                    act.wait_ge(stored[u], turn * 48)
                nc.scalar.copy(xfT[:, u, :], p_x[:, u, 0:C]).then_inc(xTc_s, 1)

            run(act, NW, UN, body)

        @block.tensor
        def _(pe):
            pe.wait_ge(zero_s, 1)
            nc.tensor.matmul(p_m[:, :], zero[:, :], r.ident[:, 0:KC], start=True, stop=False, skip_group_check=True)

            def body(i, u, turn):
                pe.wait_ge(xf_s, i + 1)
                if since(i, UN):
                    pe.wait_ge(xTc_s, i - 1)
                for c in range(KC):
                    nc.tensor.matmul(p_m[:, c:c + 1], xf[:, u, c * P:(c + 1) * P], r.valid[:, bass.ds(i, 1)],
                                     start=False, stop=False, skip_group_check=True)
                for c in range(KC):
                    last = nc.tensor.transpose(p_x[:, u, c * P:(c + 1) * P], xf[:, u, c * P:(c + 1) * P], r.ident[:, :])
                last.then_inc(xT_s, 1)

            run(pe, NW, UN, body)
            nc.tensor.matmul(p_m[:, :], zero[:, :], r.ident[:, 0:KC], start=False, stop=True,
                             skip_group_check=True).then_inc(mean_s, 1)


def route(nc, t, r, q):
    with Phase(nc, "route") as f:
        wr = f.sb("wr", [P, KC, XP])
        row = lambda n, w=XP: f.sb(n, [1, w])
        br, io, lg, ex, rw, big, sc, eq, pick, r2 = (row(n) for n in ("br", "io", "lg", "ex", "rw", "big", "sc", "eq", "pick", "r2"))
        s1, idx, top, tw = row("s1", 2), row("idx", 2), row("top", 2), row("tw", 2)
        idx_i = f.sb("idx_i", [1, 2], I32)
        one = f.sb("one", [1, P])
        twb = f.sb("twb", [P, 2])
        b2e = f.sb("b2e", [P, 2, C])
        p_l = f.ps("p_l", [1, XP])
        p_w = f.ps("p_w", [P, 2])
        w_in, e_in, l_s, x_s, a_s, i_s, tw_s, pw_s, link_s = (
            f.sem(s) for s in ("w_in", "e_in", "l", "x", "a", "i", "tw", "pw", "link"))
        block = f.ctx.enter_context(nc.Block())

        @block.sync
        def _(sp):
            sp.dma_start(wr[:, :, :], t["wr"].rearrange("(k p) n -> p k n", p=P)).then_inc(w_in, 16)
            sp.dma_start(br[:, :], t["br"]).then_inc(w_in, 16)
            sp.dma_start(io[:, :], t["c_jrow"][0:1, 0:XP]).then_inc(w_in, 16)
            sp.wait_ge(i_s, 1)
            for k in range(2):
                e = sp.value_load(idx_i[0:1, k:k + 1], min_val=0, max_val=XP - 1)
                sp.dma_start(q.w1[:, k, :, :], t["ffn_w1"][bass.ds(e * C, C), :].rearrange("(k p) n -> p k n", p=P)).then_inc(e_in, 16)
                sp.dma_start(q.w2[:, k, :, :], t["ffn_w2"][bass.ds(e * FF, FF), :].rearrange("(k p) n -> p k n", p=P)).then_inc(e_in, 16)
                sp.dma_start(q.b1[:, k, :], t["ffn_b1"][bass.ds(e * P, P), :]).then_inc(e_in, 16)
                sp.dma_start(b2e[:, k, :], t["ffn_b2"][bass.ds(e, 1), :].broadcast_to([P, C])).then_inc(e_in, 16)
            sp.dma_start(q.g[:, :], t["ffn_g"].broadcast_to([P, C])).then_inc(e_in, 16)
            sp.dma_start(q.be[:, :], t["ffn_be"].broadcast_to([P, C])).then_inc(e_in, 16)
            sp.wait_ge(e_in, 10 * 16)

        @block.vector
        def _(dve):
            link = Link(dve, link_s)
            V = nc.vector
            exps = [0]

            def exp():
                exps[0] += 1
                dve.sem_inc(x_s, 1)
                dve.wait_ge(a_s, exps[0])

            def softmax(dst, n):
                link(V.tensor_reduce(s1[:, 0:1], lg[:, 0:n], AX.X, ALU.max))
                link(V.tensor_scalar(lg[:, 0:n], lg[:, 0:n], s1[:, 0:1], None, ALU.subtract))
                exp()
                link(V.tensor_reduce(s1[:, 1:2], ex[:, 0:n], AX.X, ALU.add))
                link(V.reciprocal(s1[:, 1:2], s1[:, 1:2]))
                link(V.tensor_scalar(dst, ex[:, 0:n], s1[:, 1:2], None, ALU.mult))

            link(V.memset(one[:, :], 1.0))
            link(V.memset(lg[:, :], 0.0))
            link(V.memset(ex[:, :], 0.0))
            dve.wait_ge(w_in, 48)
            dve.wait_ge(l_s, 1)
            link(V.tensor_tensor(lg[:, :], p_l[:, :], br[:, :], ALU.add))
            softmax(rw[:, :], XP)
            link(V.tensor_scalar(big[:, :], rw[:, :], float(TOPW), None, ALU.mult))
            link(V.reciprocal(sc[:, :], big[:, :]))
            link(V.tensor_scalar(big[:, :], big[:, :], CAPACITY, None, ALU.is_gt))
            link(V.scalar_tensor_tensor(sc[:, :], sc[:, :], CAPACITY, big[:, :], ALU.mult, ALU.mult))
            link(V.tensor_scalar(big[:, :], big[:, :], -1.0, 1.0, ALU.mult, ALU.add))
            link(V.tensor_tensor(sc[:, :], sc[:, :], big[:, :], ALU.add))
            link(V.tensor_tensor(lg[:, :], rw[:, :], sc[:, :], ALU.mult))
            softmax(rw[:, :], XP)
            for k in range(2):
                link(V.tensor_reduce(top[:, k:k + 1], rw[:, :], AX.X, ALU.max))
                link(V.tensor_scalar(eq[:, :], rw[:, :], top[:, k:k + 1], float(-XP), ALU.is_equal, ALU.mult))
                link(V.scalar_tensor_tensor(pick[:, :], eq[:, :], float(XP), io[:, :], ALU.add, ALU.add))
                link(V.tensor_reduce(idx[:, k:k + 1], pick[:, :], AX.X, ALU.min))
                link(V.tensor_scalar(eq[:, :], io[:, :], idx[:, k:k + 1], -4.0, ALU.is_equal, ALU.mult))
                link(V.tensor_tensor(rw[:, :], rw[:, :], eq[:, :], ALU.add))
            link(V.tensor_copy(idx_i[:, :], idx[:, :]))
            dve.sem_inc(i_s, 1)
            link(V.tensor_copy(lg[:, 0:2], top[:, :]))
            softmax(tw[:, :], 2)
            dve.sem_inc(tw_s, 1)
            dve.wait_ge(pw_s, 1)
            link(V.tensor_copy(twb[:, :], p_w[:, :]))
            dve.wait_ge(e_in, 10 * 16)
            for k in range(2):
                w = q.w2[:, k, :, :].rearrange("p k n -> p (k n)")
                link(V.tensor_scalar(w, w, twb[:, k:k + 1], None, ALU.mult))
                link(V.tensor_scalar(b2e[:, k, :], b2e[:, k, :], twb[:, k:k + 1], None, ALU.mult))
            link(V.tensor_tensor(q.b2[:, :], b2e[:, 0, :], b2e[:, 1, :], ALU.add))

        @block.scalar
        def _(act):
            for n in range(3):
                act.wait_ge(x_s, n + 1)
                nc.scalar.activation(ex[:, :], lg[:, :], ACT.Exp).then_inc(a_s, 1)

        @block.tensor
        def _(pe):
            pe.wait_ge(w_in, 48)
            for c in range(KC):
                last = nc.tensor.matmul(p_l[:, :], r.mean[:, c:c + 1], wr[:, c, :], start=(c == 0), stop=(c == KC - 1))
            last.then_inc(l_s, 1)
            pe.wait_ge(tw_s, 1)
            nc.tensor.matmul(p_w[:, :], one[:, :], tw[:, :], start=True, stop=True).then_inc(pw_s, 1)


def experts(nc, t, r, q):
    B = 2
    NB = NW // B
    FK = FF // P
    J = 2 * FK
    with Phase(nc, "ffn") as f:
        xT = f.sb("xT", [P, 2, KC, B * P])
        xf = f.sb("xf", [P, 2, B, C])
        x2 = f.sb("x2", [P, 2, B, C])
        hT = f.sb("hT", [P, 2, J, B * P])
        y = f.sb("y", [P, 2, B, C])
        o = f.sb("o", [P, 2, B, C])
        st = f.sb("st", [P, 2, B, 6])
        mv = f.sb("mv", [P, 2, B, 2])
        rstd = f.sb("rstd", [P, 2, B])
        p_f = f.ps("p_f", [P, 4, 512])
        p_y = f.ps("p_y", [P, 2, B, C])
        ins = f.sems("ins", 2)
        stored = f.sems("stored", 2)
        f_s, h_s, y_s, o_s, link_s = (f.sem(s) for s in ("f", "h", "y", "o", "link"))
        hold_s = f.sem("hold")
        pconst = f.sb("pconst", [P, 2])
        var_s, rstd_s, plink_s, half_s = (f.sem(s) for s in ("var", "rstd", "plink", "half"))
        block = f.ctx.enter_context(nc.Block())
        block_of = lambda d, i: d[bass.ds(i * (B * P), B * P), :].rearrange("(b p) n -> p b n", p=P)

        @block.sync
        def _(sp):
            def store(i, u):
                sp.wait_ge(o_s, i + 1)
                sp.dma_start(block_of(t["out"], i), o[:, u, :, :]).then_inc(stored[u], 16)

            def body(i, u, turn):
                if since(i, 2):
                    store(i - 2, u)
                sp.dma_start(xT[:, u, :, :], t["d_xfT"][:, :, bass.ds(i * (B * P), B * P)]).then_inc(ins[u], 16)
                sp.dma_start(xf[:, u, :, :], block_of(t["d_xf"], i)).then_inc(ins[u], 16)
                sp.dma_start(x2[:, u, :, :], block_of(t["d_x2"], i)).then_inc(ins[u], 16)

            run(sp, NB, 2, body)
            for i in range(NB - 2, NB):
                store(i, i % 2)
            for u in range(2):
                n = (NB + 1 - u) // 2
                sp.wait_ge(ins[u], 48 * n)
                sp.wait_ge(stored[u], 16 * n)

        @block.tensor
        def _(pe):
            def down(i, u):
                if since(i, 2):
                    pe.wait_ge(o_s, i - 1)
                for b in range(B):
                    for j in range(J):
                        pe.wait_ge(h_s, i * J + j + 1) if b == 0 else None
                        last = nc.tensor.matmul(p_y[:, u, b, :], hT[:, u, j, b * P:(b + 1) * P],
                                                q.w2[:, j // FK, j % FK, :], start=(j == 0), stop=(j == J - 1))
                last.then_inc(y_s, 1)

            def body(i, u, turn):
                pe.wait_ge(ins[u], turn * 48 + 48)
                for j in range(J):
                    if j >= 4:
                        pe.wait_ge(h_s, i * J + j - 3)
                    elif since(i, 1):
                        pe.wait_ge(h_s, i * J + j - 3)
                    for k in range(KC):
                        last = nc.tensor.matmul(p_f[:, j % 4, 0:B * P], q.w1[:, j // FK, k, (j % FK) * P:(j % FK + 1) * P],
                                                xT[:, u, k, :], start=(k == 0), stop=(k == KC - 1))
                    last.then_inc(f_s, 1)
                if since(i, 1):
                    down(i - 1, 1 - u)

            run(pe, NB, 2, body)
            down(NB - 1, (NB - 1) % 2)

        @block.gpsimd
        def _(pool):
            nc.gpsimd.memset(pconst[:, 0:1], -0.5).then_inc(half_s, 1)
            nc.gpsimd.memset(pconst[:, 1:2], LN_EPS).then_inc(half_s, 1)
            pool.wait_ge(half_s, 2)

            def body(i, u, turn):
                for b in range(B):
                    pool.wait_ge(var_s, i * B + b + 1)
                    pool_rstd(nc, Link(pool, plink_s, i * B + b, 1), mv[:, u, b, 1:2], pconst,
                              rstd[:, u, b:b + 1]).then_inc(rstd_s, 1)

            run(pool, NB, 2, body)

        @block.scalar
        def _(act):
            def body(i, u, turn):
                if since(i, 2):
                    act.wait_ge(y_s, i - 1)
                for j in range(J):
                    act.wait_ge(f_s, i * J + j + 1)
                    nc.scalar.activation(hT[:, u, j, :], p_f[:, j % 4, 0:B * P], ACT.Gelu,
                                         bias=q.b1[:, j // FK, j % FK:j % FK + 1]).then_inc(h_s, 1)

            run(act, NB, 2, body)

        @block.vector
        def _(dve):
            def body(i, u, turn):
                link = Link(dve, link_s, i, 1 + 4 * B)
                dve.wait_ge(ins[u], turn * 48 + 48)
                for b in range(B):
                    last = nc.vector.tensor_tensor(xf[:, u, b, :], xf[:, u, b, :], q.b2[:, :], ALU.add)
                link(last)
                dve.wait_ge(y_s, i + 1)
                if since(i, 2):
                    dve.wait_ge(stored[u], turn * 16)
                for b in range(B):
                    link(nc.vector.tensor_tensor(y[:, u, b, :], p_y[:, u, b, :], xf[:, u, b, :], ALU.add))
                    layer_norm(nc, dve, link, y[:, u, b, :], o[:, u, b, :], st[:, u, b, :], mv[:, u, b, :],
                               rstd[:, u, b:b + 1], var_s, rstd_s, hold_s, i * B + b + 1, q.g[:, :], q.be[:, :])
                    last = nc.vector.tensor_tensor(o[:, u, b, :], o[:, u, b, :], x2[:, u, b, :], ALU.add)
                last.then_inc(o_s, 1)

            run(dve, NB, 2, body)


class Tensors:
    pass


def gps_layer(nc, t):
    with Phase(nc, "all") as f:
        r = Tensors()
        r.ident, r.jrow, r.jcol = f.sb("ident", [P, P]), f.sb("jrow", [P, P]), f.sb("jcol", [P, 1])
        r.headsel, r.valid = f.sb("headsel", [P, KC * H]), f.sb("valid", [P, NW])
        r.kvbd, r.mean = f.sb("kvbd", [P, KC, P + 4]), f.sb("mean", [P, KC])
        with Phase(nc, "lin") as g:
            r.wall = g.sb("wall", [P, KC, C + 2 * H])
            r.headmask = g.sb("headmask", [P, P])
            split_edge_features(nc, t)
            fold_attention_weights(nc, t, r)
            node_pass(nc, t, r)
        with Phase(nc, "edge") as g:
            r.src = g.sb("src", [P, T], U32)
            r.dst = g.sb("dst", [P, T], I32)
            al = g.sb("al", [P, CE + 4])
            pb = Tensors()
            pb.g_int, pb.w_int = g.sb("gb", [P, SB], I32), g.sb("wb", [P, SB], I32)
            pb.w_node, pb.j_node = g.sb("wnb", [P, SB]), None
            make_steps(nc, t, r, pb, GB, SB, t["last_b"], t["c_gcol_b"])
            with Phase(nc, "weights") as k:
                pa = Tensors()
                pa.g_int, pa.w_int = k.sb("ga", [P, SA], I32), k.sb("wa", [P, SA], I32)
                pa.w_node, pa.j_node = k.sb("wna", [P, SA]), k.sb("jna", [P, SA])
                pa.al, pa.asrc = al, k.sb("asrc", [P, CE + 4])
                make_steps(nc, t, r, pa, GA, SA, t["last_a"], t["c_gcol_a"])
                load_indices(nc, t, r)
                edge_scores(nc, t, r, pa)
                edge_softmax(nc, t, r, pa)
            with Phase(nc, "acc") as k:
                acc = k.sb("acc", [P, NW, C + H])
                edge_sums(nc, t, r, pb, al, acc)
                mixer(nc, t, r)
                node_update(nc, t, r, acc)
        with Phase(nc, "exp") as g:
            q = Tensors()
            q.w1, q.w2 = g.sb("w1", [P, 2, KC, FF]), g.sb("w2", [P, 2, FF // P, C])
            q.b1, q.b2 = g.sb("b1", [P, 2, FF // P]), g.sb("b2", [P, C])
            q.g, q.be = g.sb("g", [P, C]), g.sb("be", [P, C])
            route(nc, t, r, q)
            experts(nc, t, r, q)


def split_edge_features(nc, t):
    A = P // EF
    L = EP // A
    with Phase(nc, "split") as f:
        x = f.sb("x", [P, L])
        hi = f.sb("hi", [P, L], F32R)
        lo = f.sb("lo", [P, L], F32R)
        w = f.sb("w", [EF, C])
        whi = f.sb("whi", [EF, C], F32R)
        wlo = f.sb("wlo", [EF, C], F32R)
        x_in, hi_s, lo_s, out_s = (f.sem(s) for s in ("x_in", "hi", "lo", "out"))
        block = f.ctx.enter_context(nc.Block())

        @block.sync
        def _(sp):
            sp.dma_start(w[:, :], t["ew"]).then_inc(x_in, 16)
            sp.dma_start(x[:, :], t["eaT"].rearrange("f (a l) -> (f a) l", a=A)).then_inc(x_in, 16)
            part = lambda n: t["d_ea"][n * EF:(n + 1) * EF, :].rearrange("f (a l) -> (f a) l", a=A)
            sp.wait_ge(hi_s, 2)
            sp.dma_start(part(0), hi[:, :].bitcast(F32)).then_inc(out_s, 16)
            sp.dma_start(part(2), hi[:, :].bitcast(F32)).then_inc(out_s, 16)
            sp.dma_start(t["d_ew"][0:EF, :], whi[:, :].bitcast(F32)).then_inc(out_s, 16)
            sp.dma_start(t["d_ew"][EF:2 * EF, :], whi[:, :].bitcast(F32)).then_inc(out_s, 16)
            sp.wait_ge(lo_s, 2)
            sp.dma_start(part(1), lo[:, :].bitcast(F32)).then_inc(out_s, 16)
            sp.dma_start(t["d_ew"][2 * EF:3 * EF, :], wlo[:, :].bitcast(F32)).then_inc(out_s, 16)
            sp.wait_ge(out_s, 6 * 16)

        @block.scalar
        def _(act):
            act.wait_ge(x_in, 32)
            nc.scalar.copy(whi[:, :], w[:, :]).then_inc(hi_s, 1)
            nc.scalar.copy(hi[:, :], x[:, :]).then_inc(hi_s, 1)

        @block.vector
        def _(dve):
            dve.wait_ge(hi_s, 2)
            nc.vector.tensor_tensor(wlo[:, :], w[:, :], whi[:, :].bitcast(F32), ALU.subtract).then_inc(lo_s, 1)
            nc.vector.tensor_tensor(lo[:, :], x[:, :], hi[:, :].bitcast(F32), ALU.subtract).then_inc(lo_s, 1)


def load_indices(nc, t, r):
    with Phase(nc, "idx") as f:
        loaded = f.sem("loaded")
        block = f.ctx.enter_context(nc.Block())

        @block.sync
        def _(sp):
            sp.dma_start(r.src[:, :], t["src_col"]).then_inc(loaded, 16)
            sp.dma_start(r.dst[:, :], t["dst_col"]).then_inc(loaded, 16)
            sp.wait_ge(loaded, 32)


def kernel(**inputs):
    import numpy as np
    import concourse.bacc as bacc
    from concourse.bass_utils import run_bass_kernel_spmd as launch

    a = {k: np.asarray(v) for k, v in inputs.items()}
    row = lambda v: np.ascontiguousarray(v.reshape(1, -1))
    turn = lambda v: np.ascontiguousarray(v.T)
    src = np.pad(a["src"], (0, EP - E))
    dst = np.pad(a["dst"], (0, EP - E), constant_values=NP - 1)
    head = np.arange(C) // D
    groups = lambda tiles: dst.reshape(NW, T // tiles // NW, tiles * P)[:, :, -1]
    p = np.arange(P)
    arrays = {
        "x": np.pad(a["x"], ((0, NP + UN * P - N), (0, 0))),
        "src_col": turn(src.reshape(T, P)),
        "dst_col": turn(dst.reshape(T, P)),
        "dst_row": row(dst),
        "dst_ext": np.pad(row(dst), ((0, 0), (1, 1)), constant_values=-1),
        "last_a": np.ascontiguousarray(groups(GA)),
        "last_b": np.ascontiguousarray(groups(GB)),
        "eaT": np.concatenate([turn(np.pad(a["edge_attr_3"], ((0, EP - E), (0, 0)))), np.ones((1, EP), np.float32)]),
        "ew": np.concatenate([turn(a["L0_gnn_edge_W"]), row(a["L0_gnn_edge_b"])]),
        "w": a["L0_gnn_W"], "wT": turn(a["L0_gnn_W"]),
        "a_col": np.stack([a["L0_gnn_a_dst"].reshape(-1), a["L0_gnn_a_src"].reshape(-1)], 1),
        "bias": row(a["L0_gnn_bias"]),
        "wqkvT": turn(a["L0_mix_Wqkv"]), "w1T": turn(a["L0_mix_W1"]), "w2T": turn(a["L0_mix_W2"]),
        "b1_col": turn(a["L0_mix_b1"].reshape(KC, P)),
        "g1": row(a["L0_mix_ln1_g"]), "be1": row(a["L0_mix_ln1_b"]),
        "g2": row(a["L0_mix_ln2_g"]), "be2": row(a["L0_mix_ln2_b"]), "b2": row(a["L0_mix_b2"]),
        "wr": a["L0_ffn_Wr"], "br": row(a["L0_ffn_br"]),
        "ffn_w1": a["L0_ffn_W1"].reshape(XP * C, FF), "ffn_w2": a["L0_ffn_W2"].reshape(XP * FF, C),
        "ffn_b1": np.ascontiguousarray(a["L0_ffn_b1"].reshape(XP, FF // P, P).transpose(0, 2, 1)).reshape(XP * P, FF // P),
        "ffn_b2": a["L0_ffn_b2"], "ffn_g": row(a["L0_ffn_gamma"]), "ffn_be": row(a["L0_ffn_beta"]),
        "c_ident": np.eye(P, dtype=np.float32),
        "c_jrow": np.tile(p.astype(np.float32), (P, 1)),
        "c_jcol": p.astype(np.float32)[:, None],
        "c_headsel": (head.reshape(KC, P).T[:, :, None] == np.arange(H)).astype(np.float32).reshape(P, KC * H),
        "c_headmask": (p[:, None] // D == p[None, :] // D).astype(np.float32),
        "c_valid": (p[:, None] + P * np.arange(NW)[None, :] < N).astype(np.float32),
        "c_sidx": np.tile(np.arange(SB, dtype=np.float32), (P, 1)),
    }
    for n, tiles in (("a", GA), ("b", GB)):
        k = T // tiles // NW
        arrays[f"c_gcol_{n}"] = 1.0 + np.arange(NW * k, dtype=np.float32).reshape(NW, k)
    scratch = {"d_xn": [NP, C], "d_h": [NP, C], "d_as": [NP, H], "d_q": [P, NW * C], "d_x1": [NP, C],
               "d_x2": [NP, C], "d_xf": [NP, C], "d_xfT": [P, KC, NP]}

    in_parts = {"d_hw": [NP, 2 * (C + H)], "d_ea": [3 * EF, EP], "d_ew": [3 * EF, C]}

    nc = bacc.Bacc("TRN2", target_bir_lowering=False, num_devices=1)
    feed, aps = {}, {}
    for name, v in arrays.items():
        v = np.ascontiguousarray(v)
        feed[f"in_{name}"] = v
        aps[name] = nc.dram_tensor(f"in_{name}", v.shape, mybir.dt.from_np(v.dtype), kind="ExternalInput").ap()
    for name, shape in scratch.items():
        aps[name] = nc.dram_tensor(name, shape, F32).ap()
    for name, shape in in_parts.items():
        aps[name] = nc.dram_tensor(name, shape, F32).ap()
    aps["out"] = nc.dram_tensor("out", [NP, C], F32, kind="ExternalOutput").ap()
    aps["src_col"] = aps["src_col"].bitcast(U32)
    gps_layer(nc, aps)
    return launch(nc, [feed], core_ids=[0]).results[0]["out"][:N]
```

```python
import concourse.bass as bass
from concourse import mybir
from contextlib import ExitStack

F32 = mybir.dt.float32
I32 = mybir.dt.int32
U32 = mybir.dt.uint32
F32R = mybir.dt.float32r
ALU = mybir.AluOpType
ACT = mybir.ActivationFunctionType
AX = mybir.AxisListType

P = 128
N = 12500
C = 256
H = 8
D = C // H
KC = C // P
NW = -(-N // P)
NP = NW * P
E = 200000
EF = 4
CH = 16
TC = -(-E // (P * CH))
T = TC * CH
EP = T * P
CE = TC * P
GA = 4
GB = 2
BIG = 1.0e30
XP = 8
FF = 512
TOPW = N
CAPACITY = float(-(-N * 5 // (4 * XP)))
LN_EPS = 1e-5




def step_count(tiles):
    return -(-(T // tiles + NW - 1) // UE) * UE


UE = 4
UN = 2
BL = 7
NB = NW // BL
SA = step_count(GA)
SB = step_count(GB)


def run(eng, count, unroll, body, tail=0):
    for s in range(unroll):
        body(s, s, 0)
    turns = (count - unroll - tail) // unroll
    with eng.Fori(0, turns) as it:
        for k in range(unroll):
            body(it * unroll + (unroll + k), k, it + 1)
    for s in range((turns + 1) * unroll, count):
        body(s, s % unroll, turns + 1)


def since(s, n):
    return not isinstance(s, int) or s >= n


class Link:

    def __init__(self, eng, sem, s=0, each=0):
        self.eng, self.sem, self.base, self.each, self.n = eng, sem, s * each, each, 0

    def __call__(self, ins):
        ins.then_inc(self.sem, 1)
        self.n += 1
        assert not self.each or self.n <= self.each, (self.n, self.each)
        self.eng.wait_ge(self.sem, self.base + self.n)


class Phase:

    def __init__(self, nc, name):
        self.nc, self.name, self.ctx = nc, name, ExitStack()

    def __enter__(self):
        self.ctx.__enter__()
        return self

    def __exit__(self, *a):
        return self.ctx.__exit__(*a)

    def sb(self, name, shape, dt=F32):
        return self.ctx.enter_context(self.nc.sbuf_tensor(f"{self.name}_{name}", shape, dt))

    def ps(self, name, shape, dt=F32):
        return self.ctx.enter_context(self.nc.psum_tensor(f"{self.name}_{name}", shape, dt))

    def sem(self, name):
        return self.ctx.enter_context(self.nc.semaphore(f"{self.name}_{name}"))

    def sems(self, name, n):
        return [self.sem(f"{name}{k}") for k in range(n)]


def rows(dram, i, n=P):
    return dram[bass.ds(i * n, n), :]


def fold_attention_weights(nc, t, r):
    with Phase(nc, "fold") as f:
        w_nat = f.sb("w_nat", [P, KC, C])
        a_col = f.sb("a_col", [P, KC, 2])
        a_diag = f.sb("a_diag", [P, KC, 2, H])
        wa = f.ps("wa", [P, KC, 2 * H])
        loaded, diag_ready, wa_ready, done = (f.sem(s) for s in ("loaded", "diag", "wa", "done"))
        block = f.ctx.enter_context(nc.Block())

        @block.sync
        def _(sp):
            sp.dma_start(r.ident[:, :], t["c_ident"]).then_inc(loaded, 16)
            sp.dma_start(r.jrow[:, :], t["c_jrow"]).then_inc(loaded, 16)
            sp.dma_start(r.jcol[:, :], t["c_jcol"]).then_inc(loaded, 16)
            sp.dma_start(r.headsel[:, :], t["c_headsel"]).then_inc(loaded, 16)
            sp.dma_start(r.valid[:, :], t["c_valid"]).then_inc(loaded, 16)
            sp.dma_start(r.wall[:, :, 0:C], t["wT"].rearrange("(k p) n -> p k n", p=P)).then_inc(loaded, 16)
            sp.dma_start(w_nat[:, :, :], t["w"].rearrange("(k p) n -> p k n", p=P)).then_inc(loaded, 16)
            sp.dma_start(a_col[:, :, :], t["a_col"].rearrange("(k p) n -> p k n", p=P)).then_inc(loaded, 16)
            sp.wait_ge(loaded, 8 * 16)

        @block.vector
        def _(dve):
            dve.wait_ge(loaded, 8 * 16)
            for k in range(KC):
                for side in range(2):
                    nc.vector.tensor_scalar(a_diag[:, k, side, :], r.headsel[:, k * H:(k + 1) * H],
                                            a_col[:, k, side:side + 1], None, ALU.mult).then_inc(diag_ready, 1)
            dve.wait_ge(wa_ready, 1)
            nc.vector.tensor_copy(r.wall[:, :, C:C + 2 * H], wa[:, :, :]).then_inc(done, 1)

        @block.tensor
        def _(pe):
            pe.wait_ge(diag_ready, 4)
            for k in range(KC):
                for j in range(KC):
                    last = nc.tensor.matmul(wa[:, k, :], w_nat[:, j, k * P:(k + 1) * P], a_diag[:, j, :, :],
                                            start=(j == 0), stop=(j == KC - 1))
            last.then_inc(wa_ready, 1)


def make_steps(nc, t, r, ph, tiles, count, last_dst, gcol_dram):
    groups = T // tiles
    chunks = groups // NW
    half = count // 2
    with Phase(nc, f"steps{tiles}") as f:
        raw = f.sb("raw", [NW, chunks], I32)
        win = f.sb("win", [NW, chunks], I32)
        winf = f.sb("winf", [NW, chunks])
        gcol = f.sb("gcol", [NW, chunks])
        start = f.sb("start", [NW, chunks])
        sidx = f.sb("sidx", [P, count])
        begun = f.sb("begun", [NW, chunks, count])
        ones = f.sb("ones", [NW, P])
        gs = f.sb("gs", [P, count])
        ws = f.sb("ws", [P, count])
        wc = f.sb("wc", [P, count])
        acc = f.ps("acc", [P, 2, 512])
        loaded, link_s, begun_s, acc_s = (f.sem(s) for s in ("loaded", "link", "begun", "acc"))
        block = f.ctx.enter_context(nc.Block())

        @block.sync
        def _(sp):
            sp.dma_start(raw[:, :], last_dst).then_inc(loaded, 16)
            sp.dma_start(sidx[:, :], t["c_sidx"][:, 0:count]).then_inc(loaded, 16)
            sp.dma_start(gcol[:, :], gcol_dram).then_inc(loaded, 16)
            sp.wait_ge(loaded, 48)

        @block.vector
        def _(dve):
            link = Link(dve, link_s)
            dve.wait_ge(loaded, 48)
            link(nc.vector.memset(ones[:, :], 1.0))
            link(nc.vector.tensor_scalar(win[:, :], raw[:, :], 7, None, ALU.arith_shift_right))
            link(nc.vector.tensor_copy(winf[:, :], win[:, :]))
            link(nc.vector.tensor_tensor(start[:, :], winf[:, :], gcol[:, :], ALU.add))
            for c in range(chunks):
                nc.vector.tensor_scalar(begun[:, c, :], sidx[0:NW, :], start[:, c:c + 1], None,
                                        ALU.is_ge).then_inc(begun_s, 1)
            dve.wait_ge(acc_s, 1)
            for a in range(2):
                link(nc.vector.tensor_scalar(gs[:, a * half:(a + 1) * half], acc[:, a, 0:half],
                                             float(groups - 1), None, ALU.min))
            link(nc.vector.tensor_tensor(ws[:, :], sidx[:, :], gs[:, :], ALU.subtract))
            link(nc.vector.tensor_scalar(wc[:, :], ws[:, :], float(NW - 1), None, ALU.min))
            link(nc.vector.tensor_copy(ph.g_int[:, :], gs[:, :]))
            link(nc.vector.tensor_copy(ph.w_int[:, :], wc[:, :]))
            link(nc.vector.tensor_scalar(ph.w_node[:, :], ws[:, :], float(P), None, ALU.mult))
            if ph.j_node is not None:
                link(nc.vector.tensor_scalar(ph.j_node[:, :], ph.w_node[:, :], r.jcol[:, 0:1], None, ALU.add))

        @block.tensor
        def _(pe):
            pe.wait_ge(begun_s, chunks)
            for a in range(2):
                for c in range(chunks):
                    last = nc.tensor.matmul(acc[:, a, 0:half], ones[:, :], begun[:, c, a * half:(a + 1) * half],
                                            start=(c == 0), stop=(c == chunks - 1))
            last.then_inc(acc_s, 1)


def rstd_of(nc, link, var, v, a, y):
    link(nc.vector.tensor_scalar(v, var, LN_EPS, None, ALU.add))
    link(nc.vector.tensor_scalar(y.bitcast(I32), v.bitcast(I32), -0.5, float(0x5F3759DF), ALU.mult, ALU.add))
    for _ in range(3):
        link(nc.vector.tensor_tensor(a, y, y, ALU.mult))
        link(nc.vector.scalar_tensor_tensor(a, a, -0.5, v, ALU.mult, ALU.mult))
        link(nc.vector.scalar_tensor_tensor(y, a, 1.5, y, ALU.add, ALU.mult))


class Stats:

    def __init__(self, nc, f, name, n=BL):
        self.nc, self.n = nc, n
        self.st = f.sb(name + "_st", [P, 2, n, 6])
        self.mv = f.sb(name + "_mv", [P, 2, n, 2])
        self.tmp = f.sb(name + "_tmp", [P, 2, 2, n])
        self.rstd = f.sb(name + "_rstd", [P, 2, n])

    def take(self, u, b, src):
        return self.nc.vector.bn_stats(self.st[:, u, b, :], src)

    def close(self, dve, link, hold_s, u, last):
        link(last)
        dve.sem_inc(hold_s, 1)
        for b in range(self.n):
            last = self.nc.vector.bn_aggr(self.mv[:, u, b, :], self.st[:, u, b, :])
        link(last)
        rstd_of(self.nc, link, self.mv[:, u, :, 1], self.tmp[:, u, 0, :], self.tmp[:, u, 1, :], self.rstd[:, u, :])

    def mean(self, u, b):
        return self.mv[:, u, b, 0:1]

    def scale(self, u, b):
        return self.rstd[:, u, b:b + 1]


def block_rows(dram, i):
    return dram[bass.ds(i * (BL * P), BL * P), :].rearrange("(b p) n -> p b n", p=P)


def node_pass(nc, t, r):
    with Phase(nc, "node") as f:
        wqkv = f.sb("wqkv", [P, KC, 3 * C])
        x = f.sb("x", [P, 2, BL, C])
        xn = f.sb("xn", [P, 2, BL, C])
        h = f.sb("h", [P, 2, BL, C + 2 * H])
        hsp = f.sb("hsp", [P, 2, BL, 2, C + H], F32R)
        q = f.sb("q", [P, 2, BL, C])
        xnT = f.sb("xnT", [P, 2, KC * P])
        neg = f.sb("neg", [P, 2, 2, C])
        ex = f.sb("ex", [P, 2, 2, C])
        k = f.sb("k", [P, 2, C])
        v = f.sb("v", [P, 2, KC, P + 1])
        zero = f.sb("zero", [P, P])
        stats = Stats(nc, f, "x")
        p_t = f.ps("p_t", [P, 2, C])
        p_q = f.ps("p_q", [P, 2, 512])
        p_h = f.ps("p_h", [P, 2, 512])
        p_kv = f.ps("p_kv", [P, 2, 2, C])
        p_sum = f.ps("p_sum", [P, KC, P + 1])
        x_in = f.sems("x_in", 2)
        stored = f.sems("stored", 2)
        (w_in, xn_s, xT_s, xTc_s, mm_s, h_s, h_hi_s, h_lo_s, neg_s, exp_s, q_s, k_s, v_s, kv_used, link_s, zero_s,
         sum_s, hold_s) = (f.sem(s) for s in (
             "w_in", "xn", "xT", "xTc", "mm", "h", "h_hi", "h_lo", "neg", "exp", "q", "k", "v", "kv_used",
             "link", "zero", "sum", "hold"))
        block = f.ctx.enter_context(nc.Block())

        @block.sync
        def _(sp):
            for u in range(2):
                sp.dma_start(x[:, u, :, :], block_rows(t["x"], u)).then_inc(x_in[u], 16)
            sp.dma_start(wqkv[:, :, :], t["wqkvT"].rearrange("(k p) n -> p k n", p=P)).then_inc(w_in, 16)
            sp.dma_start(r.headmask[:, :], t["c_headmask"]).then_inc(w_in, 16)

            def body(i, u, turn):
                sp.wait_ge(xn_s, i * BL + BL)
                sp.dma_start(x[:, u, :, :], block_rows(t["x"], i + 2)).then_inc(x_in[u], 16)
                sp.dma_start(block_rows(t["d_xn"], i), xn[:, u, :, :]).then_inc(stored[u], 16)
                sp.wait_ge(k_s, i * BL + BL)
                sp.dma_start(block_rows(t["d_hw"], i),
                             hsp[:, u, :, :, :].rearrange("p b a c -> p b (a c)").bitcast(F32)).then_inc(stored[u], 16)
                sp.dma_start(block_rows(t["d_h"], i), h[:, u, :, 0:C]).then_inc(stored[u], 16)
                sp.dma_start(block_rows(t["d_as"], i), h[:, u, :, C + H:C + 2 * H]).then_inc(stored[u], 16)
                sp.dma_start(t["d_q"][:, bass.ds(i * (BL * C), BL * C)],
                             q[:, u, :, :].rearrange("p b c -> p (b c)")).then_inc(stored[u], 16)

            run(sp, NB, 2, body)
            for u in range(2):
                sp.wait_ge(x_in[u], 16 * (NB // 2 + 1))
                sp.wait_ge(stored[u], 80 * (NB // 2))

        @block.vector
        def _(dve):
            nc.vector.memset(zero[:, :], 0.0).then_inc(zero_s, 1)

            def normal(m, u, b):
                nc.vector.tensor_scalar(xn[:, u, b, :], x[:, u, b, :], stats.mean(u, b), stats.scale(u, b),
                                        ALU.subtract, ALU.mult).then_inc(xn_s, 1)

            def statistics(i, u, turn, link):
                dve.wait_ge(x_in[u], turn * 16 + 16)
                for b in range(BL):
                    last = stats.take(u, b, x[:, u, b, :])
                stats.close(dve, link, hold_s, u, last)

            def leave(m, w, u, b):
                dve.wait_ge(mm_s, m + 1)
                nc.vector.tensor_scalar(neg[:, w, 0, :], p_kv[:, w, 0, :], 0.0, None, ALU.min)
                nc.vector.tensor_scalar(neg[:, w, 1, :], p_q[:, w, 0:C], 0.0, None, ALU.min).then_inc(neg_s, 1)
                nc.vector.tensor_copy(h[:, u, b, :], p_h[:, w, 0:C + 2 * H]).then_inc(h_s, 1)
                if since(m, 2):
                    dve.wait_ge(kv_used, m - 1)
                nc.vector.tensor_copy(v[:, w, :, P], r.valid[:, bass.ds(m, 1)].broadcast_to([P, KC]))
                dve.wait_ge(exp_s, m + 1)
                nc.vector.scalar_tensor_tensor(q[:, u, b, :], p_q[:, w, 0:C], 0.0, ex[:, w, 1, :],
                                               ALU.max, ALU.add).then_inc(q_s, 1)
                dve.wait_ge(h_hi_s, m + 1)
                nc.vector.tensor_tensor(hsp[:, u, b, 1, :], h[:, u, b, 0:C + H], hsp[:, u, b, 0, :].bitcast(F32),
                                        ALU.subtract).then_inc(h_lo_s, 1)
                nc.vector.scalar_tensor_tensor(k[:, w, :], p_kv[:, w, 0, :], 0.0, ex[:, w, 0, :],
                                               ALU.max, ALU.add).then_inc(k_s, 1)

            def body(i, u, turn):
                more = not isinstance(i, int) or i < NB - 1
                for b in range(BL):
                    m = i * BL + b
                    if b < BL - 2:
                        normal(m + 2, u, b + 2)
                    elif more:
                        if since(i, 1) and b == BL - 2:
                            dve.wait_ge(stored[1 - u], (turn + u) * 80)
                        normal(m + 2, 1 - u, b + 2 - BL)
                    leave(m, (u * BL + b) % 2, u, b)
                    if b == 2 and more:
                        statistics(i + 1, 1 - u, turn + u, Link(dve, link_s, i + 1, 13))

            statistics(0, 0, 0, Link(dve, link_s, 0, 13))
            normal(0, 0, 0)
            normal(1, 0, 1)
            run(dve, NB, 2, body, tail=1)
            dve.wait_ge(sum_s, 1)
            for c in range(KC):
                nc.vector.tensor_tensor(r.kvbd[:, c, 0:P], p_sum[:, c, 0:P], r.headmask[:, :], ALU.mult).then_inc(link_s, 1)
                nc.vector.tensor_scalar(r.kvbd[:, c, P:P + 4], r.headsel[:, 0:4], p_sum[:, c, P:P + 1], None,
                                        ALU.mult).then_inc(link_s, 1)

        @block.scalar
        def _(act):
            def turned(m, w):
                act.wait_ge(xT_s, m + 1)
                nc.scalar.copy(xnT[:, w, :], p_t[:, w, :]).then_inc(xTc_s, 1)

            def body(i, u, turn):
                for b in range(BL):
                    m, w = i * BL + b, (u * BL + b) % 2
                    if not isinstance(i, int) or m + 1 < NW:
                        turned(m + 1, 1 - w)
                    act.wait_ge(neg_s, m + 1)
                    if since(m, 2):
                        act.wait_ge(kv_used, m - 1)
                    nc.scalar.copy(v[:, w, :, 0:P], p_kv[:, w, 1, :].rearrange("p (c n) -> p c n", c=KC)).then_inc(v_s, 1)
                    act.wait_ge(v_s, m + 1)
                    nc.scalar.activation(ex[:, w, :, :], neg[:, w, :, :], ACT.Exp).then_inc(exp_s, 1)
                    act.wait_ge(h_s, m + 1)
                    if since(i, 2) and b == 0:
                        act.wait_ge(stored[u], turn * 80)
                    nc.scalar.copy(hsp[:, u, b, 0, :], h[:, u, b, 0:C + H]).then_inc(h_hi_s, 1)

            turned(0, 0)
            run(act, NB, 2, body, tail=1)

        @block.tensor
        def _(pe):
            pe.wait_ge(w_in, 32)
            pe.wait_ge(zero_s, 1)
            for c in range(KC):
                nc.tensor.matmul(p_sum[:, c, :], zero[:, :], wqkv[:, 0, 0:P + 1], start=(c == 0), stop=False,
                                 skip_group_check=True)

            def turn_tile(m, w, u, b):
                pe.wait_ge(xn_s, m + 1)
                if since(m, 1):
                    pe.wait_ge(xTc_s, m)
                for c in range(KC):
                    last = nc.tensor.transpose(p_t[:, w, c * P:(c + 1) * P], xn[:, u, b, c * P:(c + 1) * P],
                                               r.ident[:, :])
                last.then_inc(xT_s, 1)

            def products(m, w):
                pe.wait_ge(xTc_s, m + 1)
                if since(m, 2):
                    pe.wait_ge(h_lo_s, m - 1)
                    pe.wait_ge(k_s, m - 1)
                for c in range(KC):
                    nc.tensor.matmul(p_h[:, w, 0:C + 2 * H], xnT[:, w, c * P:(c + 1) * P], r.wall[:, c, :],
                                     start=(c == 0), stop=(c == KC - 1))
                for c in range(KC):
                    nc.tensor.matmul(p_kv[:, w, :, :], xnT[:, w, c * P:(c + 1) * P], wqkv[:, c, C:3 * C],
                                     start=(c == 0), stop=(c == KC - 1))
                for o in range(KC):
                    for c in range(KC):
                        last = nc.tensor.matmul(p_q[:, w, o * P:(o + 1) * P], wqkv[:, c, o * P:(o + 1) * P],
                                                xnT[:, w, c * P:(c + 1) * P], start=(c == 0), stop=(c == KC - 1))
                last.then_inc(mm_s, 1)

            def sums(m, w):
                pe.wait_ge(k_s, m + 1)
                pe.wait_ge(v_s, m + 1)
                for c in range(KC):
                    last = nc.tensor.matmul(p_sum[:, c, :], k[:, w, c * P:(c + 1) * P], v[:, w, c, :],
                                            start=False, stop=False, skip_group_check=True)
                last.then_inc(kv_used, 1)

            def body(i, u, turn):
                for b in range(BL):
                    m, w = i * BL + b, (u * BL + b) % 2
                    if b < BL - 1:
                        turn_tile(m + 1, 1 - w, u, b + 1)
                    elif not isinstance(i, int) or i < NB - 1:
                        turn_tile(m + 1, 1 - w, 1 - u, 0)
                    products(m, w)
                    if since(m, 1):
                        sums(m - 1, 1 - w)

            turn_tile(0, 0, 0, 0)
            run(pe, NB, 2, body, tail=1)
            sums(NW - 1, (NW - 1) % 2)
            for c in range(KC):
                last = nc.tensor.matmul(p_sum[:, c, :], zero[:, :], wqkv[:, 0, 0:P + 1], start=False, stop=True,
                                        skip_group_check=True)
            last.then_inc(sum_s, 1)


def mixer(nc, t, r):
    HC = H // KC
    AHEAD = BL + 2
    LATE = {b: [] for b in range(BL)}
    for j in range(BL):
        LATE[2 + j * (BL - 2) // BL].append(j)
    with Phase(nc, "mix") as f:
        w1 = f.sb("w1", [P, KC, C])
        w2 = f.sb("w2", [P, KC, C])
        b1 = f.sb("b1", [P, KC])
        vec = f.sb("vec", [P, 6, C])
        q = f.sb("q", [P, 2, BL, C])
        xn = f.sb("xn", [P, 2, BL, C])
        x = f.sb("x", [P, 2, BL, C])
        z = f.sb("z", [P, 2, KC, HC])
        y = f.sb("y", [P, 2, BL, C])
        x1 = f.sb("x1", [P, 2, BL, C])
        x1b = f.sb("x1b", [P, 2, BL, C])
        o = f.sb("o", [P, 2, BL, C])
        x1T = f.sb("x1T", [P, 2, C])
        hT = f.sb("hT", [P, 2, KC, P])
        stats1, stats2 = Stats(nc, f, "one"), Stats(nc, f, "two")
        p_t = f.ps("p_t", [P, 2, 512])
        p_x = f.ps("p_x", [P, 2, 512])
        p_h = f.ps("p_h", [P, 2, 512])
        p_y = f.ps("p_y", [P, 2, 512])
        qxn_in, x_in, stored = f.sems("qxn_in", 2), f.sems("x_in", 2), f.sems("stored", 2)
        (w_in, t_s, a_s, x1_s, xT_s, xTc_s, h_s, hT_s, y_s, o_s, x1b_s, sum2_s, norm2_s, a_link, x1_link, st1_link,
         st2_link, n2_link, bias_link, hold_s) = (f.sem(s) for s in (
             "w_in", "t", "a", "x1", "xT", "xTc", "h", "hT", "y", "o", "x1b", "sum2", "norm2", "a_link", "x1_link",
             "st1_link", "st2_link", "n2_link", "bias_link", "hold"))
        pool_hold = f.sem("pool_hold")
        block = f.ctx.enter_context(nc.Block())

        def at(i, u, b, d):
            n = u * BL + b + d
            return (n // BL) % 2, n % BL, n % 2

        def exists(i, b, d):
            return not isinstance(i, int) or i * BL + b + d < NW

        @block.sync
        def _(sp):
            sp.dma_start(w1[:, :, :], t["w1T"].rearrange("(k p) n -> p k n", p=P)).then_inc(w_in, 16)
            sp.dma_start(w2[:, :, :], t["w2T"].rearrange("(k p) n -> p k n", p=P)).then_inc(w_in, 16)
            sp.dma_start(b1[:, :], t["b1_col"]).then_inc(w_in, 16)
            for k, v in enumerate((t["g1"], t["be1"], t["g2"], t["be2"], t["b2"], t["bias"])):
                sp.dma_start(vec[:, k, :], v.broadcast_to([P, C])).then_inc(w_in, 16)

            def load(i, u):
                sp.dma_start(q[:, u, :, :].rearrange("p b c -> p (b c)"),
                             t["d_q"][:, bass.ds(i * (BL * C), BL * C)]).then_inc(qxn_in[u], 16)
                sp.dma_start(xn[:, u, :, :], block_rows(t["d_xn"], i)).then_inc(qxn_in[u], 16)

            def body(i, u, turn):
                if not isinstance(i, int) or i + 2 < NB:
                    sp.wait_ge(a_s, i * BL + BL)
                    load(i + 2, u)
                if since(i, 2):
                    sp.wait_ge(o_s, i * BL - BL)
                    sp.dma_start(block_rows(t["d_x1"], i - 2), o[:, u, :, :]).then_inc(stored[u], 16)
                sp.dma_start(x[:, u, :, :], block_rows(t["x"], i)).then_inc(x_in[u], 16)

            load(0, 0)
            load(1, 1)
            run(sp, NB, 2, body, tail=2)
            for i in range(NB - 2, NB):
                sp.wait_ge(o_s, i * BL + BL)
                sp.dma_start(block_rows(t["d_x1"], i), o[:, i % 2, :, :]).then_inc(stored[i % 2], 16)
            for u in range(2):
                sp.wait_ge(qxn_in[u], 32 * (NB // 2))
                sp.wait_ge(x_in[u], 16 * (NB // 2))
                sp.wait_ge(stored[u], 16 * (NB // 2))

        @block.vector
        def _(dve):
            dve.wait_ge(w_in, 9 * 16)
            g1, be1, g2, be2 = (vec[:, k, :] for k in range(4))
            Link(dve, bias_link)(nc.vector.tensor_tensor(be2, be2, vec[:, 5, :], ALU.add))

            def attend(n, w, u, b, turn):
                link = Link(dve, a_link, n, 4)
                if b == 0:
                    dve.wait_ge(qxn_in[u], turn * 32 + 32)
                dve.wait_ge(t_s, n + 1)
                pt = p_t[:, w, 0:KC * (P + HC)].rearrange("p (c n) -> p c n", c=KC)
                link(nc.vector.tensor_scalar(z[:, w, :, :], pt[:, :, P:P + HC], 1e-6, None, ALU.add))
                link(nc.vector.reciprocal(z[:, w, :, :], z[:, w, :, :]))
                y4 = y[:, u, b, :].rearrange("p (c h d) -> p c h d", c=KC, h=HC)
                for c in range(KC):
                    last = nc.vector.tensor_tensor(y4[:, c, :, :], pt[:, c, 0:P].rearrange("p (h d) -> p h d", h=HC),
                                                   z[:, w, c, :, None].broadcast_to([P, HC, D]), ALU.mult)
                link(last)
                link(nc.vector.tensor_tensor(y[:, u, b, :], y[:, u, b, :], xn[:, u, b, :], ALU.add))
                dve.sem_inc(a_s, 1)
                return stats1.take(u, b, y[:, u, b, :])

            def normal1(n, u, b):
                link = Link(dve, x1_link, n, 1)
                link(nc.vector.scalar_tensor_tensor(x1[:, u, b, :], y[:, u, b, :], stats1.mean(u, b), g1,
                                                    ALU.subtract, ALU.mult))
                nc.vector.scalar_tensor_tensor(x1[:, u, b, :], x1[:, u, b, :], stats1.scale(u, b), be1,
                                               ALU.mult, ALU.add).then_inc(x1_s, 1)

            def sum2(n, w, u, b):
                dve.wait_ge(y_s, n + 1)
                dve.wait_ge(x1b_s, n + 1)
                Link(dve, sum2_s, n, 1)(nc.vector.tensor_tensor(o[:, u, b, :], p_y[:, w, 0:C], x1b[:, u, b, :], ALU.add))
                return stats2.take(u, b, o[:, u, b, :])

            def normal2(n, u, b):
                link = Link(dve, n2_link, n, 1)
                link(nc.vector.scalar_tensor_tensor(o[:, u, b, :], o[:, u, b, :], stats2.mean(u, b), g2,
                                                    ALU.subtract, ALU.mult))
                nc.vector.scalar_tensor_tensor(o[:, u, b, :], o[:, u, b, :], stats2.scale(u, b), be2,
                                               ALU.mult, ALU.add).then_inc(norm2_s, 1)

            def body(i, u, turn):
                for b in range(BL):
                    m = i * BL + b
                    if exists(i, b, 2):
                        v, a, _w = at(i, u, b, 2)
                        normal1(m + 2, v, a)
                    if since(m, 2):
                        v, a, w = at(i, u, b, 2 * BL - 2)
                        if a == 0 and since(i, 2):
                            dve.wait_ge(stored[v], turn * 16)
                        last = sum2(m - 2, w, v, a)
                        if b == 1:
                            stats2.close(dve, Link(dve, st2_link, i - 1, 13), hold_s, v, last)
                    if since(i, 1):
                        for j in LATE[b]:
                            normal2((i - 1) * BL + j, 1 - u, j)
                    if exists(i, b, AHEAD):
                        v, a, w = at(i, u, b, AHEAD)
                        last = attend(m + AHEAD, w, v, a, turn + (u * BL + b + AHEAD) // (2 * BL))
                        if a == BL - 1:
                            stats1.close(dve, Link(dve, st1_link, i + 1, 13), hold_s, v, last)

            for n in range(AHEAD):
                last = attend(n, n % 2, n // BL, n % BL, 0)
                if n == BL - 1:
                    stats1.close(dve, Link(dve, st1_link, 0, 13), hold_s, 0, last)
            for n in range(2):
                normal1(n, 0, n)
            run(dve, NB, 2, body, tail=2)
            for n in (NW - 2, NW - 1):
                last = sum2(n, n % 2, (NB - 1) % 2, n % BL)
            stats2.close(dve, Link(dve, st2_link, NB - 1, 13), hold_s, (NB - 1) % 2, last)
            for j in range(BL):
                normal2(NW - BL + j, (NB - 1) % 2, j)

        @block.gpsimd
        def _(pool):
            pool.wait_ge(w_in, 9 * 16)

            def add_b2(n, u, b):
                pool.wait_ge(x1_s, n + 1)
                nc.gpsimd.tensor_tensor(x1b[:, u, b, :], x1[:, u, b, :], vec[:, 4, :], ALU.add).then_inc(x1b_s, 1)

            def add_x(n, u, b):
                pool.wait_ge(norm2_s, n + 1)
                nc.gpsimd.tensor_tensor(o[:, u, b, :], o[:, u, b, :], x[:, u, b, :], ALU.add).then_inc(o_s, 1)

            def body(i, u, turn):
                for b in range(BL):
                    if exists(i, b, 2):
                        v, a, _w = at(i, u, b, 2)
                        add_b2(i * BL + b + 2, v, a)
                    if since(i, 1):
                        if b == 2:
                            pool.wait_ge(x_in[1 - u], (turn + u) * 16)
                            pool.sem_inc(pool_hold, 1)
                        for j in LATE[b]:
                            add_x((i - 1) * BL + j, 1 - u, j)

            for n in range(2):
                add_b2(n, 0, n)
            run(pool, NB, 2, body, tail=2)
            pool.wait_ge(x_in[(NB - 1) % 2], (NB // 2) * 16)
            for j in range(BL):
                add_x(NW - BL + j, (NB - 1) % 2, j)

        @block.scalar
        def _(act):
            act.wait_ge(w_in, 9 * 16)

            def turned(n, w):
                act.wait_ge(xT_s, n + 1)
                nc.scalar.copy(x1T[:, w, :], p_x[:, w, 0:C]).then_inc(xTc_s, 1)

            def body(i, u, turn):
                for b in range(BL):
                    m, w = i * BL + b, (u * BL + b) % 2
                    if exists(i, b, 1):
                        turned(m + 1, 1 - w)
                    act.wait_ge(h_s, m + 1)
                    for c in range(KC):
                        last = nc.scalar.activation(hT[:, w, c, :], p_h[:, w, c * P:(c + 1) * P], ACT.Gelu,
                                                    bias=b1[:, c:c + 1])
                    last.then_inc(hT_s, 1)

            turned(0, 0)
            run(act, NB, 2, body, tail=2)

        @block.tensor
        def _(pe):
            pe.wait_ge(w_in, 9 * 16)

            def read(n, w, u, b, turn):
                if b == 0:
                    pe.wait_ge(qxn_in[u], turn * 32 + 32)
                if since(n, 2):
                    pe.wait_ge(a_s, n - 1)
                for c in range(KC):
                    last = nc.tensor.matmul(p_t[:, w, c * (P + HC):(c + 1) * (P + HC)], q[:, u, b, c * P:(c + 1) * P],
                                            r.kvbd[:, c, :], start=True, stop=True)
                last.then_inc(t_s, 1)

            def turn_tile(n, w, u, b):
                pe.wait_ge(x1_s, n + 1)
                for c in range(KC):
                    last = nc.tensor.transpose(p_x[:, w, c * P:(c + 1) * P], x1[:, u, b, c * P:(c + 1) * P],
                                               r.ident[:, :])
                last.then_inc(xT_s, 1)

            def inner(n, w):
                pe.wait_ge(xTc_s, n + 1)
                for c in range(KC):
                    for k in range(KC):
                        last = nc.tensor.matmul(p_h[:, w, c * P:(c + 1) * P], w1[:, k, c * P:(c + 1) * P],
                                                x1T[:, w, k * P:(k + 1) * P], start=(k == 0), stop=(k == KC - 1))
                last.then_inc(h_s, 1)

            def outer(n, w):
                pe.wait_ge(hT_s, n + 1)
                if since(n, 2):
                    pe.wait_ge(sum2_s, n - 1)
                for k in range(KC):
                    last = nc.tensor.matmul(p_y[:, w, 0:C], hT[:, w, k, :], w2[:, k, :],
                                            start=(k == 0), stop=(k == KC - 1))
                last.then_inc(y_s, 1)

            def body(i, u, turn):
                for b in range(BL):
                    m, w = i * BL + b, (u * BL + b) % 2
                    if exists(i, b, 1):
                        v, a, _w = at(i, u, b, 1)
                        turn_tile(m + 1, 1 - w, v, a)
                    inner(m, w)
                    if exists(i, b, AHEAD):
                        v, a, w_ = at(i, u, b, AHEAD)
                        read(m + AHEAD, w_, v, a, turn + (u * BL + b + AHEAD) // (2 * BL))
                    if since(m, 1):
                        outer(m - 1, 1 - w)

            for n in range(AHEAD):
                read(n, n % 2, n // BL, n % BL, 0)
            turn_tile(0, 0, 0, 0)
            run(pe, NB, 2, body, tail=2)
            outer(NW - 1, (NW - 1) % 2)


def edge_scores(nc, t, r, ph):
    W = GA * P
    CX = C + H
    with Phase(nc, "score") as f:
        hw = f.sb("hw", [P, UE, 2, CX], F32R)
        dstb = f.sb("dstb", [P, UE, W], I32)
        ea = f.sb("ea", [3 * EF, UE, W], F32R)
        mt = f.sb("mt", [P, UE, W], F32R)
        rel = f.sb("rel", [P, 2, 2 * C])
        pr = f.sb("pr", [P, 2, 2 * C])
        red = f.sb("red", [P, 2, GA * H])
        ew = f.sb("ew", [3 * EF, C], F32R)
        sring = f.sb("sring", [P, 2, GA], U32)
        gring = f.sb("gring", [P, 2, GA, H])
        p_enc = f.ps("p_enc", [P, 2, 2 * C])
        p_hd = f.ps("p_hd", [P, 2, 2 * C])
        p_ad = f.ps("p_ad", [P, 2, 512])
        ins = f.sems("ins", UE)
        gat = f.sems("gat", 2)
        w_in, mt_s, enc_s, hd_s, rel_s, pr_s, red_s, add_s, turn_s, ring_s, out_s, link_s = (
            f.sem(s) for s in ("w_in", "mt", "enc", "hd", "rel", "pr", "red", "add", "turn", "ring", "out", "link"))
        block = f.ctx.enter_context(nc.Block())
        PAIRS = GA // 2

        @block.sync
        def _(sp):
            sp.dma_start(ew[:, :].bitcast(F32), t["d_ew"]).then_inc(w_in, 16)

            def body(s, u, turn):
                if since(s, UE):
                    sp.wait_ge(hd_s, (s - UE) * PAIRS + PAIRS)
                g = sp.value_load(ph.g_int[0:1, bass.ds(s, 1)], min_val=0, max_val=T // GA - 1)
                w = sp.value_load(ph.w_int[0:1, bass.ds(s, 1)], min_val=0, max_val=NW - 1)
                sp.dma_start(hw[:, u, :, :].bitcast(F32), rows(t["d_hw"], w).rearrange("p (a c) -> p a c", a=2)).then_inc(ins[u], 16)
                sp.dma_start(dstb[:, u, :], t["dst_row"][:, bass.ds(g * W, W)].broadcast_to([P, W])).then_inc(ins[u], 16)
                sp.dma_start(ea[:, u, :].bitcast(F32), t["d_ea"][:, bass.ds(g * W, W)]).then_inc(ins[u], 16)

            run(sp, SA, UE, body)
            for u in range(UE):
                sp.wait_ge(ins[u], 48 * (SA // UE))

        @block.gpsimd
        def _(pool):
            def take(i, u, turn):
                pool.wait_ge(gat[u], turn * (16 * GA) + 16 * GA)
                nc.gpsimd.tensor_copy(ph.asrc[:, bass.ds(i * (GA * H), GA * H)],
                                      gring[:, u, :, :].rearrange("p k h -> p (k h)")).then_inc(out_s, 1)

            def body(i, u, turn):
                if since(i, 2):
                    take(i - 2, u, turn - 1)
                    pool.wait_ge(out_s, i - 1)
                nc.gpsimd.tensor_copy(sring[:, u, :], r.src[:, bass.ds(i * GA, GA)]).then_inc(ring_s, 1)
                pool.wait_ge(ring_s, i + 1)
                pool.sem_inc(turn_s, 1)
                for k in range(GA):
                    nc.gpsimd.indirect_dma_start(gring[:, u, k, :], None, t["d_as"][:, :],
                                                 bass.IndirectOffsetOnAxis(sring[:, u, k:k + 1], 0)).then_inc(gat[u], 16)

            n = T // GA
            run(pool, n, 2, body)
            for i in (n - 2, n - 1):
                take(i, i % 2, i // 2)

        @block.vector
        def _(dve):
            nc.vector.memset(ph.al[:, :], 0.0).then_inc(add_s, 1)

            def onehot(s, u, turn):
                dve.wait_ge(ins[u], turn * 48 + 48)
                nc.vector.tensor_scalar(mt[:, u, :], dstb[:, u, :], ph.j_node[:, bass.ds(s, 1)], None,
                                        ALU.is_equal).then_inc(mt_s, 1)

            def body(s, u, turn):
                v = u % 2
                link = Link(dve, link_s, s, 1)
                g = dve.value_load(ph.g_int[0:1, bass.ds(s, 1)], min_val=0, max_val=T // GA - 1)
                if not isinstance(s, int) or s < SA - 1:
                    onehot(s + 1, (u + 1) % UE, turn + (u == UE - 1))
                for p in range(PAIRS):
                    m = s * PAIRS + p
                    dve.wait_ge(hd_s, m + 1)
                    dve.wait_ge(rel_s, m + 1)
                    if since(s, 1):
                        dve.wait_ge(red_s, m - 1)
                    nc.vector.tensor_tensor(pr[:, p, :], rel[:, p, :], p_hd[:, p, :], ALU.mult).then_inc(pr_s, 1)
                for p in range(PAIRS):
                    m = s * PAIRS + p
                    dve.wait_ge(pr_s, m + 1)
                    nc.vector.tensor_reduce(red[:, v, p * 2 * H:(p + 1) * 2 * H],
                                            pr[:, p, :].rearrange("p (h d) -> p h d", d=D), AX.X, ALU.add).then_inc(red_s, 1)
                dve.wait_ge(red_s, s * PAIRS + PAIRS)
                link(nc.vector.tensor_tensor(red[:, v, :], red[:, v, :], p_ad[:, v, 0:GA * H], ALU.add))
                dve.wait_ge(add_s, s + 1)
                sl = ph.al[:, bass.ds(g * (GA * H), GA * H)]
                nc.vector.tensor_tensor(sl, sl, red[:, v, :], ALU.add).then_inc(add_s, 1)

            onehot(0, 0, 0)
            run(dve, SA, UE, body, tail=1)

        @block.scalar
        def _(act):
            def body(s, u, turn):
                for p in range(PAIRS):
                    m = s * PAIRS + p
                    act.wait_ge(enc_s, m + 1)
                    if since(s, 1):
                        act.wait_ge(pr_s, m - 1)
                    nc.scalar.activation(rel[:, p, :], p_enc[:, p, :], ACT.Relu).then_inc(rel_s, 1)

            run(act, SA, UE, body)

        @block.tensor
        def _(pe):
            pe.wait_ge(w_in, 16)

            def body(s, u, turn):
                v = u % 2
                pe.wait_ge(ins[u], turn * 48 + 48)
                pe.wait_ge(mt_s, s + 1)
                for p in range(PAIRS):
                    m = s * PAIRS + p
                    if since(s, 1):
                        pe.wait_ge(rel_s, m - 1)
                    for k in range(2):
                        e = slice((2 * p + k) * P, (2 * p + k + 1) * P)
                        last = nc.tensor.matmul(p_enc[:, p, k * C:(k + 1) * C], ea[:, u, e], ew[:, :],
                                                start=True, stop=True)
                    last.then_inc(enc_s, 1)
                    if since(s, 1):
                        pe.wait_ge(pr_s, m - 1)
                    if p == 0 and since(s, 2):
                        pe.wait_ge(add_s, s)
                    for k in range(2):
                        e = slice((2 * p + k) * P, (2 * p + k + 1) * P)
                        for part in range(2):
                            nc.tensor.matmul(p_hd[:, p, k * C:(k + 1) * C], mt[:, u, e], hw[:, u, part, 0:C],
                                             start=(part == 0), stop=(part == 1))
                        for part in range(2):
                            last = nc.tensor.matmul(p_ad[:, v, (2 * p + k) * H:(2 * p + k + 1) * H], mt[:, u, e],
                                                    hw[:, u, part, C:CX], start=(part == 0), stop=(part == 1))
                    last.then_inc(hd_s, 1)

            run(pe, SA, UE, body)


def edge_softmax(nc, t, r, ph):
    by_block = lambda x, b: x[:, 0:T * H].rearrange("p (c b h) -> p c b h", c=CH, h=H)[:, :, bass.ds(b, 1), :] \
        .rearrange("p c b h -> p c (b h)")
    pen, db, ex = ph.al, ph.asrc, ph.al
    PIECE = CE // 8
    with Phase(nc, "soft") as f:
        a = f.sb("a", [P, CE])
        slot = f.sb("slot", [P, 2, P])
        back = f.sb("back", [P, 2, P])
        trash = f.sb("trash", [P, 2, PIECE])
        ends = f.sb("ends", [P, 2])
        srow = f.sb("srow", [1, 2, P])
        crow = f.sb("crow", [1, P + H])
        carry = f.sb("carry", [P, 1])
        one = f.sb("one", [1, 1])
        p_a = f.ps("p_a", [P, 2, 512])
        p_e = f.ps("p_e", [P, 2, 512])
        p_row = f.ps("p_row", [1, 2, P])
        p_c = f.ps("p_c", [P, 1])

        link_s, slot_s, turned, got = (f.sem(s) for s in ("t_link", "t_slot", "t_turned", "t_got"))
        with nc.Block() as block:
            @block.vector
            def _(dve):
                def body(b, u, turn):
                    link = Link(dve, link_s, b, 1)
                    o = slot[:, u, :].rearrange("p (c h) -> p c h", h=H)
                    if since(b, 2):
                        dve.wait_ge(turned, b - 1)
                    link(nc.vector.tensor_tensor(o, by_block(ph.al, b), by_block(ph.asrc, b), ALU.add))
                    nc.vector.scalar_tensor_tensor(slot[:, u, :], slot[:, u, :], 0.2, slot[:, u, :],
                                                   ALU.mult, ALU.max).then_inc(slot_s, 1)

                run(dve, TC, 2, body)

            @block.tensor
            def _(pe):
                def body(b, u, turn):
                    pe.wait_ge(slot_s, b + 1)
                    if since(b, 2):
                        pe.wait_ge(got, b - 1)
                    nc.tensor.transpose(p_a[:, u, 0:P], slot[:, u, :], r.ident[:, :]).then_inc(turned, 1)

                run(pe, TC, 2, body)

            @block.scalar
            def _(act):
                def body(b, u, turn):
                    act.wait_ge(turned, b + 1)
                    nc.scalar.copy(a[:, bass.ds(b * P, P)], p_a[:, u, 0:P]).then_inc(got, 1)

                run(act, TC, 2, body)

        dst_in, link_s, rows_s, row_ps, carry_ps, crow_s = (
            f.sem(s) for s in ("dst_in", "s_link", "s_rows", "s_row_ps", "s_carry_ps", "s_crow"))
        with nc.Block() as block:
            @block.sync
            def _(sp):
                for c in range(CH):
                    sp.dma_start(db[c * H:(c + 1) * H, 0:CE + 2].bitcast(I32),
                                 t["dst_ext"][0:1, c * CE:c * CE + CE + 2].broadcast_to([H, CE + 2])).then_inc(dst_in, 16)
                sp.wait_ge(dst_in, 16 * CH)

            @block.vector
            def _(dve):
                link = Link(dve, link_s)
                dve.wait_ge(dst_in, 16 * CH)
                di = db[:, :].bitcast(I32)
                link(nc.vector.memset(one[:, :], 1.0))
                link(nc.vector.tensor_tensor(pen[:, 0:CE + 1], di[:, 0:CE + 1], di[:, 1:CE + 2], ALU.not_equal))
                link(nc.vector.tensor_scalar(pen[:, 0:CE + 1], pen[:, 0:CE + 1], -BIG, None, ALU.mult))

                def sweep(data, out, shift, reverse, n):
                    step = slice(None, None, -1) if reverse else slice(None)
                    state = -BIG
                    for j in (range(7, -1, -1) if reverse else range(8)):
                        a0 = j * PIECE
                        o = trash[:, j % 2, :]
                        link(nc.vector.tensor_tensor_scan(o[:, step], pen[:, shift + a0:shift + a0 + PIECE][:, step],
                                                          data[:, a0:a0 + PIECE][:, step], state, ALU.add, ALU.max))
                        state = o[:, 0:1] if reverse else o[:, PIECE - 1:PIECE]
                    link(nc.vector.tensor_copy(ends[:, 0:1], state))
                    link(nc.vector.tensor_reduce(ends[:, 1:2], pen[:, shift:shift + CE], AX.X, ALU.min))
                    nc.vector.memset(crow[:, :], -BIG).then_inc(rows_s, 1)
                    dve.wait_ge(rows_s, n)
                    dve.wait_ge(row_ps, n)
                    link(nc.vector.tensor_copy(srow[:, :, :], p_row[:, :, :]))
                    for h in range(H):
                        own = srow[:, 0, h:P:H][:, step]
                        through = srow[:, 1, h:P:H][:, step]
                        o = (crow[:, h:P:H] if reverse else crow[:, h + H:P + H:H])[:, step]
                        link(nc.vector.tensor_tensor_scan(o, through, own, -BIG, ALU.add, ALU.max))
                    dve.sem_inc(crow_s, 1)
                    dve.wait_ge(carry_ps, n)
                    link(nc.vector.tensor_copy(carry[:, :], p_c[:, :]))
                    link(nc.vector.tensor_tensor_scan(out[:, 0:CE][:, step], pen[:, shift:shift + CE][:, step],
                                                      data[:, 0:CE][:, step], carry[:, 0:1], ALU.add, ALU.max))

                sweep(a, db, 0, False, 1)
                sweep(db, db, 1, True, 2)
                link(nc.vector.tensor_tensor(a[:, :], a[:, :], db[:, 0:CE], ALU.subtract))

            @block.tensor
            def _(pe):
                for n in (1, 2):
                    pe.wait_ge(rows_s, n)
                    for k in range(2):
                        last = nc.tensor.transpose(p_row[:, k, :], ends[:, k:k + 1], r.ident[:, :])
                    last.then_inc(row_ps, 1)
                    pe.wait_ge(crow_s, n)
                    off = 0 if n == 1 else H
                    nc.tensor.matmul(p_c[:, :], crow[:, off:off + P], one[:, :], start=True, stop=True).then_inc(carry_ps, 1)

        exp_s, turned, got = (f.sem(s) for s in ("e_exp", "e_turned", "e_got"))
        with nc.Block() as block:
            @block.scalar
            def _(act):
                def body(b, u, turn):
                    if since(b, 2):
                        act.wait_ge(turned, b - 1)
                    nc.scalar.activation(back[:, u, :], a[:, bass.ds(b * P, P)], ACT.Exp).then_inc(exp_s, 1)

                run(act, TC, 2, body)

            @block.tensor
            def _(pe):
                def body(b, u, turn):
                    pe.wait_ge(exp_s, b + 1)
                    if since(b, 2):
                        pe.wait_ge(got, b - 1)
                    nc.tensor.transpose(p_e[:, u, 0:P], back[:, u, :], r.ident[:, :]).then_inc(turned, 1)

                run(pe, TC, 2, body)

            @block.vector
            def _(dve):
                def body(b, u, turn):
                    dve.wait_ge(turned, b + 1)
                    nc.vector.tensor_copy(by_block(ex, b), p_e[:, u, 0:P].rearrange("p (c h) -> p c h", h=H)).then_inc(got, 1)

                run(dve, TC, 2, body)


def edge_sums(nc, t, r, ph, ex, acc):
    CX = C + H
    with Phase(nc, "sum") as f:
        sring = f.sb("sring", [P, UE, GB], U32)
        hg = f.sb("hg", [P, UE, GB, C])
        x = f.sb("x", [P, 2, GB, CX])
        dc = f.sb("dc", [P, 2, GB])
        mm = f.sb("mm", [P, 2, GB, P])
        p_o = f.ps("p_o", [P, 2, 512])
        gat = f.sems("gat", UE)
        ring_s, turn_s, x_s, m_s, o_s, acc_s, link_s = (
            f.sem(s) for s in ("ring", "turn", "x", "m", "o", "acc", "link"))
        block = f.ctx.enter_context(nc.Block())

        @block.gpsimd
        def _(pool):
            def body(s, u, turn):
                g = pool.value_load(ph.g_int[0:1, bass.ds(s, 1)], min_val=0, max_val=T // GB - 1)
                if since(s, UE):
                    pool.wait_ge(x_s, s - UE + 1)
                nc.gpsimd.tensor_copy(sring[:, u, :], r.src[:, bass.ds(g * GB, GB)]).then_inc(ring_s, 1)
                pool.wait_ge(ring_s, s + 1)
                pool.sem_inc(turn_s, 1)
                for k in range(GB):
                    nc.gpsimd.indirect_dma_start(hg[:, u, k, :], None, t["d_h"][:, :],
                                                 bass.IndirectOffsetOnAxis(sring[:, u, k:k + 1], 0)).then_inc(gat[u], 16)

            run(pool, SB, UE, body)

        @block.vector
        def _(dve):
            nc.vector.memset(acc[:, :, :], 0.0).then_inc(acc_s, 1)

            def add(s, v):
                w = dve.value_load(ph.w_int[0:1, bass.ds(s, 1)], min_val=0, max_val=NW - 1)
                dve.wait_ge(o_s, s + 1)
                dve.wait_ge(acc_s, s + 1)
                sl = acc[:, bass.ds(w, 1), :].rearrange("p a c -> p (a c)")
                nc.vector.tensor_tensor(sl, sl, p_o[:, v, 0:CX], ALU.add).then_inc(acc_s, 1)

            def body(s, u, turn):
                v = u % 2
                link = Link(dve, link_s, s, 1)
                g = dve.value_load(ph.g_int[0:1, bass.ds(s, 1)], min_val=0, max_val=T // GB - 1)
                if since(s, 2):
                    dve.wait_ge(o_s, s - 1)
                link(nc.vector.tensor_scalar(dc[:, v, :], r.dst[:, bass.ds(g * GB, GB)], ph.w_node[:, bass.ds(s, 1)],
                                             None, ALU.subtract))
                nc.vector.tensor_tensor(mm[:, v, :, :], r.jrow[:, None, :].broadcast_to([P, GB, P]),
                                        dc[:, v, :, None].broadcast_to([P, GB, P]), ALU.is_equal).then_inc(m_s, 1)
                eg = ex[:, bass.ds(g * (GB * H), GB * H)].rearrange("p (k h) -> p k h", h=H)
                nc.vector.tensor_copy(x[:, v, :, C:CX], eg)
                dve.wait_ge(gat[u], turn * (16 * GB) + 16 * GB)
                for k in range(GB):
                    last = nc.vector.tensor_tensor(x[:, v, k, 0:C].rearrange("p (h d) -> p h d", h=H),
                                                   hg[:, u, k, :].rearrange("p (h d) -> p h d", h=H),
                                                   eg[:, k, :, None].broadcast_to([P, H, D]), ALU.mult)
                last.then_inc(x_s, 1)
                if since(s, 1):
                    add(s - 1, 1 - v)

            run(dve, SB, UE, body)
            add(SB - 1, (SB - 1) % 2)

        @block.tensor
        def _(pe):
            def body(s, u, turn):
                v = u % 2
                pe.wait_ge(m_s, s + 1)
                pe.wait_ge(x_s, s + 1)
                if since(s, 2):
                    pe.wait_ge(acc_s, s)
                for k in range(GB):
                    last = nc.tensor.matmul(p_o[:, v, 0:CX], mm[:, v, k, :], x[:, v, k, :],
                                            start=(k == 0), stop=(k == GB - 1))
                last.then_inc(o_s, 1)

            run(pe, SB, UE, body)
def node_update(nc, t, r, acc, spare):
    with Phase(nc, "upd") as f:
        part = 2 * BL * C
        x1 = spare[:, 0:part].rearrange("p (u b c) -> p u b c", u=2, c=C)
        xfT = spare[:, part:2 * part].rearrange("p (u k n) -> p u k n", u=2, k=KC)
        den = f.sb("den", [P, 2, BL, H])
        xf = f.sb("xf", [P, 2, BL, C])
        stats = Stats(nc, f, "x2")
        zero = f.sb("zero", [P, P])
        p_x = f.ps("p_x", [P, 2, 512])
        p_m = f.ps("p_m", [P, KC])
        x1_in, stored = f.sems("x1_in", 2), f.sems("stored", 2)
        x2_s, xf_s, xT_s, xTc_s, link_s, st_link, zero_s, mean_s, kept_s, hold_s = (
            f.sem(s) for s in ("x2", "xf", "xT", "xTc", "link", "st_link", "zero", "mean", "kept", "hold"))
        block = f.ctx.enter_context(nc.Block())

        @block.sync
        def _(sp):
            def load(i, u):
                sp.dma_start(x1[:, u, :, :], block_rows(t["d_x1"], i)).then_inc(x1_in[u], 16)

            def body(i, u, turn):
                if not isinstance(i, int) or i + 2 < NB:
                    sp.wait_ge(x2_s, i + 1)
                    load(i + 2, u)
                sp.wait_ge(xTc_s, i * BL + BL)
                sp.sem_inc(hold_s, 1)
                sp.dma_start(t["d_xfT"][:, :, bass.ds(i * (BL * P), BL * P)], xfT[:, u, :, :]).then_inc(stored[u], 16)

            load(0, 0)
            load(1, 1)
            run(sp, NB, 2, body, tail=2)
            for u in range(2):
                sp.wait_ge(x1_in[u], 16 * (NB // 2))
                sp.wait_ge(stored[u], 16 * (NB // 2))

        @block.vector
        def _(dve):
            nc.vector.memset(zero[:, :], 0.0).then_inc(zero_s, 1)

            def body(i, u, turn):
                link = Link(dve, link_s, i, 3)
                a = acc[:, bass.ds(i * BL, BL), :]
                link(nc.vector.tensor_scalar(den[:, u, :, :], a[:, :, C:C + H], 1e-10, None, ALU.max))
                link(nc.vector.reciprocal(den[:, u, :, :], den[:, u, :, :]))
                for b in range(BL):
                    ab = acc[:, bass.ds(i * BL + b, 1), 0:C].rearrange("p a (h d) -> p (a h) d", h=H)
                    last = nc.vector.tensor_tensor(ab, ab, den[:, u, b, :, None].broadcast_to([P, H, D]), ALU.mult)
                link(last)
                dve.wait_ge(x1_in[u], turn * 16 + 16)
                nc.vector.tensor_tensor(a[:, :, 0:C], a[:, :, 0:C], x1[:, u, :, :], ALU.add).then_inc(x2_s, 1)
                dve.wait_ge(x2_s, i + 1)
                dve.sem_inc(hold_s, 1)
                tile = lambda b: acc[:, bass.ds(i * BL + b, 1), 0:C].rearrange("p a c -> p (a c)")
                for b in range(BL):
                    last = stats.take(u, b, tile(b))
                stats.close(dve, Link(dve, st_link, i, 13), hold_s, u, last)
                nc.vector.tensor_copy(r.mu[:, bass.ds(i * BL, BL)], stats.mv[:, u, :, 0])
                nc.vector.tensor_copy(r.rs[:, bass.ds(i * BL, BL)], stats.rstd[:, u, :])
                if since(i, 2):
                    dve.wait_ge(xTc_s, i * BL - BL)
                for b in range(BL):
                    nc.vector.tensor_scalar(xf[:, u, b, :], tile(b), stats.mean(u, b), stats.scale(u, b),
                                            ALU.subtract, ALU.mult).then_inc(xf_s, 1)

            run(dve, NB, 2, body)
            dve.wait_ge(mean_s, 1)
            nc.vector.tensor_scalar(r.mean[:, :], p_m[:, :], 1.0 / N, None, ALU.mult).then_inc(zero_s, 1)

        @block.scalar
        def _(act):
            def body(i, u, turn):
                for b in range(BL):
                    act.wait_ge(xT_s, i * BL + b + 1)
                    if b == 0 and since(i, 2):
                        act.wait_ge(stored[u], turn * 16)
                    nc.scalar.copy(xfT[:, u, :, b * P:(b + 1) * P],
                                   p_x[:, (u * BL + b) % 2, 0:C].rearrange("p (k n) -> p k n", k=KC)).then_inc(xTc_s, 1)

            run(act, NB, 2, body)

        @block.tensor
        def _(pe):
            pe.wait_ge(zero_s, 1)
            nc.tensor.matmul(p_m[:, :], zero[:, :], r.ident[:, 0:KC], start=True, stop=False, skip_group_check=True)

            def body(i, u, turn):
                for b in range(BL):
                    m, w = i * BL + b, (u * BL + b) % 2
                    pe.wait_ge(xf_s, m + 1)
                    if since(m, 2):
                        pe.wait_ge(xTc_s, m - 1)
                    for c in range(KC):
                        nc.tensor.matmul(p_m[:, c:c + 1], xf[:, u, b, c * P:(c + 1) * P], r.valid[:, bass.ds(m, 1)],
                                         start=False, stop=False, skip_group_check=True)
                    for c in range(KC):
                        last = nc.tensor.transpose(p_x[:, w, c * P:(c + 1) * P], xf[:, u, b, c * P:(c + 1) * P],
                                                   r.ident[:, :])
                    last.then_inc(xT_s, 1)

            run(pe, NB, 2, body)
            nc.tensor.matmul(p_m[:, :], zero[:, :], r.ident[:, 0:KC], start=False, stop=True,
                             skip_group_check=True).then_inc(mean_s, 1)


def route(nc, t, r, q):
    with Phase(nc, "route") as f:
        wr = f.sb("wr", [P, KC, XP])
        row = lambda n, w=XP: f.sb(n, [1, w])
        br, io, lg, ex, rw, big, sc, eq, pick, r2 = (row(n) for n in ("br", "io", "lg", "ex", "rw", "big", "sc", "eq", "pick", "r2"))
        s1, idx, top, tw = row("s1", 2), row("idx", 2), row("top", 2), row("tw", 2)
        idx_i = f.sb("idx_i", [1, 2], I32)
        one = f.sb("one", [1, P])
        twb = f.sb("twb", [P, 2])
        b2e = f.sb("b2e", [P, 2, C])
        p_l = f.ps("p_l", [1, XP])
        p_w = f.ps("p_w", [P, 2])
        w_in, e_in, l_s, x_s, a_s, i_s, tw_s, pw_s, link_s = (
            f.sem(s) for s in ("w_in", "e_in", "l", "x", "a", "i", "tw", "pw", "link"))
        block = f.ctx.enter_context(nc.Block())

        @block.sync
        def _(sp):
            sp.dma_start(wr[:, :, :], t["wr"].rearrange("(k p) n -> p k n", p=P)).then_inc(w_in, 16)
            sp.dma_start(br[:, :], t["br"]).then_inc(w_in, 16)
            sp.dma_start(io[:, :], t["c_jrow"][0:1, 0:XP]).then_inc(w_in, 16)
            sp.wait_ge(i_s, 1)
            for k in range(2):
                e = sp.value_load(idx_i[0:1, k:k + 1], min_val=0, max_val=XP - 1)
                sp.dma_start(q.w1[:, k, :, :], t["ffn_w1"][bass.ds(e * C, C), :].rearrange("(k p) n -> p k n", p=P)).then_inc(e_in, 16)
                sp.dma_start(q.w2[:, k, :, :], t["ffn_w2"][bass.ds(e * FF, FF), :].rearrange("(k p) n -> p k n", p=P)).then_inc(e_in, 16)
                sp.dma_start(q.b1[:, k, :], t["ffn_b1"][bass.ds(e * P, P), :]).then_inc(e_in, 16)
                sp.dma_start(b2e[:, k, :], t["ffn_b2"][bass.ds(e, 1), :].broadcast_to([P, C])).then_inc(e_in, 16)
            sp.dma_start(q.g[:, :], t["ffn_g"].broadcast_to([P, C])).then_inc(e_in, 16)
            sp.dma_start(q.be[:, :], t["ffn_be"].broadcast_to([P, C])).then_inc(e_in, 16)
            sp.wait_ge(e_in, 10 * 16)

        @block.vector
        def _(dve):
            link = Link(dve, link_s)
            V = nc.vector
            exps = [0]

            def exp():
                exps[0] += 1
                dve.sem_inc(x_s, 1)
                dve.wait_ge(a_s, exps[0])

            def softmax(dst, n):
                link(V.tensor_reduce(s1[:, 0:1], lg[:, 0:n], AX.X, ALU.max))
                link(V.tensor_scalar(lg[:, 0:n], lg[:, 0:n], s1[:, 0:1], None, ALU.subtract))
                exp()
                link(V.tensor_reduce(s1[:, 1:2], ex[:, 0:n], AX.X, ALU.add))
                link(V.reciprocal(s1[:, 1:2], s1[:, 1:2]))
                link(V.tensor_scalar(dst, ex[:, 0:n], s1[:, 1:2], None, ALU.mult))

            link(V.memset(one[:, :], 1.0))
            link(V.memset(lg[:, :], 0.0))
            link(V.memset(ex[:, :], 0.0))
            dve.wait_ge(w_in, 48)
            dve.wait_ge(l_s, 1)
            link(V.tensor_tensor(lg[:, :], p_l[:, :], br[:, :], ALU.add))
            softmax(rw[:, :], XP)
            link(V.tensor_scalar(big[:, :], rw[:, :], float(TOPW), None, ALU.mult))
            link(V.reciprocal(sc[:, :], big[:, :]))
            link(V.tensor_scalar(big[:, :], big[:, :], CAPACITY, None, ALU.is_gt))
            link(V.scalar_tensor_tensor(sc[:, :], sc[:, :], CAPACITY, big[:, :], ALU.mult, ALU.mult))
            link(V.tensor_scalar(big[:, :], big[:, :], -1.0, 1.0, ALU.mult, ALU.add))
            link(V.tensor_tensor(sc[:, :], sc[:, :], big[:, :], ALU.add))
            link(V.tensor_tensor(lg[:, :], rw[:, :], sc[:, :], ALU.mult))
            softmax(rw[:, :], XP)
            for k in range(2):
                link(V.tensor_reduce(top[:, k:k + 1], rw[:, :], AX.X, ALU.max))
                link(V.tensor_scalar(eq[:, :], rw[:, :], top[:, k:k + 1], float(-XP), ALU.is_equal, ALU.mult))
                link(V.scalar_tensor_tensor(pick[:, :], eq[:, :], float(XP), io[:, :], ALU.add, ALU.add))
                link(V.tensor_reduce(idx[:, k:k + 1], pick[:, :], AX.X, ALU.min))
                link(V.tensor_scalar(eq[:, :], io[:, :], idx[:, k:k + 1], -4.0, ALU.is_equal, ALU.mult))
                link(V.tensor_tensor(rw[:, :], rw[:, :], eq[:, :], ALU.add))
            link(V.tensor_copy(idx_i[:, :], idx[:, :]))
            dve.sem_inc(i_s, 1)
            link(V.tensor_copy(lg[:, 0:2], top[:, :]))
            softmax(tw[:, :], 2)
            dve.sem_inc(tw_s, 1)
            dve.wait_ge(pw_s, 1)
            link(V.tensor_copy(twb[:, :], p_w[:, :]))
            dve.wait_ge(e_in, 10 * 16)
            for k in range(2):
                w = q.w2[:, k, :, :].rearrange("p k n -> p (k n)")
                link(V.tensor_scalar(w, w, twb[:, k:k + 1], None, ALU.mult))
                link(V.tensor_scalar(b2e[:, k, :], b2e[:, k, :], twb[:, k:k + 1], None, ALU.mult))
            link(V.tensor_tensor(q.b2[:, :], b2e[:, 0, :], b2e[:, 1, :], ALU.add))

        @block.scalar
        def _(act):
            for n in range(3):
                act.wait_ge(x_s, n + 1)
                nc.scalar.activation(ex[:, :], lg[:, :], ACT.Exp).then_inc(a_s, 1)

        @block.tensor
        def _(pe):
            pe.wait_ge(w_in, 48)
            for c in range(KC):
                last = nc.tensor.matmul(p_l[:, :], r.mean[:, c:c + 1], wr[:, c, :], start=(c == 0), stop=(c == KC - 1))
            last.then_inc(l_s, 1)
            pe.wait_ge(tw_s, 1)
            nc.tensor.matmul(p_w[:, :], one[:, :], tw[:, :], start=True, stop=True).then_inc(pw_s, 1)


def experts(nc, t, r, q, acc, spare):
    B = 2
    NF = NW // B
    FK = FF // P
    J = 2 * FK
    with Phase(nc, "ffn") as f:
        xT = f.sb("xT", [P, 2, KC, B * P])
        xf = f.sb("xf", [P, 2, B, C])
        hT = spare[:, 0:2 * J * B * P].rearrange("p (u j n) -> p u j n", u=2, j=J)
        o = f.sb("o", [P, 2, B, C])
        stats = Stats(nc, f, "y", B)
        p_f = f.ps("p_f", [P, 4, 512])
        p_y = f.ps("p_y", [P, 2, B, C])
        xT_in = f.sems("xT_in", 2)
        stored = f.sems("stored", 2)
        f_s, h_s, y_s, sum_s, norm_s, o_s, xf_s, xfb_s, st_link, norm_link, hold_s = (f.sem(s) for s in (
            "f", "h", "y", "sum", "norm", "o", "xf", "xfb", "st_link", "norm_link", "hold"))
        block = f.ctx.enter_context(nc.Block())
        x2_of = lambda n: acc[:, bass.ds(n, 1), 0:C].rearrange("p a c -> p (a c)")

        @block.sync
        def _(sp):
            def load(i, u):
                sp.dma_start(xT[:, u, :, :], t["d_xfT"][:, :, bass.ds(i * (B * P), B * P)]).then_inc(xT_in[u], 16)

            def store(i, u):
                sp.wait_ge(o_s, i + 1)
                sp.dma_start(t["out"][bass.ds(i * (B * P), B * P), :].rearrange("(b p) n -> p b n", p=P),
                             o[:, u, :, :]).then_inc(stored[u], 16)

            def body(i, u, turn):
                if since(i, 2):
                    sp.wait_ge(f_s, i * J - J)
                load(i, u)
                if since(i, 2):
                    store(i - 2, u)

            run(sp, NF, 2, body)
            for i in range(NF - 2, NF):
                store(i, i % 2)
            for u in range(2):
                n = (NF + 1 - u) // 2
                sp.wait_ge(xT_in[u], 16 * n)
                sp.wait_ge(stored[u], 16 * n)

        @block.tensor
        def _(pe):
            def down(i, u):
                if since(i, 2):
                    pe.wait_ge(sum_s, i * B - B)
                for b in range(B):
                    for j in range(J):
                        pe.wait_ge(h_s, i * J + j + 1) if b == 0 else None
                        last = nc.tensor.matmul(p_y[:, u, b, :], hT[:, u, j, b * P:(b + 1) * P],
                                                q.w2[:, j // FK, j % FK, :], start=(j == 0), stop=(j == J - 1))
                last.then_inc(y_s, 1)

            def body(i, u, turn):
                pe.wait_ge(xT_in[u], turn * 16 + 16)
                for j in range(J):
                    if j >= 4 or since(i, 1):
                        pe.wait_ge(h_s, i * J + j - 3)
                    for k in range(KC):
                        last = nc.tensor.matmul(p_f[:, j % 4, 0:B * P], q.w1[:, j // FK, k, (j % FK) * P:(j % FK + 1) * P],
                                                xT[:, u, k, :], start=(k == 0), stop=(k == KC - 1))
                    last.then_inc(f_s, 1)
                if since(i, 1):
                    down(i - 1, 1 - u)

            run(pe, NF, 2, body)
            down(NF - 1, (NF - 1) % 2)

        @block.gpsimd
        def _(pool):
            def add_b2(n, u, b):
                pool.wait_ge(xf_s, n + 1)
                nc.gpsimd.tensor_tensor(xf[:, u, b, :], xf[:, u, b, :], q.b2[:, :], ALU.add).then_inc(xfb_s, 1)

            def finish(i, u):
                for b in range(B):
                    pool.wait_ge(norm_s, i * B + b + 1)
                    last = nc.gpsimd.tensor_tensor(o[:, u, b, :], o[:, u, b, :], x2_of(i * B + b), ALU.add)
                last.then_inc(o_s, 1)

            def body(i, u, turn):
                for b in range(B):
                    add_b2(i * B + b, u, b)
                if since(i, 1):
                    finish(i - 1, 1 - u)

            run(pool, NF, 2, body)
            finish(NF - 1, (NF - 1) % 2)

        @block.scalar
        def _(act):
            def body(i, u, turn):
                if since(i, 2):
                    act.wait_ge(y_s, i - 1)
                for j in range(J):
                    act.wait_ge(f_s, i * J + j + 1)
                    nc.scalar.activation(hT[:, u, j, :], p_f[:, j % 4, 0:B * P], ACT.Gelu,
                                         bias=q.b1[:, j // FK, j % FK:j % FK + 1]).then_inc(h_s, 1)

            run(act, NF, 2, body)

        @block.vector
        def _(dve):
            def normal_x2(i, u):
                if since(i, 2):
                    dve.wait_ge(xfb_s, i * B)
                for b in range(B):
                    n = i * B + b
                    nc.vector.tensor_scalar(xf[:, u, b, :], x2_of(n), r.mu[:, bass.ds(n, 1)], r.rs[:, bass.ds(n, 1)],
                                            ALU.subtract, ALU.mult).then_inc(xf_s, 1)

            def finish(i, u, turn):
                dve.wait_ge(y_s, i + 1)
                dve.wait_ge(xfb_s, i * B + B)
                if since(i, 2):
                    dve.wait_ge(stored[u], turn * 16)
                for b in range(B):
                    last = nc.vector.tensor_tensor(o[:, u, b, :], p_y[:, u, b, :], xf[:, u, b, :], ALU.add)
                    last.then_inc(sum_s, 1)
                dve.wait_ge(sum_s, i * B + B)
                dve.sem_inc(hold_s, 1)
                for b in range(B):
                    last = stats.take(u, b, o[:, u, b, :])
                stats.close(dve, Link(dve, st_link, i, 13), hold_s, u, last)
                for b in range(B):
                    last = nc.vector.scalar_tensor_tensor(o[:, u, b, :], o[:, u, b, :], stats.mean(u, b), q.g[:, :],
                                                          ALU.subtract, ALU.mult)
                Link(dve, norm_link, i, 1)(last)
                for b in range(B):
                    nc.vector.scalar_tensor_tensor(o[:, u, b, :], o[:, u, b, :], stats.scale(u, b), q.be[:, :],
                                                   ALU.mult, ALU.add).then_inc(norm_s, 1)

            def body(i, u, turn):
                normal_x2(i, u)
                if since(i, 1):
                    finish(i - 1, 1 - u, turn - 1 if u == 0 else turn)

            run(dve, NF, 2, body)
            finish(NF - 1, (NF - 1) % 2, (NF - 1) // 2)


class Tensors:
    pass


def gps_layer(nc, t):
    with Phase(nc, "all") as f:
        r = Tensors()
        r.ident, r.jrow, r.jcol = f.sb("ident", [P, P]), f.sb("jrow", [P, P]), f.sb("jcol", [P, 1])
        r.headsel, r.valid = f.sb("headsel", [P, KC * H]), f.sb("valid", [P, NW])
        r.kvbd, r.mean = f.sb("kvbd", [P, KC, P + 4]), f.sb("mean", [P, KC])
        with Phase(nc, "lin") as g:
            r.wall = g.sb("wall", [P, KC, C + 2 * H])
            r.headmask = g.sb("headmask", [P, P])
            split_edge_features(nc, t)
            fold_attention_weights(nc, t, r)
            node_pass(nc, t, r)
        mixer(nc, t, r)
        with Phase(nc, "edge") as g:
            r.src = g.sb("src", [P, T], U32)
            r.dst = g.sb("dst", [P, T], I32)
            al = g.sb("al", [P, CE + 4])
            pb = Tensors()
            pb.g_int, pb.w_int = g.sb("gb", [P, SB], I32), g.sb("wb", [P, SB], I32)
            pb.w_node, pb.j_node = g.sb("wnb", [P, SB]), None
            make_steps(nc, t, r, pb, GB, SB, t["last_b"], t["c_gcol_b"])
            with Phase(nc, "weights") as k:
                pa = Tensors()
                pa.g_int, pa.w_int = k.sb("ga", [P, SA], I32), k.sb("wa", [P, SA], I32)
                pa.w_node, pa.j_node = k.sb("wna", [P, SA]), k.sb("jna", [P, SA])
                pa.al, pa.asrc = al, k.sb("asrc", [P, CE + 4])
                make_steps(nc, t, r, pa, GA, SA, t["last_a"], t["c_gcol_a"])
                load_indices(nc, t, r)
                edge_scores(nc, t, r, pa)
                edge_softmax(nc, t, r, pa)
            with Phase(nc, "acc") as k:
                acc = k.sb("acc", [P, NW, C + H])
                edge_sums(nc, t, r, pb, al, acc)
                r.mu, r.rs = k.sb("mu", [P, NW]), k.sb("rs", [P, NW])
                node_update(nc, t, r, acc, al)
                q = Tensors()
                q.w1 = al[:, 0:2 * KC * FF].rearrange("p (e k n) -> p e k n", e=2, k=KC)
                q.w2 = al[:, 2 * KC * FF:4 * KC * FF].rearrange("p (e k n) -> p e k n", e=2, n=C)
                q.b1, q.b2 = k.sb("b1", [P, 2, FF // P]), k.sb("b2", [P, C])
                q.g, q.be = k.sb("g", [P, C]), k.sb("be", [P, C])
                route(nc, t, r, q)
                experts(nc, t, r, q, acc, al[:, 4 * KC * FF:CE])


def split_edge_features(nc, t):
    A = P // EF
    L = EP // A
    with Phase(nc, "split") as f:
        x = f.sb("x", [P, L])
        hi = f.sb("hi", [P, L], F32R)
        lo = f.sb("lo", [P, L], F32R)
        w = f.sb("w", [EF, C])
        whi = f.sb("whi", [EF, C], F32R)
        wlo = f.sb("wlo", [EF, C], F32R)
        x_in, hi_s, lo_s, out_s = (f.sem(s) for s in ("x_in", "hi", "lo", "out"))
        block = f.ctx.enter_context(nc.Block())

        @block.sync
        def _(sp):
            sp.dma_start(w[:, :], t["ew"]).then_inc(x_in, 16)
            sp.dma_start(x[:, :], t["eaT"].rearrange("f (a l) -> (f a) l", a=A)).then_inc(x_in, 16)
            part = lambda n: t["d_ea"][n * EF:(n + 1) * EF, :].rearrange("f (a l) -> (f a) l", a=A)
            sp.wait_ge(hi_s, 2)
            sp.dma_start(part(0), hi[:, :].bitcast(F32)).then_inc(out_s, 16)
            sp.dma_start(part(2), hi[:, :].bitcast(F32)).then_inc(out_s, 16)
            sp.dma_start(t["d_ew"][0:EF, :], whi[:, :].bitcast(F32)).then_inc(out_s, 16)
            sp.dma_start(t["d_ew"][EF:2 * EF, :], whi[:, :].bitcast(F32)).then_inc(out_s, 16)
            sp.wait_ge(lo_s, 2)
            sp.dma_start(part(1), lo[:, :].bitcast(F32)).then_inc(out_s, 16)
            sp.dma_start(t["d_ew"][2 * EF:3 * EF, :], wlo[:, :].bitcast(F32)).then_inc(out_s, 16)
            sp.wait_ge(out_s, 6 * 16)

        @block.scalar
        def _(act):
            act.wait_ge(x_in, 32)
            nc.scalar.copy(whi[:, :], w[:, :]).then_inc(hi_s, 1)
            nc.scalar.copy(hi[:, :], x[:, :]).then_inc(hi_s, 1)

        @block.vector
        def _(dve):
            dve.wait_ge(hi_s, 2)
            nc.vector.tensor_tensor(wlo[:, :], w[:, :], whi[:, :].bitcast(F32), ALU.subtract).then_inc(lo_s, 1)
            nc.vector.tensor_tensor(lo[:, :], x[:, :], hi[:, :].bitcast(F32), ALU.subtract).then_inc(lo_s, 1)


def load_indices(nc, t, r):
    with Phase(nc, "idx") as f:
        loaded = f.sem("loaded")
        block = f.ctx.enter_context(nc.Block())

        @block.sync
        def _(sp):
            sp.dma_start(r.src[:, :], t["src_col"]).then_inc(loaded, 16)
            sp.dma_start(r.dst[:, :], t["dst_col"]).then_inc(loaded, 16)
            sp.wait_ge(loaded, 32)


def kernel(**inputs):
    import numpy as np
    import concourse.bacc as bacc
    from concourse.bass_utils import run_bass_kernel_spmd as launch

    a = {k: np.asarray(v) for k, v in inputs.items()}
    row = lambda v: np.ascontiguousarray(v.reshape(1, -1))
    turn = lambda v: np.ascontiguousarray(v.T)
    src = np.pad(a["src"], (0, EP - E))
    dst = np.pad(a["dst"], (0, EP - E), constant_values=NP - 1)
    head = np.arange(C) // D
    groups = lambda tiles: dst.reshape(NW, T // tiles // NW, tiles * P)[:, :, -1]
    p = np.arange(P)
    arrays = {
        "x": np.pad(a["x"], ((0, NP + 2 * BL * P - N), (0, 0))),
        "src_col": turn(src.reshape(T, P)),
        "dst_col": turn(dst.reshape(T, P)),
        "dst_row": row(dst),
        "dst_ext": np.pad(row(dst), ((0, 0), (1, 1)), constant_values=-1),
        "last_a": np.ascontiguousarray(groups(GA)),
        "last_b": np.ascontiguousarray(groups(GB)),
        "eaT": np.concatenate([turn(np.pad(a["edge_attr_3"], ((0, EP - E), (0, 0)))), np.ones((1, EP), np.float32)]),
        "ew": np.concatenate([turn(a["L0_gnn_edge_W"]), row(a["L0_gnn_edge_b"])]),
        "w": a["L0_gnn_W"], "wT": turn(a["L0_gnn_W"]),
        "a_col": np.stack([a["L0_gnn_a_dst"].reshape(-1), a["L0_gnn_a_src"].reshape(-1)], 1),
        "bias": row(a["L0_gnn_bias"]),
        "wqkvT": turn(a["L0_mix_Wqkv"]), "w1T": turn(a["L0_mix_W1"]), "w2T": turn(a["L0_mix_W2"]),
        "b1_col": turn(a["L0_mix_b1"].reshape(KC, P)),
        "g1": row(a["L0_mix_ln1_g"]), "be1": row(a["L0_mix_ln1_b"]),
        "g2": row(a["L0_mix_ln2_g"]), "be2": row(a["L0_mix_ln2_b"]), "b2": row(a["L0_mix_b2"]),
        "wr": a["L0_ffn_Wr"], "br": row(a["L0_ffn_br"]),
        "ffn_w1": a["L0_ffn_W1"].reshape(XP * C, FF), "ffn_w2": a["L0_ffn_W2"].reshape(XP * FF, C),
        "ffn_b1": np.ascontiguousarray(a["L0_ffn_b1"].reshape(XP, FF // P, P).transpose(0, 2, 1)).reshape(XP * P, FF // P),
        "ffn_b2": a["L0_ffn_b2"], "ffn_g": row(a["L0_ffn_gamma"]), "ffn_be": row(a["L0_ffn_beta"]),
        "c_ident": np.eye(P, dtype=np.float32),
        "c_jrow": np.tile(p.astype(np.float32), (P, 1)),
        "c_jcol": p.astype(np.float32)[:, None],
        "c_headsel": (head.reshape(KC, P).T[:, :, None] == np.arange(H)).astype(np.float32).reshape(P, KC * H),
        "c_headmask": (p[:, None] // D == p[None, :] // D).astype(np.float32),
        "c_valid": (p[:, None] + P * np.arange(NW)[None, :] < N).astype(np.float32),
        "c_sidx": np.tile(np.arange(SB, dtype=np.float32), (P, 1)),
    }
    for n, tiles in (("a", GA), ("b", GB)):
        k = T // tiles // NW
        arrays[f"c_gcol_{n}"] = 1.0 + np.arange(NW * k, dtype=np.float32).reshape(NW, k)
    scratch = {"d_xn": [NP, C], "d_h": [NP, C], "d_as": [NP, H], "d_q": [P, NW * C], "d_x1": [NP, C],
               "d_xfT": [P, KC, NP]}

    in_parts = {"d_hw": [NP, 2 * (C + H)], "d_ea": [3 * EF, EP], "d_ew": [3 * EF, C]}

    nc = bacc.Bacc("TRN2", target_bir_lowering=False, num_devices=1)
    feed, aps = {}, {}
    for name, v in arrays.items():
        v = np.ascontiguousarray(v)
        feed[f"in_{name}"] = v
        aps[name] = nc.dram_tensor(f"in_{name}", v.shape, mybir.dt.from_np(v.dtype), kind="ExternalInput").ap()
    for name, shape in scratch.items():
        aps[name] = nc.dram_tensor(name, shape, F32).ap()
    for name, shape in in_parts.items():
        aps[name] = nc.dram_tensor(name, shape, F32).ap()
    aps["out"] = nc.dram_tensor("out", [NP, C], F32, kind="ExternalOutput").ap()
    aps["src_col"] = aps["src_col"].bitcast(U32)
    gps_layer(nc, aps)
    return launch(nc, [feed], core_ids=[0]).results[0]["out"][:N]
```

```python
import concourse.bass as bass
from concourse import mybir
from contextlib import ExitStack

F32 = mybir.dt.float32
I32 = mybir.dt.int32
U32 = mybir.dt.uint32
F32R = mybir.dt.float32r
ALU = mybir.AluOpType
ACT = mybir.ActivationFunctionType
AX = mybir.AxisListType

P = 128
N = 12500
C = 256
H = 8
D = C // H
KC = C // P
NW = -(-N // P)
NP = NW * P
E = 200000
EF = 4
CH = 16
TC = -(-E // (P * CH))
T = TC * CH
EP = T * P
CE = TC * P
GT = 4
GP = 16
R = 4
LAG = 2
BIG = 1.0e30
XP = 8
FF = 512
TOPW = N
CAPACITY = float(-(-N * 5 // (4 * XP)))
LN_EPS = 1e-5
UE = 4
BL = 7
NB = NW // BL
STEPS = -(-(T // GT + NW - 1) // UE) * UE


def run(eng, count, unroll, body, tail=0, times=1):
    wide = unroll * times
    for s in range(wide):
        body(s, s % unroll, s // unroll)
    turns = (count - wide - tail) // wide
    with eng.Fori(0, turns) as it:
        for k in range(wide):
            body(it * wide + (wide + k), k % unroll, it * times + (times + k // unroll))
    for s in range((turns + 1) * wide, count):
        body(s, s % unroll, s // unroll)


def since(s, n):
    return not isinstance(s, int) or s >= n


class Link:

    def __init__(self, eng, sem, s=0, each=0):
        self.eng, self.sem, self.base, self.each, self.n = eng, sem, s * each, each, 0

    def __call__(self, ins):
        ins.then_inc(self.sem, 1)
        self.n += 1
        assert not self.each or self.n <= self.each, (self.n, self.each)
        self.eng.wait_ge(self.sem, self.base + self.n)


class Phase:

    def __init__(self, nc, name):
        self.nc, self.name, self.ctx = nc, name, ExitStack()

    def __enter__(self):
        self.ctx.__enter__()
        return self

    def __exit__(self, *a):
        return self.ctx.__exit__(*a)

    def sb(self, name, shape, dt=F32):
        return self.ctx.enter_context(self.nc.sbuf_tensor(f"{self.name}_{name}", shape, dt))

    def ps(self, name, shape, dt=F32):
        return self.ctx.enter_context(self.nc.psum_tensor(f"{self.name}_{name}", shape, dt))

    def sem(self, name):
        return self.ctx.enter_context(self.nc.semaphore(f"{self.name}_{name}"))

    def sems(self, name, n):
        return [self.sem(f"{name}{k}") for k in range(n)]


def rows(dram, i, n=P):
    return dram[bass.ds(i * n, n), :]


def fold_attention_weights(nc, t, r):
    with Phase(nc, "fold") as f:
        w_nat = f.sb("w_nat", [P, KC, C])
        a_col = f.sb("a_col", [P, KC, 2])
        a_diag = f.sb("a_diag", [P, KC, 2, H])
        wa = f.ps("wa", [P, KC, 2 * H])
        loaded, diag_ready, wa_ready, done = (f.sem(s) for s in ("loaded", "diag", "wa", "done"))
        block = f.ctx.enter_context(nc.Block())

        @block.sync
        def _(sp):
            sp.dma_start(r.ident[:, :], t["c_ident"]).then_inc(loaded, 16)
            sp.dma_start(r.jrow[:, :], t["c_jrow"]).then_inc(loaded, 16)
            sp.dma_start(r.jcol[:, :], t["c_jcol"]).then_inc(loaded, 16)
            sp.dma_start(r.headsel[:, :], t["c_headsel"]).then_inc(loaded, 16)
            sp.dma_start(r.valid[:, :], t["c_valid"]).then_inc(loaded, 16)
            sp.dma_start(r.wall[:, :, 0:C], t["wT"].rearrange("(k p) n -> p k n", p=P)).then_inc(loaded, 16)
            sp.dma_start(w_nat[:, :, :], t["w"].rearrange("(k p) n -> p k n", p=P)).then_inc(loaded, 16)
            sp.dma_start(a_col[:, :, :], t["a_col"].rearrange("(k p) n -> p k n", p=P)).then_inc(loaded, 16)
            sp.wait_ge(loaded, 8 * 16)

        @block.vector
        def _(dve):
            dve.wait_ge(loaded, 8 * 16)
            for k in range(KC):
                for side in range(2):
                    nc.vector.tensor_scalar(a_diag[:, k, side, :], r.headsel[:, k * H:(k + 1) * H],
                                            a_col[:, k, side:side + 1], None, ALU.mult).then_inc(diag_ready, 1)
            dve.wait_ge(wa_ready, 1)
            nc.vector.tensor_copy(r.wall[:, :, C:C + 2 * H], wa[:, :, :]).then_inc(done, 1)

        @block.tensor
        def _(pe):
            pe.wait_ge(diag_ready, 4)
            for k in range(KC):
                for j in range(KC):
                    last = nc.tensor.matmul(wa[:, k, :], w_nat[:, j, k * P:(k + 1) * P], a_diag[:, j, :, :],
                                            start=(j == 0), stop=(j == KC - 1))
            last.then_inc(wa_ready, 1)


def make_steps(nc, t, r, ph, tiles=GT, count=STEPS):
    groups = T // tiles
    chunks = groups // NW
    half = count // 2
    with Phase(nc, "steps") as f:
        raw = f.sb("raw", [NW, chunks], I32)
        win = f.sb("win", [NW, chunks], I32)
        winf = f.sb("winf", [NW, chunks])
        gcol = f.sb("gcol", [NW, chunks])
        start = f.sb("start", [NW, chunks])
        start_int = f.sb("start_int", [NW, chunks], I32)
        sidx = f.sb("sidx", [P, count])
        begun = f.sb("begun", [NW, chunks, count])
        ones = f.sb("ones", [NW, P])
        gs = f.sb("gs", [P, count])
        ws = f.sb("ws", [P, count])
        wc = f.sb("wc", [P, count])
        acc = f.ps("acc", [P, 2, 512])
        loaded, link_s, begun_s, acc_s, starts_s, laid = (
            f.sem(s) for s in ("loaded", "link", "begun", "acc", "starts", "laid"))
        block = f.ctx.enter_context(nc.Block())

        @block.sync
        def _(sp):
            sp.dma_start(raw[:, :], t["last"]).then_inc(loaded, 16)
            sp.dma_start(sidx[:, :], t["c_sidx"]).then_inc(loaded, 16)
            sp.dma_start(gcol[:, :], t["c_gcol"]).then_inc(loaded, 16)
            sp.wait_ge(loaded, 48)
            sp.wait_ge(starts_s, 1)
            sp.dma_start(t["d_start"].rearrange("(w c) -> w c", c=chunks), start_int[:, :]).then_inc(laid, 16)
            sp.wait_ge(laid, 16)
            sp.dma_start(ph.start[:, :], t["d_start"][None, :]).then_inc(laid, 16)
            sp.wait_ge(laid, 32)

        @block.vector
        def _(dve):
            link = Link(dve, link_s)
            dve.wait_ge(loaded, 48)
            link(nc.vector.memset(ones[:, :], 1.0))
            link(nc.vector.tensor_scalar(win[:, :], raw[:, :], 7, None, ALU.arith_shift_right))
            link(nc.vector.tensor_copy(winf[:, :], win[:, :]))
            link(nc.vector.tensor_tensor(start[:, :], winf[:, :], gcol[:, :], ALU.add))
            for c in range(chunks):
                nc.vector.tensor_scalar(begun[:, c, :], sidx[0:NW, :], start[:, c:c + 1], None,
                                        ALU.is_ge).then_inc(begun_s, 1)
            dve.wait_ge(acc_s, 1)
            for a in range(2):
                link(nc.vector.tensor_scalar(gs[:, a * half:(a + 1) * half], acc[:, a, 0:half],
                                             float(groups - 1), None, ALU.min))
            link(nc.vector.tensor_tensor(ws[:, :], sidx[:, :], gs[:, :], ALU.subtract))
            link(nc.vector.tensor_scalar(wc[:, :], ws[:, :], float(NW - 1), None, ALU.min))
            link(nc.vector.tensor_copy(ph.g_int[:, :], gs[:, :]))
            link(nc.vector.tensor_copy(ph.w_int[:, :], wc[:, :]))
            link(nc.vector.tensor_scalar(ph.w_node[:, :], ws[:, :], float(P), None, ALU.mult))
            link(nc.vector.tensor_copy(start_int[:, :], start[:, :]))
            dve.sem_inc(starts_s, 1)
            link(nc.vector.tensor_scalar(ph.j_node[:, :], ph.w_node[:, :], r.jcol[:, 0:1], None, ALU.add))

        @block.tensor
        def _(pe):
            pe.wait_ge(begun_s, chunks)
            for a in range(2):
                for c in range(chunks):
                    last = nc.tensor.matmul(acc[:, a, 0:half], ones[:, :], begun[:, c, a * half:(a + 1) * half],
                                            start=(c == 0), stop=(c == chunks - 1))
            last.then_inc(acc_s, 1)


def rstd_of(nc, link, var, v, a, y):
    link(nc.vector.tensor_scalar(v, var, LN_EPS, None, ALU.add))
    link(nc.vector.tensor_scalar(y.bitcast(I32), v.bitcast(I32), -0.5, float(0x5F3759DF), ALU.mult, ALU.add))
    for _ in range(3):
        link(nc.vector.tensor_tensor(a, y, y, ALU.mult))
        link(nc.vector.scalar_tensor_tensor(a, a, -0.5, v, ALU.mult, ALU.mult))
        link(nc.vector.scalar_tensor_tensor(y, a, 1.5, y, ALU.add, ALU.mult))


class Stats:

    def __init__(self, nc, f, name, n=BL):
        self.nc, self.n = nc, n
        self.st = f.sb(name + "_st", [P, 2, n, 6])
        self.mv = f.sb(name + "_mv", [P, 2, n, 2])
        self.tmp = f.sb(name + "_tmp", [P, 2, 2, n])
        self.rstd = f.sb(name + "_rstd", [P, 2, n])

    def take(self, u, b, src):
        return self.nc.vector.bn_stats(self.st[:, u, b, :], src)

    def close(self, dve, link, hold, u, last):
        link(last)
        dve.sem_inc(hold, 1)
        for b in range(self.n):
            last = self.nc.vector.bn_aggr(self.mv[:, u, b, :], self.st[:, u, b, :])
        link(last)
        rstd_of(self.nc, link, self.mv[:, u, :, 1], self.tmp[:, u, 0, :], self.tmp[:, u, 1, :], self.rstd[:, u, :])

    def hand_over(self, dve, link, hold, u, last, var_s):
        link(last)
        dve.sem_inc(hold, 1)
        for b in range(self.n):
            last = self.nc.vector.bn_aggr(self.mv[:, u, b, :], self.st[:, u, b, :])
        last.then_inc(var_s, 1)

    def pool_close(self, link, u, power, rstd_s):
        v = self.tmp[:, u, 0, :]
        link(self.nc.gpsimd.tensor_tensor(v, self.mv[:, u, :, 1], power[:, 1, :], ALU.add))
        self.nc.gpsimd.tensor_tensor(self.rstd[:, u, :], v, power[:, 0, :], ALU.pow).then_inc(rstd_s, 1)

    def mean(self, u, b):
        return self.mv[:, u, b, 0:1]

    def scale(self, u, b):
        return self.rstd[:, u, b:b + 1]


def block_rows(dram, i):
    return dram[bass.ds(i * (BL * P), BL * P), :].rearrange("(b p) n -> p b n", p=P)


def node_pass(nc, t, r):
    with Phase(nc, "node") as f:
        wqkv = f.sb("wqkv", [P, KC, 3 * C])
        x = f.sb("x", [P, 2, BL, C])
        xn = f.sb("xn", [P, 2, BL, C])
        h = f.sb("h", [P, 2, BL, C + 2 * H])
        hsp = f.sb("hsp", [P, 2, BL, 2, C + H], F32R)
        q = f.sb("q", [P, 2, BL, C])
        xnT = f.sb("xnT", [P, 2, KC * P])
        neg = f.sb("neg", [P, 2, 2, C])
        ex = f.sb("ex", [P, 2, 2, C])
        k = f.sb("k", [P, 2, C])
        v = f.sb("v", [P, 2, KC, P + 1])
        xb = f.sb("xb", [P, 2, BL, C])
        off = f.sb("off", [P, 2, C])
        zero = f.sb("zero", [P, P])
        stats = Stats(nc, f, "x")
        p_t = f.ps("p_t", [P, 2, C])
        p_q = f.ps("p_q", [P, 2, 512])
        p_h = f.ps("p_h", [P, 2, 512])
        p_kv = f.ps("p_kv", [P, 2, 2, C])
        p_sum = f.ps("p_sum", [P, KC, P + 1])
        x_in = f.sems("x_in", 2)
        stored = f.sems("stored", 2)
        (w_in, xn_s, xT_s, xTc_s, mm_s, h_s, h_hi_s, h_lo_s, neg_s, exp_s, k_s, v_s, kv_used, link_s, zero_s,
         sum_s) = (f.sem(s) for s in (
             "w_in", "xn", "xT", "xTc", "mm", "h", "h_hi", "h_lo", "neg", "exp", "k", "v", "kv_used",
             "link", "zero", "sum"))
        off_in, off_s, xb_s, var_s, rstd_s, pool_link = (
            f.sem(s) for s in ("off_in", "off", "xb", "var", "rstd", "pool_link"))
        block = f.ctx.enter_context(nc.Block())

        @block.sync
        def _(sp):
            sp.dma_start(off[:, 0, :], t["be2"].broadcast_to([P, C])).then_inc(off_in, 16)
            sp.dma_start(off[:, 1, :], t["bias"].broadcast_to([P, C])).then_inc(off_in, 16)
            for u in range(2):
                sp.dma_start(x[:, u, :, :], block_rows(t["x"], u)).then_inc(x_in[u], 16)
            sp.dma_start(wqkv[:, :, :], t["wqkvT"].rearrange("(k p) n -> p k n", p=P)).then_inc(w_in, 16)
            sp.dma_start(r.headmask[:, :], t["c_headmask"]).then_inc(w_in, 16)

            def body(i, u, turn):
                sp.wait_ge(xb_s, i * BL + BL)
                sp.wait_ge(xn_s, i * BL + BL)
                sp.dma_start(x[:, u, :, :], block_rows(t["x"], i + 2)).then_inc(x_in[u], 16)
                sp.dma_start(block_rows(t["d_xn"], i), xn[:, u, :, :]).then_inc(stored[u], 16)
                sp.dma_start(block_rows(t["d_xb"], i), xb[:, u, :, :]).then_inc(stored[u], 16)
                sp.wait_ge(k_s, i * BL + BL)
                sp.dma_start(block_rows(t["d_hw"], i),
                             hsp[:, u, :, :, :].rearrange("p b a c -> p b (a c)").bitcast(F32)).then_inc(stored[u], 16)
                sp.dma_start(block_rows(t["d_h"], i), h[:, u, :, 0:C]).then_inc(stored[u], 16)
                sp.dma_start(block_rows(t["d_as"], i), h[:, u, :, C + H:C + 2 * H]).then_inc(stored[u], 16)
                sp.dma_start(t["d_q"][:, bass.ds(i * (BL * C), BL * C)],
                             q[:, u, :, :].rearrange("p b c -> p (b c)")).then_inc(stored[u], 16)

            run(sp, NB, 2, body)
            for u in range(2):
                sp.wait_ge(x_in[u], 16 * (NB // 2 + 1))
                sp.wait_ge(stored[u], 96 * (NB // 2))

        @block.vector
        def _(dve):
            nc.vector.memset(zero[:, :], 0.0).then_inc(zero_s, 1)

            def normal(m, u, b, blocks=None):
                if blocks is not None:
                    dve.wait_ge(rstd_s, blocks)
                nc.vector.tensor_scalar(xn[:, u, b, :], x[:, u, b, :], stats.mean(u, b), stats.scale(u, b),
                                        ALU.subtract, ALU.mult).then_inc(xn_s, 1)

            def statistics(i, u, turn, link):
                dve.wait_ge(x_in[u], turn * 16 + 16)
                for b in range(BL):
                    last = stats.take(u, b, x[:, u, b, :])
                stats.hand_over(dve, link, r.hold, u, last, var_s)

            def leave(m, w, u, b):
                dve.wait_ge(mm_s, m + 1)
                nc.vector.tensor_scalar(neg[:, w, 0, :], p_kv[:, w, 0, :], 0.0, None, ALU.min)
                nc.vector.tensor_scalar(neg[:, w, 1, :], p_q[:, w, 0:C], 0.0, None, ALU.min).then_inc(neg_s, 1)
                nc.vector.tensor_copy(h[:, u, b, :], p_h[:, w, 0:C + 2 * H]).then_inc(h_s, 1)
                if since(m, 2):
                    dve.wait_ge(kv_used, m - 1)
                nc.vector.tensor_copy(v[:, w, :, P], r.valid[:, bass.ds(m, 1)].broadcast_to([P, KC]))
                dve.wait_ge(exp_s, m + 1)
                nc.vector.scalar_tensor_tensor(q[:, u, b, :], p_q[:, w, 0:C], 0.0, ex[:, w, 1, :],
                                               ALU.max, ALU.add)
                dve.wait_ge(h_hi_s, m + 1)
                nc.vector.tensor_tensor(hsp[:, u, b, 1, :], h[:, u, b, 0:C + H], hsp[:, u, b, 0, :].bitcast(F32),
                                        ALU.subtract).then_inc(h_lo_s, 1)
                nc.vector.scalar_tensor_tensor(k[:, w, :], p_kv[:, w, 0, :], 0.0, ex[:, w, 0, :],
                                               ALU.max, ALU.add).then_inc(k_s, 1)

            def body(i, u, turn):
                more = not isinstance(i, int) or i < NB - 1
                for b in range(BL):
                    m = i * BL + b
                    if b < BL - 2:
                        normal(m + 2, u, b + 2)
                    elif more:
                        if since(i, 1) and b == BL - 2:
                            dve.wait_ge(stored[1 - u], (turn + u) * 96)
                        normal(m + 2, 1 - u, b + 2 - BL, i + 2 if b == BL - 2 else None)
                    leave(m, (u * BL + b) % 2, u, b)
                    if b == 2 and more:
                        statistics(i + 1, 1 - u, turn + u, Link(dve, link_s, i + 1, 1))

            statistics(0, 0, 0, Link(dve, link_s, 0, 1))
            normal(0, 0, 0, 1)
            normal(1, 0, 1)
            run(dve, NB, 2, body, tail=1)
            dve.wait_ge(sum_s, 1)
            for c in range(KC):
                nc.vector.tensor_tensor(r.kvbd[:, c, 0:P], p_sum[:, c, 0:P], r.headmask[:, :], ALU.mult).then_inc(link_s, 1)
                nc.vector.tensor_scalar(r.kvbd[:, c, P:P + 4], r.headsel[:, 0:4], p_sum[:, c, P:P + 1], None,
                                        ALU.mult).then_inc(link_s, 1)

        @block.gpsimd
        def _(pool):
            pool.wait_ge(off_in, 32)
            nc.gpsimd.tensor_tensor(off[:, 0, :], off[:, 0, :], off[:, 1, :], ALU.add).then_inc(off_s, 1)
            nc.gpsimd.memset(r.power[:, 0, :], -0.5).then_inc(off_s, 1)
            nc.gpsimd.memset(r.power[:, 1, :], LN_EPS).then_inc(off_s, 1)
            pool.wait_ge(off_s, 3)

            def body(i, u, turn):
                pool.wait_ge(var_s, i + 1)
                stats.pool_close(Link(pool, pool_link, i, 1), u, r.power, rstd_s)
                pool.wait_ge(x_in[u], turn * 16 + 16)
                if since(i, 2):
                    pool.wait_ge(stored[u], turn * 96)
                pool.sem_inc(r.pool_hold, 1)
                for b in range(BL):
                    nc.gpsimd.tensor_tensor(xb[:, u, b, :], x[:, u, b, :], off[:, 0, :], ALU.add).then_inc(xb_s, 1)

            run(pool, NB, 2, body)

        @block.scalar
        def _(act):
            def turned(m, w):
                act.wait_ge(xT_s, m + 1)
                nc.scalar.copy(xnT[:, w, :], p_t[:, w, :]).then_inc(xTc_s, 1)

            def body(i, u, turn):
                for b in range(BL):
                    m, w = i * BL + b, (u * BL + b) % 2
                    if not isinstance(i, int) or m + 1 < NW:
                        turned(m + 1, 1 - w)
                    act.wait_ge(neg_s, m + 1)
                    if since(m, 2):
                        act.wait_ge(kv_used, m - 1)
                    nc.scalar.copy(v[:, w, :, 0:P], p_kv[:, w, 1, :].rearrange("p (c n) -> p c n", c=KC)).then_inc(v_s, 1)
                    act.wait_ge(v_s, m + 1)
                    nc.scalar.activation(ex[:, w, :, :], neg[:, w, :, :], ACT.Exp).then_inc(exp_s, 1)
                    act.wait_ge(h_s, m + 1)
                    if since(i, 2) and b == 0:
                        act.wait_ge(stored[u], turn * 96)
                    nc.scalar.copy(hsp[:, u, b, 0, :], h[:, u, b, 0:C + H]).then_inc(h_hi_s, 1)

            turned(0, 0)
            run(act, NB, 2, body, tail=1)

        @block.tensor
        def _(pe):
            pe.wait_ge(w_in, 32)
            pe.wait_ge(zero_s, 1)
            for c in range(KC):
                nc.tensor.matmul(p_sum[:, c, :], zero[:, :], wqkv[:, 0, 0:P + 1], start=(c == 0), stop=False,
                                 skip_group_check=True)

            def turn_tile(m, w, u, b):
                pe.wait_ge(xn_s, m + 1)
                if since(m, 1):
                    pe.wait_ge(xTc_s, m)
                for c in range(KC):
                    last = nc.tensor.transpose(p_t[:, w, c * P:(c + 1) * P], xn[:, u, b, c * P:(c + 1) * P],
                                               r.ident[:, :])
                last.then_inc(xT_s, 1)

            def products(m, w):
                pe.wait_ge(xTc_s, m + 1)
                if since(m, 2):
                    pe.wait_ge(h_lo_s, m - 1)
                    pe.wait_ge(k_s, m - 1)
                for c in range(KC):
                    nc.tensor.matmul(p_h[:, w, 0:C + 2 * H], xnT[:, w, c * P:(c + 1) * P], r.wall[:, c, :],
                                     start=(c == 0), stop=(c == KC - 1))
                for c in range(KC):
                    nc.tensor.matmul(p_kv[:, w, :, :], xnT[:, w, c * P:(c + 1) * P], wqkv[:, c, C:3 * C],
                                     start=(c == 0), stop=(c == KC - 1))
                for o in range(KC):
                    for c in range(KC):
                        last = nc.tensor.matmul(p_q[:, w, o * P:(o + 1) * P], wqkv[:, c, o * P:(o + 1) * P],
                                                xnT[:, w, c * P:(c + 1) * P], start=(c == 0), stop=(c == KC - 1))
                last.then_inc(mm_s, 1)

            def sums(m, w):
                pe.wait_ge(k_s, m + 1)
                pe.wait_ge(v_s, m + 1)
                for c in range(KC):
                    last = nc.tensor.matmul(p_sum[:, c, :], k[:, w, c * P:(c + 1) * P], v[:, w, c, :],
                                            start=False, stop=False, skip_group_check=True)
                last.then_inc(kv_used, 1)

            def body(i, u, turn):
                for b in range(BL):
                    m, w = i * BL + b, (u * BL + b) % 2
                    if b < BL - 1:
                        turn_tile(m + 1, 1 - w, u, b + 1)
                    elif not isinstance(i, int) or i < NB - 1:
                        turn_tile(m + 1, 1 - w, 1 - u, 0)
                    products(m, w)
                    if since(m, 1):
                        sums(m - 1, 1 - w)

            turn_tile(0, 0, 0, 0)
            run(pe, NB, 2, body, tail=1)
            sums(NW - 1, (NW - 1) % 2)
            for c in range(KC):
                last = nc.tensor.matmul(p_sum[:, c, :], zero[:, :], wqkv[:, 0, 0:P + 1], start=False, stop=True,
                                        skip_group_check=True)
            last.then_inc(sum_s, 1)


def mixer(nc, t, r):
    HC = H // KC
    AHEAD = BL + 4
    LATE = {b: [] for b in range(BL)}
    for j in range(BL):
        LATE[2 + j * (BL - 2) // BL].append(j)
    with Phase(nc, "mix") as f:
        w1 = f.sb("w1", [P, KC, C])
        w2 = f.sb("w2", [P, KC, C])
        b1 = f.sb("b1", [P, KC])
        vec = f.sb("vec", [P, 4, C])
        col = f.sb("col", [P, 2, KC])
        one = f.sb("one", [1, P])
        q = f.sb("q", [P, 2, BL, C])
        xn = f.sb("xn", [P, 2, BL, C])
        x = f.sb("x", [P, 2, BL, C])
        z = f.sb("z", [P, 2, KC, HC])
        y = f.sb("y", [P, 2, BL, C])
        x1 = f.sb("x1", [P, 2, BL, C])
        gn = f.sb("gn", [P, 2, BL, C])
        o = f.sb("o", [P, 2, BL, C])
        x1T = f.sb("x1T", [P, 2, C])
        hT = f.sb("hT", [P, 2, KC, P])
        stats1, stats2 = Stats(nc, f, "one"), Stats(nc, f, "two")
        p_t = f.ps("p_t", [P, 2, 512])
        p_x = f.ps("p_x", [P, 2, 512])
        p_h = f.ps("p_h", [P, 2, 512])
        p_y = f.ps("p_y", [P, 2, 512])
        qxn_in, x_in, stored = f.sems("qxn_in", 2), f.sems("x_in", 2), f.sems("stored", 2)
        (w_in, t_s, a_s, yx_s, x1_s, xT_s, xTc_s, h_s, hT_s, y_s, o_s, gn_s, sum2_s, norm2_s, a_link, st1_link,
         st2_link, var1_s, rstd1_s, var2_s, rstd2_s, pool_link, be1_s, ready) = (
             f.sem(s) for s in (
                 "w_in", "t", "a", "yx", "x1", "xT", "xTc", "h", "hT", "y", "o", "gn", "sum2", "norm2", "a_link",
                 "st1_link", "st2_link", "var1", "rstd1", "var2", "rstd2", "pool_link", "be1",
                 "ready"))
        scaled_s = f.sem("scaled")
        block = f.ctx.enter_context(nc.Block())

        def at(i, u, b, d):
            n = u * BL + b + d
            return (n // BL) % 2, n % BL, n % 2

        def exists(i, b, d):
            return not isinstance(i, int) or i * BL + b + d < NW

        @block.sync
        def _(sp):
            sp.dma_start(w1[:, :, :], t["w1T"].rearrange("(k p) n -> p k n", p=P)).then_inc(w_in, 16)
            sp.dma_start(w2[:, :, :], t["w2T"].rearrange("(k p) n -> p k n", p=P)).then_inc(w_in, 16)
            sp.dma_start(b1[:, :], t["b1_col"]).then_inc(w_in, 16)
            for k, v in enumerate((t["g1"], t["be1"], t["g2"], t["b2"])):
                sp.dma_start(vec[:, k, :], v.broadcast_to([P, C])).then_inc(w_in, 16)
            sp.dma_start(col[:, 0, :], t["g1_col"]).then_inc(w_in, 16)
            sp.dma_start(col[:, 1, :], t["be1_col"]).then_inc(w_in, 16)

            def load(i, u):
                sp.dma_start(q[:, u, :, :].rearrange("p b c -> p (b c)"),
                             t["d_q"][:, bass.ds(i * (BL * C), BL * C)]).then_inc(qxn_in[u], 16)
                sp.dma_start(xn[:, u, :, :], block_rows(t["d_xn"], i)).then_inc(qxn_in[u], 16)

            def body(i, u, turn):
                if not isinstance(i, int) or i + 2 < NB:
                    sp.wait_ge(yx_s, i * BL + BL)
                    load(i + 2, u)
                if since(i, 2):
                    sp.wait_ge(o_s, i * BL - BL)
                    sp.dma_start(block_rows(t["d_x1"], i - 2), o[:, u, :, :]).then_inc(stored[u], 16)
                sp.dma_start(x[:, u, :, :], block_rows(t["d_xb"], i)).then_inc(x_in[u], 16)

            load(0, 0)
            load(1, 1)
            run(sp, NB, 2, body, tail=2)
            for i in range(NB - 2, NB):
                sp.wait_ge(o_s, i * BL + BL)
                sp.dma_start(block_rows(t["d_x1"], i), o[:, i % 2, :, :]).then_inc(stored[i % 2], 16)
            for u in range(2):
                sp.wait_ge(qxn_in[u], 32 * (NB // 2))
                sp.wait_ge(x_in[u], 16 * (NB // 2))
                sp.wait_ge(stored[u], 16 * (NB // 2))

        @block.vector
        def _(dve):
            dve.wait_ge(w_in, 9 * 16)
            dve.wait_ge(be1_s, 1)
            nc.vector.memset(one[:, :], 1.0).then_inc(ready, 1)
            nc.vector.tensor_tensor(b1[:, :], b1[:, :], p_h[:, 0, 0:KC], ALU.add).then_inc(ready, 1)
            for k in range(KC):
                nc.vector.tensor_scalar(w1[:, k, :], w1[:, k, :], col[:, 0, k:k + 1], None, ALU.mult).then_inc(ready, 1)
            nc.vector.tensor_tensor(vec[:, 1, :], vec[:, 1, :], vec[:, 3, :], ALU.add).then_inc(ready, 1)

            def attend(n, w, u, b):
                link = Link(dve, a_link, n, 2)
                dve.wait_ge(t_s, n + 1)
                pt = p_t[:, w, 0:KC * (P + HC)].rearrange("p (c n) -> p c n", c=KC)
                link(nc.vector.tensor_scalar(z[:, w, :, :], pt[:, :, P:P + HC], 1e-6, None, ALU.add))
                link(nc.vector.reciprocal(z[:, w, :, :], z[:, w, :, :]))
                y4 = y[:, u, b, :].rearrange("p (c h d) -> p c h d", c=KC, h=HC)
                for c in range(KC):
                    last = nc.vector.tensor_tensor(y4[:, c, :, :], pt[:, c, 0:P].rearrange("p (h d) -> p h d", h=HC),
                                                   z[:, w, c, :, None].broadcast_to([P, HC, D]), ALU.mult)
                last.then_inc(a_s, 1)

            def look1(n, u, b, i):
                dve.wait_ge(yx_s, n + 1)
                last = stats1.take(u, b, y[:, u, b, :])
                if b == BL - 1:
                    stats1.hand_over(dve, Link(dve, st1_link, i, 1), r.hold, u, last, var1_s)

            def normal1(n, u, b, i):
                if b == 0:
                    dve.wait_ge(rstd1_s, i + 1)
                nc.vector.tensor_scalar(x1[:, u, b, :], y[:, u, b, :], stats1.mean(u, b), stats1.scale(u, b),
                                        ALU.subtract, ALU.mult).then_inc(x1_s, 1)

            def sum2(n, w, u, b):
                dve.wait_ge(y_s, n + 1)
                dve.wait_ge(gn_s, n + 1)
                nc.vector.tensor_tensor(o[:, u, b, :], p_y[:, w, 0:C], gn[:, u, b, :], ALU.add).then_inc(sum2_s, 1)

            def look2(n, u, b, i):
                dve.wait_ge(sum2_s, n + 1)
                last = stats2.take(u, b, o[:, u, b, :])
                if b == BL - 1:
                    stats2.hand_over(dve, Link(dve, st2_link, i, 1), r.hold, u, last, var2_s)

            def normal2(n, u, b, blocks):
                if b == 0:
                    dve.wait_ge(var2_s, blocks)
                nc.vector.scalar_tensor_tensor(o[:, u, b, :], o[:, u, b, :], stats2.mean(u, b), vec[:, 2, :],
                                               ALU.subtract, ALU.mult).then_inc(norm2_s, 1)

            def body(i, u, turn):
                for b in range(BL):
                    m = i * BL + b
                    if exists(i, b, 2):
                        v, a, _w = at(i, u, b, 2)
                        normal1(m + 2, v, a, i + (b + 2) // BL)
                    if since(m, 2):
                        v, a, w = at(i, u, b, 2 * BL - 2)
                        if a == 0 and since(i, 2):
                            dve.wait_ge(stored[v], turn * 16)
                        sum2(m - 2, w, v, a)
                    if exists(i, b, AHEAD):
                        v, a, w = at(i, u, b, AHEAD)
                        attend(m + AHEAD, w, v, a)
                    if since(m, 2):
                        v, a, w = at(i, u, b, 2 * BL - 2)
                        look2(m - 2, v, a, i if b >= 2 else i - 1)
                    if exists(i, b, AHEAD - 1):
                        v, a, w = at(i, u, b, AHEAD - 1)
                        look1(m + AHEAD - 1, v, a, i + (b + AHEAD - 1) // BL)
                    if since(i, 1):
                        for j in LATE[b]:
                            normal2((i - 1) * BL + j, 1 - u, j, i)

            for n in range(AHEAD):
                attend(n, n % 2, n // BL, n % BL)
                if n:
                    look1(n - 1, (n - 1) // BL, (n - 1) % BL, (n - 1) // BL)
            for n in range(2):
                normal1(n, 0, n, 0)
            run(dve, NB, 2, body, tail=2)
            for n in (NW - 2, NW - 1):
                sum2(n, n % 2, (NB - 1) % 2, n % BL)
                look2(n, (NB - 1) % 2, n % BL, NB - 1)
            for j in range(BL):
                normal2(NW - BL + j, (NB - 1) % 2, j, NB)

        @block.gpsimd
        def _(pool):
            pool.wait_ge(w_in, 9 * 16)
            pool.wait_ge(ready, 3 + KC)

            def add_xn(n, u, b, turn):
                if b == 0:
                    pool.wait_ge(qxn_in[u], turn * 32 + 32)
                    pool.sem_inc(r.pool_hold, 1)
                pool.wait_ge(a_s, n + 1)
                nc.gpsimd.tensor_tensor(y[:, u, b, :], y[:, u, b, :], xn[:, u, b, :], ALU.add).then_inc(yx_s, 1)

            def scale_x1(n, u, b):
                pool.wait_ge(x1_s, n + 1)
                nc.gpsimd.tensor_tensor(gn[:, u, b, :], x1[:, u, b, :], vec[:, 0, :], ALU.mult).then_inc(gn_s, 1)

            def finish(n, u, b):
                pool.wait_ge(scaled_s, n + 1)
                nc.gpsimd.tensor_tensor(o[:, u, b, :], o[:, u, b, :], x[:, u, b, :], ALU.add).then_inc(o_s, 1)

            def close(stats, var_s, rstd_s, n, i, u):
                pool.wait_ge(var_s, i + 1)
                stats.pool_close(Link(pool, pool_link, n, 1), u, r.power, rstd_s)

            def body(i, u, turn):
                for b in range(BL):
                    m = i * BL + b
                    if exists(i, b, 2):
                        v, a, _w = at(i, u, b, 2)
                        scale_x1(m + 2, v, a)
                    if exists(i, b, AHEAD):
                        v, a, _w = at(i, u, b, AHEAD)
                        add_xn(m + AHEAD, v, a, turn + (u * BL + b + AHEAD) // (2 * BL))
                    if since(i, 1):
                        if b == 1:
                            close(stats2, var2_s, rstd2_s, 2 * i, i - 1, 1 - u)
                            pool.wait_ge(x_in[1 - u], (turn + u) * 16)
                            pool.sem_inc(r.pool_hold, 1)
                        for j in LATE[b]:
                            finish((i - 1) * BL + j, 1 - u, j)
                    if b == 3 and (not isinstance(i, int) or i + 1 < NB):
                        close(stats1, var1_s, rstd1_s, 2 * i + 1, i + 1, 1 - u)

            for n in range(AHEAD):
                add_xn(n, n // BL, n % BL, 0)
                if n == BL:
                    close(stats1, var1_s, rstd1_s, 0, 0, 0)
            for n in range(2):
                scale_x1(n, 0, n)
            run(pool, NB, 2, body, tail=2)
            close(stats2, var2_s, rstd2_s, 2 * NB - 1, NB - 1, (NB - 1) % 2)
            pool.wait_ge(x_in[(NB - 1) % 2], (NB // 2) * 16)
            for j in range(BL):
                finish(NW - BL + j, (NB - 1) % 2, j)

        @block.scalar
        def _(act):
            act.wait_ge(ready, 3 + KC)

            def turned(n, w):
                act.wait_ge(xT_s, n + 1)
                nc.scalar.copy(x1T[:, w, :], p_x[:, w, 0:C]).then_inc(xTc_s, 1)

            def body(i, u, turn):
                for b in range(BL):
                    m, w = i * BL + b, (u * BL + b) % 2
                    if exists(i, b, 1):
                        turned(m + 1, 1 - w)
                    act.wait_ge(h_s, m + 1)
                    for c in range(KC):
                        last = nc.scalar.activation(hT[:, w, c, :], p_h[:, w, c * P:(c + 1) * P], ACT.Gelu,
                                                    bias=b1[:, c:c + 1])
                    last.then_inc(hT_s, 1)
                    if since(i, 1):
                        for j in LATE[b]:
                            scaled((i - 1) * BL + j, 1 - u, j, i)

            def scaled(n, u, b, blocks):
                if b == 0:
                    act.wait_ge(rstd2_s, blocks)
                act.wait_ge(norm2_s, n + 1)
                nc.scalar.activation(o[:, u, b, :], o[:, u, b, :], ACT.Identity,
                                     scale=stats2.scale(u, b)).then_inc(scaled_s, 1)

            turned(0, 0)
            run(act, NB, 2, body, tail=2)
            for j in range(BL):
                scaled(NW - BL + j, (NB - 1) % 2, j, NB)

        @block.tensor
        def _(pe):
            pe.wait_ge(w_in, 9 * 16)
            for c in range(KC):
                for k in range(KC):
                    last = nc.tensor.matmul(p_h[:, 0, c:c + 1], w1[:, k, c * P:(c + 1) * P], col[:, 1, k:k + 1],
                                            start=(k == 0), stop=(k == KC - 1))
            last.then_inc(be1_s, 1)
            pe.wait_ge(ready, 3 + KC)

            def read(n, w, u, b, turn):
                if b == 0:
                    pe.wait_ge(qxn_in[u], turn * 32 + 32)
                if since(n, 2):
                    pe.wait_ge(a_s, n - 1)
                for c in range(KC):
                    last = nc.tensor.matmul(p_t[:, w, c * (P + HC):(c + 1) * (P + HC)], q[:, u, b, c * P:(c + 1) * P],
                                            r.kvbd[:, c, :], start=True, stop=True)
                last.then_inc(t_s, 1)

            def turn_tile(n, w, u, b):
                pe.wait_ge(x1_s, n + 1)
                for c in range(KC):
                    last = nc.tensor.transpose(p_x[:, w, c * P:(c + 1) * P], x1[:, u, b, c * P:(c + 1) * P],
                                               r.ident[:, :])
                last.then_inc(xT_s, 1)

            def inner(n, w):
                pe.wait_ge(xTc_s, n + 1)
                for c in range(KC):
                    for k in range(KC):
                        last = nc.tensor.matmul(p_h[:, w, c * P:(c + 1) * P], w1[:, k, c * P:(c + 1) * P],
                                                x1T[:, w, k * P:(k + 1) * P], start=(k == 0), stop=(k == KC - 1))
                last.then_inc(h_s, 1)

            def outer(n, w):
                pe.wait_ge(hT_s, n + 1)
                if since(n, 2):
                    pe.wait_ge(sum2_s, n - 1)
                nc.tensor.matmul(p_y[:, w, 0:C], one[:, :], vec[0:1, 1, :], start=True, stop=False)
                for k in range(KC):
                    last = nc.tensor.matmul(p_y[:, w, 0:C], hT[:, w, k, :], w2[:, k, :],
                                            start=False, stop=(k == KC - 1))
                last.then_inc(y_s, 1)

            def body(i, u, turn):
                for b in range(BL):
                    m, w = i * BL + b, (u * BL + b) % 2
                    if exists(i, b, 1):
                        v, a, _w = at(i, u, b, 1)
                        turn_tile(m + 1, 1 - w, v, a)
                    inner(m, w)
                    if exists(i, b, AHEAD):
                        v, a, w_ = at(i, u, b, AHEAD)
                        read(m + AHEAD, w_, v, a, turn + (u * BL + b + AHEAD) // (2 * BL))
                    if since(m, 1):
                        outer(m - 1, 1 - w)

            for n in range(AHEAD):
                read(n, n % 2, n // BL, n % BL, 0)
            turn_tile(0, 0, 0, 0)
            run(pe, NB, 2, body, tail=2)
            outer(NW - 1, (NW - 1) % 2)


def edge_scores(nc, t, r, ph, al, asrc):
    W = GT * P
    CX = C + H
    with Phase(nc, "score") as f:
        hw = f.sb("hw", [P, UE, 2, CX], F32R)
        dstb = f.sb("dstb", [P, UE, W], I32)
        ea = f.sb("ea", [3 * EF, UE, W], F32R)
        mt = f.sb("mt", [P, UE, W], F32R)
        rel = f.sb("rel", [P, 2, 2 * C])
        pr = f.sb("pr", [P, 2, 2 * C])
        ad = f.sb("ad", [P, 2, GT * H])
        red = f.sb("red", [P, 2, GT * H])
        ew = f.sb("ew", [3 * EF, C], F32R)
        sring = f.sb("sring", [P, 2, GP], U32)
        gring = f.sb("gring", [P, 2, GP, H])
        p_enc = f.ps("p_enc", [P, 2, 2 * C])
        p_hd = f.ps("p_hd", [P, 2, 2, 512])
        ins = f.sems("ins", UE)
        gat = f.sems("gat", 2)
        w_in, mt_s, enc_s, hd_s, rel_s, pr_s, ad_s, red_s, add_s, ring_s, out_s, link_s = (f.sem(s) for s in (
            "w_in", "mt", "enc", "hd", "rel", "pr", "ad", "red", "add", "ring", "out", "link"))
        block = f.ctx.enter_context(nc.Block())
        PAIRS = GT // 2

        @block.sync
        def _(sp):
            sp.dma_start(ew[:, :].bitcast(F32), t["d_ew"]).then_inc(w_in, 16)

            def body(s, u, turn):
                if since(s, UE):
                    sp.wait_ge(hd_s, (s - UE) * PAIRS + PAIRS)
                g = sp.value_load(ph.g_int[0:1, bass.ds(s, 1)], min_val=0, max_val=T // GT - 1)
                w = sp.value_load(ph.w_int[0:1, bass.ds(s, 1)], min_val=0, max_val=NW - 1)
                sp.dma_start(hw[:, u, :, :].bitcast(F32), rows(t["d_hw"], w).rearrange("p (a c) -> p a c", a=2)).then_inc(ins[u], 16)
                sp.dma_start(dstb[:, u, :], t["dst_row"][:, bass.ds(g * W, W)].broadcast_to([P, W])).then_inc(ins[u], 16)
                sp.dma_start(ea[:, u, :].bitcast(F32), t["d_ea"][:, bass.ds(g * W, W)]).then_inc(ins[u], 16)

            run(sp, STEPS, UE, body, times=3)
            for u in range(UE):
                sp.wait_ge(ins[u], 48 * (STEPS // UE))

        @block.gpsimd
        def _(pool):
            last_batch = T // GP - 1

            def indices(i, u):
                nc.gpsimd.tensor_copy(sring[:, u, :], r.src[:, bass.ds(i * GP, GP)]).then_inc(ring_s, 1)

            def take(i, u, turn):
                pool.wait_ge(gat[u], turn * (16 * GP) + 16 * GP)
                nc.gpsimd.tensor_copy(asrc[:, bass.ds(i * (GP * H), GP * H)],
                                      gring[:, u, :, :].rearrange("p k h -> p (k h)")).then_inc(out_s, 1)

            def body(i, u, turn):
                pool.wait_ge(ring_s, i + 1)
                pool.sem_inc(r.pool_hold, 1)
                if since(i, 2):
                    pool.wait_ge(out_s, i - 1)
                    pool.sem_inc(r.pool_hold, 1)
                for k in range(GP):
                    if k == GP // 2:
                        if since(i, 1):
                            take(i - 1, 1 - u, turn - 1 if u == 0 else turn)
                        if not isinstance(i, int) or i < last_batch:
                            indices(i + 1, 1 - u)
                    nc.gpsimd.indirect_dma_start(gring[:, u, k, :], None, t["d_as"][:, :],
                                                 bass.IndirectOffsetOnAxis(sring[:, u, k:k + 1], 0)).then_inc(gat[u], 16)

            indices(0, 0)
            run(pool, T // GP, 2, body, tail=1)
            take(last_batch, last_batch % 2, last_batch // 2)

        @block.vector
        def _(dve):
            nc.vector.memset(al[:, :], 0.0).then_inc(add_s, 1)

            def onehot(s, u, turn):
                dve.wait_ge(ins[u], turn * 48 + 48)
                nc.vector.tensor_scalar(mt[:, u, :], dstb[:, u, :], ph.j_node[:, bass.ds(s, 1)], None,
                                        ALU.is_equal).then_inc(mt_s, 1)

            def finish(s, u):
                v = u % 2
                dve.wait_ge(red_s, s * PAIRS + PAIRS)
                dve.wait_ge(ad_s, s * PAIRS + PAIRS)
                nc.vector.tensor_tensor(red[:, v, :], red[:, v, :], ad[:, v, :], ALU.add).then_inc(link_s, 1)

            def add(s, u):
                g = dve.value_load(ph.g_int[0:1, bass.ds(s, 1)], min_val=0, max_val=T // GT - 1)
                dve.wait_ge(link_s, s + 1)
                dve.wait_ge(add_s, s + 1)
                sl = al[:, bass.ds(g * (GT * H), GT * H)]
                nc.vector.tensor_tensor(sl, sl, red[:, u % 2, :], ALU.add).then_inc(add_s, 1)

            def multiply(s, p):
                m = s * PAIRS + p
                dve.wait_ge(hd_s, m + 1)
                dve.wait_ge(rel_s, m + 1)
                if since(s, 1):
                    dve.wait_ge(red_s, m - 1)
                nc.vector.tensor_tensor(pr[:, p, :].rearrange("p (k c) -> p k c", k=2),
                                        rel[:, p, :].rearrange("p (k c) -> p k c", k=2), p_hd[:, p, :, 0:C],
                                        ALU.mult).then_inc(pr_s, 1)

            def body(s, u, turn):
                v = u % 2
                if not isinstance(s, int) or s < STEPS - 1:
                    onehot(s + 1, (u + 1) % UE, turn + (u == UE - 1))
                for p in range(PAIRS):
                    multiply(s, p)
                    if since(s, 1):
                        (finish, add)[p](s - 1, (u - 1) % UE)
                for p in range(PAIRS):
                    m = s * PAIRS + p
                    dve.wait_ge(pr_s, m + 1)
                    nc.vector.tensor_reduce(red[:, v, p * 2 * H:(p + 1) * 2 * H],
                                            pr[:, p, :].rearrange("p (h d) -> p h d", d=D), AX.X, ALU.add).then_inc(red_s, 1)

            onehot(0, 0, 0)
            run(dve, STEPS, UE, body, tail=1, times=3)
            finish(STEPS - 1, (STEPS - 1) % UE)
            add(STEPS - 1, (STEPS - 1) % UE)

        @block.scalar
        def _(act):
            def destination(s, v, p):
                m = s * PAIRS + p
                act.wait_ge(pr_s, m + 1)
                if since(s, 2):
                    act.wait_ge(link_s, s - 1)
                nc.scalar.copy(ad[:, v, p * 2 * H:(p + 1) * 2 * H].rearrange("p (k h) -> p k h", k=2),
                               p_hd[:, p, :, C:CX]).then_inc(ad_s, 1)

            def body(s, u, turn):
                for p in range(PAIRS):
                    m = s * PAIRS + p
                    if since(s, 1):
                        destination(s - 1, (u - 1) % 2, p)
                    act.wait_ge(enc_s, m + 1)
                    if since(s, 1):
                        act.wait_ge(pr_s, m - 1)
                    nc.scalar.activation(rel[:, p, :], p_enc[:, p, :], ACT.Relu).then_inc(rel_s, 1)

            run(act, STEPS, UE, body, times=3)
            for p in range(PAIRS):
                destination(STEPS - 1, (STEPS - 1) % 2, p)

        @block.tensor
        def _(pe):
            pe.wait_ge(w_in, 16)

            def body(s, u, turn):
                v = u % 2
                pe.wait_ge(ins[u], turn * 48 + 48)
                pe.wait_ge(mt_s, s + 1)
                for p in range(PAIRS):
                    m = s * PAIRS + p
                    if since(s, 1):
                        pe.wait_ge(rel_s, m - 1)
                    for k in range(2):
                        e = slice((2 * p + k) * P, (2 * p + k + 1) * P)
                        last = nc.tensor.matmul(p_enc[:, p, k * C:(k + 1) * C], ea[:, u, e], ew[:, :],
                                                start=True, stop=True)
                    last.then_inc(enc_s, 1)
                    if since(s, 1):
                        pe.wait_ge(ad_s, m - 1)
                    for k in range(2):
                        e = slice((2 * p + k) * P, (2 * p + k + 1) * P)
                        for part in range(2):
                            last = nc.tensor.matmul(p_hd[:, p, k, 0:CX], mt[:, u, e], hw[:, u, part, :],
                                                    start=(part == 0), stop=(part == 1))
                    last.then_inc(hd_s, 1)

            run(pe, STEPS, UE, body, times=3)


def edge_softmax(nc, t, r, al, asrc):
    by_pair = lambda x, b: x[:, 0:T * H].rearrange("p (c b h) -> p c b h", c=CH, h=H)[:, :, bass.ds(b * 2, 2), :] \
        .rearrange("p c b h -> p b c h")
    pen, db, ex = al, asrc, al
    PIECE = CE // 8
    with Phase(nc, "soft") as f:
        a = f.sb("a", [P, CE])
        slot = f.sb("slot", [P, 2, 2, P])
        back = f.sb("back", [P, 2, 2 * P])
        trash = f.sb("trash", [P, 2, PIECE])
        ends = f.sb("ends", [P, 2])
        inner = f.sb("inner", [P, 1])
        srow = f.sb("srow", [1, 2, P])
        crow = f.sb("crow", [1, P + H])
        carry = f.sb("carry", [P, 1])
        one = f.sb("one", [1, 1])
        p_a = f.ps("p_a", [P, 2, 512])
        p_e = f.ps("p_e", [P, 2, 512])
        p_row = f.ps("p_row", [1, 2, P])
        p_c = f.ps("p_c", [P, 1])

        link_s, slot_s, turned, got = (f.sem(s) for s in ("t_link", "t_slot", "t_turned", "t_got"))
        with nc.Block() as block:
            @block.vector
            def _(dve):
                def body(b, u, turn):
                    link = Link(dve, link_s, b, 1)
                    o = slot[:, u, :, :].rearrange("p b (c h) -> p b c h", h=H)
                    if since(b, 2):
                        dve.wait_ge(turned, b - 1)
                    link(nc.vector.tensor_tensor(o, by_pair(al, b), by_pair(asrc, b), ALU.add))
                    nc.vector.scalar_tensor_tensor(slot[:, u, :, :], slot[:, u, :, :], 0.2, slot[:, u, :, :],
                                                   ALU.mult, ALU.max).then_inc(slot_s, 1)

                run(dve, TC // 2, 2, body)

            @block.tensor
            def _(pe):
                def body(b, u, turn):
                    pe.wait_ge(slot_s, b + 1)
                    if since(b, 2):
                        pe.wait_ge(got, b - 1)
                    for k in range(2):
                        last = nc.tensor.transpose(p_a[:, u, k * P:(k + 1) * P], slot[:, u, k, :], r.ident[:, :])
                    last.then_inc(turned, 1)

                run(pe, TC // 2, 2, body)

            @block.scalar
            def _(act):
                def body(b, u, turn):
                    act.wait_ge(turned, b + 1)
                    nc.scalar.copy(a[:, bass.ds(b * (2 * P), 2 * P)], p_a[:, u, 0:2 * P]).then_inc(got, 1)

                run(act, TC // 2, 2, body)

        dst_in, link_s, rows_s, row_ps, carry_ps, crow_s = (
            f.sem(s) for s in ("dst_in", "s_link", "s_rows", "s_row_ps", "s_carry_ps", "s_crow"))
        with nc.Block() as block:
            @block.sync
            def _(sp):
                for c in range(CH):
                    sp.dma_start(db[c * H:(c + 1) * H, 0:CE + 2].bitcast(I32),
                                 t["dst_ext"][0:1, c * CE:c * CE + CE + 2].broadcast_to([H, CE + 2])).then_inc(dst_in, 16)
                sp.wait_ge(dst_in, 16 * CH)

            @block.vector
            def _(dve):
                link = Link(dve, link_s)
                dve.wait_ge(dst_in, 16 * CH)
                di = db[:, :].bitcast(I32)
                link(nc.vector.memset(one[:, :], 1.0))
                link(nc.vector.tensor_tensor(pen[:, 0:CE + 1], di[:, 0:CE + 1], di[:, 1:CE + 2], ALU.not_equal))
                link(nc.vector.tensor_scalar(pen[:, 0:CE + 1], pen[:, 0:CE + 1], -BIG, None, ALU.mult))

                def sweep(data, out, shift, reverse, n):
                    step = slice(None, None, -1) if reverse else slice(None)
                    state = -BIG
                    for j in (range(7, -1, -1) if reverse else range(8)):
                        a0 = j * PIECE
                        o = trash[:, j % 2, :]
                        link(nc.vector.tensor_tensor_scan(o[:, step], pen[:, shift + a0:shift + a0 + PIECE][:, step],
                                                          data[:, a0:a0 + PIECE][:, step], state, ALU.add, ALU.max))
                        state = o[:, 0:1] if reverse else o[:, PIECE - 1:PIECE]
                    link(nc.vector.tensor_copy(ends[:, 0:1], state))
                    link(nc.vector.tensor_tensor(ends[:, 1:2], inner[:, :], pen[:, 0:1] if shift == 0 else pen[:, CE:CE + 1],
                                                 ALU.min))
                    nc.vector.memset(crow[:, :], -BIG).then_inc(rows_s, 1)
                    dve.wait_ge(rows_s, n)
                    dve.wait_ge(row_ps, n)
                    link(nc.vector.tensor_copy(srow[:, :, :], p_row[:, :, :]))
                    for h in range(H):
                        own = srow[:, 0, h:P:H][:, step]
                        through = srow[:, 1, h:P:H][:, step]
                        o = (crow[:, h:P:H] if reverse else crow[:, h + H:P + H:H])[:, step]
                        link(nc.vector.tensor_tensor_scan(o, through, own, -BIG, ALU.add, ALU.max))
                    dve.sem_inc(crow_s, 1)
                    dve.wait_ge(carry_ps, n)
                    link(nc.vector.tensor_copy(carry[:, :], p_c[:, :]))
                    link(nc.vector.tensor_tensor_scan(out[:, 0:CE][:, step], pen[:, shift:shift + CE][:, step],
                                                      data[:, 0:CE][:, step], carry[:, 0:1], ALU.add, ALU.max))

                link(nc.vector.tensor_reduce(inner[:, :], pen[:, 1:CE], AX.X, ALU.min))
                sweep(a, db, 0, False, 1)
                sweep(db, db, 1, True, 2)
                link(nc.vector.tensor_tensor(a[:, :], a[:, :], db[:, 0:CE], ALU.subtract))

            @block.tensor
            def _(pe):
                for n in (1, 2):
                    pe.wait_ge(rows_s, n)
                    for k in range(2):
                        last = nc.tensor.transpose(p_row[:, k, :], ends[:, k:k + 1], r.ident[:, :])
                    last.then_inc(row_ps, 1)
                    pe.wait_ge(crow_s, n)
                    off = 0 if n == 1 else H
                    nc.tensor.matmul(p_c[:, :], crow[:, off:off + P], one[:, :], start=True, stop=True).then_inc(carry_ps, 1)

        exp_s, turned, got = (f.sem(s) for s in ("e_exp", "e_turned", "e_got"))
        with nc.Block() as block:
            @block.scalar
            def _(act):
                def body(b, u, turn):
                    if since(b, 2):
                        act.wait_ge(turned, b - 1)
                    nc.scalar.activation(back[:, u, :], a[:, bass.ds(b * (2 * P), 2 * P)], ACT.Exp).then_inc(exp_s, 1)

                run(act, TC // 2, 2, body)

            @block.tensor
            def _(pe):
                def body(b, u, turn):
                    pe.wait_ge(exp_s, b + 1)
                    if since(b, 2):
                        pe.wait_ge(got, b - 1)
                    for k in range(2):
                        last = nc.tensor.transpose(p_e[:, u, k * P:(k + 1) * P], back[:, u, k * P:(k + 1) * P],
                                                   r.ident[:, :])
                    last.then_inc(turned, 1)

                run(pe, TC // 2, 2, body)

            @block.vector
            def _(dve):
                def body(b, u, turn):
                    dve.wait_ge(turned, b + 1)
                    nc.vector.tensor_copy(by_pair(ex, b), p_e[:, u, 0:2 * P].rearrange("p (b c h) -> p b c h", b=2, h=H)
                                          ).then_inc(got, 1)

                run(dve, TC // 2, 2, body)


def edge_sums(nc, t, r, ph, ex, acc):
    CX = C + H
    with Phase(nc, "sum") as f:
        sring = f.sb("sring", [P, R, GT], U32)
        hg = f.sb("hg", [P, R, GT, C])
        x = f.sb("x", [P, 2, GT, CX])
        dc = f.sb("dc", [P, 2, GT])
        mm = f.sb("mm", [P, 2, GT, P])
        p_o = f.ps("p_o", [P, UE, 512])
        gat = f.sems("gat", R)
        ring_s, landed, x_s, m_s, o_s, acc_s, link_s = (
            f.sem(s) for s in ("ring", "landed", "x", "m", "o", "acc", "link"))
        block = f.ctx.enter_context(nc.Block())

        @block.gpsimd
        def _(pool):
            G = T // GT

            def indices(g, k):
                nc.gpsimd.tensor_copy(sring[:, k:k + R // 2, :].rearrange("p r k -> p (r k)"),
                                      r.src[:, bass.ds(g * GT, R // 2 * GT)]).then_inc(ring_s, 1)

            def land(g, k, turn):
                pool.wait_ge(gat[k], turn * (16 * GT) + 16 * GT)
                pool.sem_inc(landed, 1)

            def body(g, k, turn):
                if since(g, LAG):
                    land(g - LAG, (k - LAG) % R, turn - 1 if k < LAG else turn)
                if since(g, R):
                    begin = pool.value_load(ph.start[0:1, bass.ds(g - R + 1, 1)], min_val=1, max_val=STEPS)
                    pool.wait_ge(x_s, begin)
                    pool.sem_inc(r.pool_hold, 1)
                if k % (R // 2) == 0:
                    pool.wait_ge(ring_s, turn * 2 + 1 + k // (R // 2))
                    pool.sem_inc(r.pool_hold, 1)
                for j in range(GT):
                    nc.gpsimd.indirect_dma_start(hg[:, k, j, :], None, t["d_h"][:, :],
                                                 bass.IndirectOffsetOnAxis(sring[:, k, j:j + 1], 0)).then_inc(gat[k], 16)
                if k % (R // 2) == R // 2 - 1 and (not isinstance(g, int) or g < G - 1):
                    indices(g + 1, (k + 1) % R)

            indices(0, 0)
            run(pool, G, R, body, tail=1, times=2)
            for g in range(G - LAG, G):
                land(g, g % R, g // R)

        @block.vector
        def _(dve):
            nc.vector.memset(acc[:, :, :], 0.0).then_inc(acc_s, 1)

            def add(s, u):
                w = dve.value_load(ph.w_int[0:1, bass.ds(s, 1)], min_val=0, max_val=NW - 1)
                dve.wait_ge(o_s, s + 1)
                dve.wait_ge(acc_s, s + 1)
                sl = acc[:, bass.ds(w, 1), :].rearrange("p a c -> p (a c)")
                nc.vector.tensor_tensor(sl, sl, p_o[:, u, 0:CX], ALU.add).then_inc(acc_s, 1)

            def body(s, u, turn):
                v = u % 2
                g = dve.value_load(ph.g_int[0:1, bass.ds(s, 1)], min_val=0, max_val=T // GT - 1)
                if since(s, 2):
                    dve.wait_ge(o_s, s - 1)
                nc.vector.tensor_scalar(dc[:, v, :], r.dst[:, bass.ds(g * GT, GT)], ph.w_node[:, bass.ds(s, 1)],
                                        None, ALU.subtract).then_inc(link_s, 1)
                eg = ex[:, bass.ds(g * (GT * H), GT * H)].rearrange("p (k h) -> p k h", h=H)
                nc.vector.tensor_copy(x[:, v, :, C:CX], eg)
                dve.wait_ge(link_s, s + 1)
                nc.vector.tensor_tensor(mm[:, v, :, :], r.jrow[:, None, :].broadcast_to([P, GT, P]),
                                        dc[:, v, :, None].broadcast_to([P, GT, P]), ALU.is_equal).then_inc(m_s, 1)
                dve.wait_ge(landed, g + 1)
                dve.sem_inc(r.hold, 1)
                for k in range(GT):
                    rows_k = hg[:, bass.ds(g & (R - 1), 1), k, :].rearrange("p a (h d) -> p (a h) d", d=D)
                    last = nc.vector.tensor_tensor(x[:, v, k, 0:C].rearrange("p (h d) -> p h d", h=H), rows_k,
                                                   eg[:, k, :, None].broadcast_to([P, H, D]), ALU.mult)
                last.then_inc(x_s, 1)
                if since(s, 2):
                    add(s - 2, (u - 2) % UE)

            run(dve, STEPS, UE, body, times=3)
            for s in (STEPS - 2, STEPS - 1):
                add(s, s % UE)

        @block.tensor
        def _(pe):
            def body(s, u, turn):
                v = u % 2
                pe.wait_ge(m_s, s + 1)
                pe.wait_ge(x_s, s + 1)
                if since(s, UE):
                    pe.wait_ge(acc_s, s - UE + 2)
                for k in range(GT):
                    last = nc.tensor.matmul(p_o[:, u, 0:CX], mm[:, v, k, :], x[:, v, k, :],
                                            start=(k == 0), stop=(k == GT - 1))
                last.then_inc(o_s, 1)

            run(pe, STEPS, UE, body, times=3)


def node_update(nc, t, r, acc, spare):
    with Phase(nc, "upd") as f:
        part = 2 * BL * C
        x1 = spare[:, 0:part].rearrange("p (u b c) -> p u b c", u=2, c=C)
        xfT = spare[:, part:2 * part].rearrange("p (u k n) -> p u k n", u=2, k=KC)
        den = f.sb("den", [P, 2, BL, H])
        xf = f.sb("xf", [P, 2, BL, C])
        stats = Stats(nc, f, "x2")
        zero = f.sb("zero", [P, P])
        p_x = f.ps("p_x", [P, 2, 512])
        p_m = f.ps("p_m", [P, KC])
        x1_in, stored = f.sems("x1_in", 2), f.sems("stored", 2)
        mul_s, x2_s, xf_s, xT_s, xTc_s, link_s, st_link, zero_s, mean_s, var_s, rstd_s, pool_link = (
            f.sem(s) for s in ("mul", "x2", "xf", "xT", "xTc", "link", "st_link", "zero", "mean", "var",
                               "rstd", "pool_link"))
        block = f.ctx.enter_context(nc.Block())

        @block.sync
        def _(sp):
            def load(i, u):
                sp.dma_start(x1[:, u, :, :], block_rows(t["d_x1"], i)).then_inc(x1_in[u], 16)

            def store(i, u):
                sp.wait_ge(xTc_s, i * BL + BL)
                sp.sem_inc(r.hold, 1)
                sp.dma_start(t["d_xfT"][:, :, bass.ds(i * (BL * P), BL * P)], xfT[:, u, :, :]).then_inc(stored[u], 16)

            def body(i, u, turn):
                if not isinstance(i, int) or i + 2 < NB:
                    sp.wait_ge(x2_s, i * BL + BL)
                    load(i + 2, u)
                if since(i, 1):
                    store(i - 1, 1 - u)

            load(0, 0)
            load(1, 1)
            run(sp, NB, 2, body, tail=2)
            store(NB - 1, (NB - 1) % 2)
            for u in range(2):
                sp.wait_ge(x1_in[u], 16 * (NB // 2))
                sp.wait_ge(stored[u], 16 * (NB // 2))

        @block.vector
        def _(dve):
            nc.vector.memset(zero[:, :], 0.0).then_inc(zero_s, 1)

            tile = lambda n: acc[:, bass.ds(n, 1), 0:C].rearrange("p a c -> p (a c)")

            def divide(i, u):
                link = Link(dve, link_s, i, 2)
                a = acc[:, bass.ds(i * BL, BL), :]
                link(nc.vector.tensor_scalar(den[:, u, :, :], a[:, :, C:C + H], 1e-10, None, ALU.max))
                link(nc.vector.reciprocal(den[:, u, :, :], den[:, u, :, :]))
                for b in range(BL):
                    ab = acc[:, bass.ds(i * BL + b, 1), 0:C].rearrange("p a (h d) -> p (a h) d", h=H)
                    nc.vector.tensor_tensor(ab, ab, den[:, u, b, :, None].broadcast_to([P, H, D]),
                                            ALU.mult).then_inc(mul_s, 1)

            def look(i, u):
                for b in range(BL):
                    dve.wait_ge(x2_s, i * BL + b + 1)
                    dve.sem_inc(r.hold, 1)
                    last = stats.take(u, b, tile(i * BL + b))
                stats.hand_over(dve, Link(dve, st_link, i, 1), r.hold, u, last, var_s)

            def normal(i, u):
                dve.wait_ge(rstd_s, i + 1)
                if since(i, 2):
                    dve.wait_ge(xTc_s, i * BL - BL)
                dve.sem_inc(r.hold, 1)
                nc.vector.tensor_copy(r.mu[:, bass.ds(i * BL, BL)], stats.mv[:, u, :, 0])
                nc.vector.tensor_copy(r.rs[:, bass.ds(i * BL, BL)], stats.rstd[:, u, :])
                for b in range(BL):
                    nc.vector.tensor_scalar(xf[:, u, b, :], tile(i * BL + b), stats.mean(u, b), stats.scale(u, b),
                                            ALU.subtract, ALU.mult).then_inc(xf_s, 1)

            def body(i, u, turn):
                if not isinstance(i, int) or i + 1 < NB:
                    divide(i + 1, 1 - u)
                look(i, u)
                if since(i, 1):
                    normal(i - 1, 1 - u)

            divide(0, 0)
            run(dve, NB, 2, body, tail=1)
            normal(NB - 1, (NB - 1) % 2)
            dve.wait_ge(mean_s, 1)
            nc.vector.tensor_scalar(r.mean[:, :], p_m[:, :], 1.0 / N, None, ALU.mult).then_inc(zero_s, 1)

        @block.gpsimd
        def _(pool):
            def body(i, u, turn):
                pool.wait_ge(x1_in[u], turn * 16 + 16)
                pool.sem_inc(r.pool_hold, 1)
                for b in range(BL):
                    pool.wait_ge(mul_s, i * BL + b + 1)
                    x2 = acc[:, bass.ds(i * BL + b, 1), 0:C].rearrange("p a c -> p (a c)")
                    nc.gpsimd.tensor_tensor(x2, x2, x1[:, u, b, :], ALU.add).then_inc(x2_s, 1)
                pool.wait_ge(var_s, i + 1)
                stats.pool_close(Link(pool, pool_link, i, 1), u, r.power, rstd_s)

            run(pool, NB, 2, body)

        @block.scalar
        def _(act):
            def body(i, u, turn):
                for b in range(BL):
                    act.wait_ge(xT_s, i * BL + b + 1)
                    if b == 0 and since(i, 2):
                        act.wait_ge(stored[u], turn * 16)
                    nc.scalar.copy(xfT[:, u, :, b * P:(b + 1) * P],
                                   p_x[:, (u * BL + b) % 2, 0:C].rearrange("p (k n) -> p k n", k=KC)).then_inc(xTc_s, 1)

            run(act, NB, 2, body)

        @block.tensor
        def _(pe):
            pe.wait_ge(zero_s, 1)
            nc.tensor.matmul(p_m[:, :], zero[:, :], r.ident[:, 0:KC], start=True, stop=False, skip_group_check=True)

            def body(i, u, turn):
                for b in range(BL):
                    m, w = i * BL + b, (u * BL + b) % 2
                    pe.wait_ge(xf_s, m + 1)
                    if since(m, 2):
                        pe.wait_ge(xTc_s, m - 1)
                    for c in range(KC):
                        nc.tensor.matmul(p_m[:, c:c + 1], xf[:, u, b, c * P:(c + 1) * P], r.valid[:, bass.ds(m, 1)],
                                         start=False, stop=False, skip_group_check=True)
                    for c in range(KC):
                        last = nc.tensor.transpose(p_x[:, w, c * P:(c + 1) * P], xf[:, u, b, c * P:(c + 1) * P],
                                                   r.ident[:, :])
                    last.then_inc(xT_s, 1)

            run(pe, NB, 2, body)
            nc.tensor.matmul(p_m[:, :], zero[:, :], r.ident[:, 0:KC], start=False, stop=True,
                             skip_group_check=True).then_inc(mean_s, 1)


def route(nc, t, r, q):
    with Phase(nc, "route") as f:
        wr = f.sb("wr", [P, KC, XP])
        row = lambda n, w=XP: f.sb(n, [1, w])
        br, io, lg, ex, rw, big, sc, eq, pick, r2 = (row(n) for n in ("br", "io", "lg", "ex", "rw", "big", "sc", "eq", "pick", "r2"))
        s1, idx, top, tw = row("s1", 2), row("idx", 2), row("top", 2), row("tw", 2)
        idx_i = f.sb("idx_i", [1, 2], I32)
        one = f.sb("one", [1, P])
        twb = f.sb("twb", [P, 2])
        b2e = f.sb("b2e", [P, 2, C])
        p_l = f.ps("p_l", [1, XP])
        p_w = f.ps("p_w", [P, 2])
        w_in, e_in, l_s, x_s, a_s, i_s, tw_s, pw_s, link_s = (
            f.sem(s) for s in ("w_in", "e_in", "l", "x", "a", "i", "tw", "pw", "link"))
        block = f.ctx.enter_context(nc.Block())

        @block.sync
        def _(sp):
            sp.dma_start(wr[:, :, :], t["wr"].rearrange("(k p) n -> p k n", p=P)).then_inc(w_in, 16)
            sp.dma_start(br[:, :], t["br"]).then_inc(w_in, 16)
            sp.dma_start(io[:, :], t["c_jrow"][0:1, 0:XP]).then_inc(w_in, 16)
            sp.wait_ge(i_s, 1)
            for k in range(2):
                e = sp.value_load(idx_i[0:1, k:k + 1], min_val=0, max_val=XP - 1)
                sp.dma_start(q.w1[:, k, :, :], t["ffn_w1"][bass.ds(e * C, C), :].rearrange("(k p) n -> p k n", p=P)).then_inc(e_in, 16)
                sp.dma_start(q.w2[:, k, :, :], t["ffn_w2"][bass.ds(e * FF, FF), :].rearrange("(k p) n -> p k n", p=P)).then_inc(e_in, 16)
                sp.dma_start(q.b1[:, k, :], t["ffn_b1"][bass.ds(e * P, P), :]).then_inc(e_in, 16)
                sp.dma_start(b2e[:, k, :], t["ffn_b2"][bass.ds(e, 1), :].broadcast_to([P, C])).then_inc(e_in, 16)
            sp.dma_start(q.g[:, :], t["ffn_g"].broadcast_to([P, C])).then_inc(e_in, 16)
            sp.dma_start(q.be[:, :], t["ffn_be"].broadcast_to([P, C])).then_inc(e_in, 16)
            sp.wait_ge(e_in, 10 * 16)

        @block.vector
        def _(dve):
            link = Link(dve, link_s)
            V = nc.vector
            exps = [0]

            def exp():
                exps[0] += 1
                dve.sem_inc(x_s, 1)
                dve.wait_ge(a_s, exps[0])

            def softmax(dst, n):
                link(V.tensor_reduce(s1[:, 0:1], lg[:, 0:n], AX.X, ALU.max))
                link(V.tensor_scalar(lg[:, 0:n], lg[:, 0:n], s1[:, 0:1], None, ALU.subtract))
                exp()
                link(V.tensor_reduce(s1[:, 1:2], ex[:, 0:n], AX.X, ALU.add))
                link(V.reciprocal(s1[:, 1:2], s1[:, 1:2]))
                link(V.tensor_scalar(dst, ex[:, 0:n], s1[:, 1:2], None, ALU.mult))

            link(V.memset(one[:, :], 1.0))
            link(V.memset(lg[:, :], 0.0))
            link(V.memset(ex[:, :], 0.0))
            dve.wait_ge(w_in, 48)
            dve.wait_ge(l_s, 1)
            link(V.tensor_tensor(lg[:, :], p_l[:, :], br[:, :], ALU.add))
            softmax(rw[:, :], XP)
            link(V.tensor_scalar(big[:, :], rw[:, :], float(TOPW), None, ALU.mult))
            link(V.reciprocal(sc[:, :], big[:, :]))
            link(V.tensor_scalar(big[:, :], big[:, :], CAPACITY, None, ALU.is_gt))
            link(V.scalar_tensor_tensor(sc[:, :], sc[:, :], CAPACITY, big[:, :], ALU.mult, ALU.mult))
            link(V.tensor_scalar(big[:, :], big[:, :], -1.0, 1.0, ALU.mult, ALU.add))
            link(V.tensor_tensor(sc[:, :], sc[:, :], big[:, :], ALU.add))
            link(V.tensor_tensor(lg[:, :], rw[:, :], sc[:, :], ALU.mult))
            softmax(rw[:, :], XP)
            for k in range(2):
                link(V.tensor_reduce(top[:, k:k + 1], rw[:, :], AX.X, ALU.max))
                link(V.tensor_scalar(eq[:, :], rw[:, :], top[:, k:k + 1], float(-XP), ALU.is_equal, ALU.mult))
                link(V.scalar_tensor_tensor(pick[:, :], eq[:, :], float(XP), io[:, :], ALU.add, ALU.add))
                link(V.tensor_reduce(idx[:, k:k + 1], pick[:, :], AX.X, ALU.min))
                link(V.tensor_scalar(eq[:, :], io[:, :], idx[:, k:k + 1], -4.0, ALU.is_equal, ALU.mult))
                link(V.tensor_tensor(rw[:, :], rw[:, :], eq[:, :], ALU.add))
            link(V.tensor_copy(idx_i[:, :], idx[:, :]))
            dve.sem_inc(i_s, 1)
            link(V.tensor_copy(lg[:, 0:2], top[:, :]))
            softmax(tw[:, :], 2)
            dve.sem_inc(tw_s, 1)
            dve.wait_ge(pw_s, 1)
            link(V.tensor_copy(twb[:, :], p_w[:, :]))
            dve.wait_ge(e_in, 10 * 16)
            for k in range(2):
                w = q.w2[:, k, :, :].rearrange("p k n -> p (k n)")
                link(V.tensor_scalar(w, w, twb[:, k:k + 1], None, ALU.mult))
                link(V.tensor_scalar(b2e[:, k, :], b2e[:, k, :], twb[:, k:k + 1], None, ALU.mult))
            link(V.tensor_tensor(q.b2[:, :], b2e[:, 0, :], b2e[:, 1, :], ALU.add))

        @block.scalar
        def _(act):
            for n in range(3):
                act.wait_ge(x_s, n + 1)
                nc.scalar.activation(ex[:, :], lg[:, :], ACT.Exp).then_inc(a_s, 1)

        @block.tensor
        def _(pe):
            pe.wait_ge(w_in, 48)
            for c in range(KC):
                last = nc.tensor.matmul(p_l[:, :], r.mean[:, c:c + 1], wr[:, c, :], start=(c == 0), stop=(c == KC - 1))
            last.then_inc(l_s, 1)
            pe.wait_ge(tw_s, 1)
            nc.tensor.matmul(p_w[:, :], one[:, :], tw[:, :], start=True, stop=True).then_inc(pw_s, 1)


def experts(nc, t, r, q, acc, spare):
    B = 2
    NF = NW // B
    FK = FF // P
    J = 2 * FK
    with Phase(nc, "ffn") as f:
        xT = f.sb("xT", [P, 2, KC, B * P])
        xf = f.sb("xf", [P, 2, B, C])
        hT = spare[:, 0:2 * J * B * P].rearrange("p (u j n) -> p u j n", u=2, j=J)
        o = f.sb("o", [P, 2, B, C])
        stats = Stats(nc, f, "y", B)
        p_f = f.ps("p_f", [P, 4, 512])
        p_y = f.ps("p_y", [P, 2, B, C])
        xT_in = f.sems("xT_in", 2)
        stored = f.sems("stored", 2)
        f_s, h_s, y_s, sum_s, norm_s, o_s, xf_s, xfb_s, st_link, norm_link = (f.sem(s) for s in (
            "f", "h", "y", "sum", "norm", "o", "xf", "xfb", "st_link", "norm_link"))
        block = f.ctx.enter_context(nc.Block())
        x2_of = lambda n: acc[:, bass.ds(n, 1), 0:C].rearrange("p a c -> p (a c)")

        @block.sync
        def _(sp):
            def load(i, u):
                sp.dma_start(xT[:, u, :, :], t["d_xfT"][:, :, bass.ds(i * (B * P), B * P)]).then_inc(xT_in[u], 16)

            def store(i, u):
                sp.wait_ge(o_s, i + 1)
                sp.dma_start(t["out"][bass.ds(i * (B * P), B * P), :].rearrange("(b p) n -> p b n", p=P),
                             o[:, u, :, :]).then_inc(stored[u], 16)

            def body(i, u, turn):
                if since(i, 2):
                    sp.wait_ge(f_s, i * J - J)
                load(i, u)
                if since(i, 2):
                    store(i - 2, u)

            run(sp, NF, 2, body)
            for i in range(NF - 2, NF):
                store(i, i % 2)
            for u in range(2):
                n = (NF + 1 - u) // 2
                sp.wait_ge(xT_in[u], 16 * n)
                sp.wait_ge(stored[u], 16 * n)

        @block.tensor
        def _(pe):
            def down(i, u):
                if since(i, 2):
                    pe.wait_ge(sum_s, i * B - B)
                for b in range(B):
                    for j in range(J):
                        pe.wait_ge(h_s, i * J + j + 1) if b == 0 else None
                        last = nc.tensor.matmul(p_y[:, u, b, :], hT[:, u, j, b * P:(b + 1) * P],
                                                q.w2[:, j // FK, j % FK, :], start=(j == 0), stop=(j == J - 1))
                last.then_inc(y_s, 1)

            def body(i, u, turn):
                pe.wait_ge(xT_in[u], turn * 16 + 16)
                for j in range(J):
                    if j >= 4 or since(i, 1):
                        pe.wait_ge(h_s, i * J + j - 3)
                    for k in range(KC):
                        last = nc.tensor.matmul(p_f[:, j % 4, 0:B * P], q.w1[:, j // FK, k, (j % FK) * P:(j % FK + 1) * P],
                                                xT[:, u, k, :], start=(k == 0), stop=(k == KC - 1))
                    last.then_inc(f_s, 1)
                if since(i, 1):
                    down(i - 1, 1 - u)

            run(pe, NF, 2, body)
            down(NF - 1, (NF - 1) % 2)

        @block.gpsimd
        def _(pool):
            def add_b2(n, u, b):
                pool.wait_ge(xf_s, n + 1)
                nc.gpsimd.tensor_tensor(xf[:, u, b, :], xf[:, u, b, :], q.b2[:, :], ALU.add).then_inc(xfb_s, 1)

            def finish(i, u):
                for b in range(B):
                    pool.wait_ge(norm_s, i * B + b + 1)
                    last = nc.gpsimd.tensor_tensor(o[:, u, b, :], o[:, u, b, :], x2_of(i * B + b), ALU.add)
                last.then_inc(o_s, 1)

            def body(i, u, turn):
                for b in range(B):
                    add_b2(i * B + b, u, b)
                if since(i, 1):
                    finish(i - 1, 1 - u)

            run(pool, NF, 2, body)
            finish(NF - 1, (NF - 1) % 2)

        @block.scalar
        def _(act):
            def body(i, u, turn):
                if since(i, 2):
                    act.wait_ge(y_s, i - 1)
                for j in range(J):
                    act.wait_ge(f_s, i * J + j + 1)
                    nc.scalar.activation(hT[:, u, j, :], p_f[:, j % 4, 0:B * P], ACT.Gelu,
                                         bias=q.b1[:, j // FK, j % FK:j % FK + 1]).then_inc(h_s, 1)

            run(act, NF, 2, body)

        @block.vector
        def _(dve):
            def normal_x2(i, u):
                if since(i, 2):
                    dve.wait_ge(xfb_s, i * B)
                for b in range(B):
                    n = i * B + b
                    nc.vector.tensor_scalar(xf[:, u, b, :], x2_of(n), r.mu[:, bass.ds(n, 1)], r.rs[:, bass.ds(n, 1)],
                                            ALU.subtract, ALU.mult).then_inc(xf_s, 1)

            def finish(i, u, turn):
                dve.wait_ge(y_s, i + 1)
                dve.wait_ge(xfb_s, i * B + B)
                if since(i, 2):
                    dve.wait_ge(stored[u], turn * 16)
                for b in range(B):
                    last = nc.vector.tensor_tensor(o[:, u, b, :], p_y[:, u, b, :], xf[:, u, b, :], ALU.add)
                    last.then_inc(sum_s, 1)
                dve.wait_ge(sum_s, i * B + B)
                dve.sem_inc(r.hold, 1)
                for b in range(B):
                    last = stats.take(u, b, o[:, u, b, :])
                stats.close(dve, Link(dve, st_link, i, 13), r.hold, u, last)
                for b in range(B):
                    last = nc.vector.scalar_tensor_tensor(o[:, u, b, :], o[:, u, b, :], stats.mean(u, b), q.g[:, :],
                                                          ALU.subtract, ALU.mult)
                Link(dve, norm_link, i, 1)(last)
                for b in range(B):
                    nc.vector.scalar_tensor_tensor(o[:, u, b, :], o[:, u, b, :], stats.scale(u, b), q.be[:, :],
                                                   ALU.mult, ALU.add).then_inc(norm_s, 1)

            def body(i, u, turn):
                normal_x2(i, u)
                if since(i, 1):
                    finish(i - 1, 1 - u, turn - 1 if u == 0 else turn)

            run(dve, NF, 2, body)
            finish(NF - 1, (NF - 1) % 2, (NF - 1) // 2)


class Tensors:
    pass


def gps_layer(nc, t):
    with Phase(nc, "all") as f:
        r = Tensors()
        r.ident, r.jrow, r.jcol = f.sb("ident", [P, P]), f.sb("jrow", [P, P]), f.sb("jcol", [P, 1])
        r.headsel, r.valid = f.sb("headsel", [P, KC * H]), f.sb("valid", [P, NW])
        r.hold, r.pool_hold = f.sem("hold"), f.sem("pool_hold")
        r.power = f.sb("power", [P, 2, BL])
        r.kvbd, r.mean = f.sb("kvbd", [P, KC, P + 4]), f.sb("mean", [P, KC])
        with Phase(nc, "lin") as g:
            r.wall = g.sb("wall", [P, KC, C + 2 * H])
            r.headmask = g.sb("headmask", [P, P])
            split_edge_features(nc, t)
            fold_attention_weights(nc, t, r)
            node_pass(nc, t, r)
        mixer(nc, t, r)
        with Phase(nc, "edge") as g:
            r.src = g.sb("src", [P, T], U32)
            r.dst = g.sb("dst", [P, T], I32)
            al = g.sb("al", [P, CE + 4])
            steps = Tensors()
            steps.g_int, steps.w_int = g.sb("g_int", [P, STEPS], I32), g.sb("w_int", [P, STEPS], I32)
            steps.w_node, steps.j_node = g.sb("w_node", [P, STEPS]), g.sb("j_node", [P, STEPS])
            steps.start = g.sb("start", [1, T // GT], I32)
            make_steps(nc, t, r, steps)
            load_indices(nc, t, r)
            with Phase(nc, "weights") as k:
                asrc = k.sb("asrc", [P, CE + 4])
                edge_scores(nc, t, r, steps, al, asrc)
                edge_softmax(nc, t, r, al, asrc)
            with Phase(nc, "acc") as k:
                acc = k.sb("acc", [P, NW, C + H])
                edge_sums(nc, t, r, steps, al, acc)
                r.mu, r.rs = k.sb("mu", [P, NW]), k.sb("rs", [P, NW])
                node_update(nc, t, r, acc, al)
                q = Tensors()
                q.w1 = al[:, 0:2 * KC * FF].rearrange("p (e k n) -> p e k n", e=2, k=KC)
                q.w2 = al[:, 2 * KC * FF:4 * KC * FF].rearrange("p (e k n) -> p e k n", e=2, n=C)
                q.b1, q.b2 = k.sb("b1", [P, 2, FF // P]), k.sb("b2", [P, C])
                q.g, q.be = k.sb("g", [P, C]), k.sb("be", [P, C])
                route(nc, t, r, q)
                experts(nc, t, r, q, acc, al[:, 4 * KC * FF:CE])


def split_edge_features(nc, t):
    A = P // EF
    L = EP // A
    with Phase(nc, "split") as f:
        x = f.sb("x", [P, L])
        hi = f.sb("hi", [P, L], F32R)
        lo = f.sb("lo", [P, L], F32R)
        w = f.sb("w", [EF, C])
        whi = f.sb("whi", [EF, C], F32R)
        wlo = f.sb("wlo", [EF, C], F32R)
        x_in, hi_s, lo_s, out_s = (f.sem(s) for s in ("x_in", "hi", "lo", "out"))
        block = f.ctx.enter_context(nc.Block())

        @block.sync
        def _(sp):
            sp.dma_start(w[:, :], t["ew"]).then_inc(x_in, 16)
            sp.dma_start(x[:, :], t["eaT"].rearrange("f (a l) -> (f a) l", a=A)).then_inc(x_in, 16)
            part = lambda n: t["d_ea"][n * EF:(n + 1) * EF, :].rearrange("f (a l) -> (f a) l", a=A)
            sp.wait_ge(hi_s, 2)
            sp.dma_start(part(0), hi[:, :].bitcast(F32)).then_inc(out_s, 16)
            sp.dma_start(part(2), hi[:, :].bitcast(F32)).then_inc(out_s, 16)
            sp.dma_start(t["d_ew"][0:EF, :], whi[:, :].bitcast(F32)).then_inc(out_s, 16)
            sp.dma_start(t["d_ew"][EF:2 * EF, :], whi[:, :].bitcast(F32)).then_inc(out_s, 16)
            sp.wait_ge(lo_s, 2)
            sp.dma_start(part(1), lo[:, :].bitcast(F32)).then_inc(out_s, 16)
            sp.dma_start(t["d_ew"][2 * EF:3 * EF, :], wlo[:, :].bitcast(F32)).then_inc(out_s, 16)
            sp.wait_ge(out_s, 6 * 16)

        @block.scalar
        def _(act):
            act.wait_ge(x_in, 32)
            nc.scalar.copy(whi[:, :], w[:, :]).then_inc(hi_s, 1)
            nc.scalar.copy(hi[:, :], x[:, :]).then_inc(hi_s, 1)

        @block.vector
        def _(dve):
            dve.wait_ge(hi_s, 2)
            nc.vector.tensor_tensor(wlo[:, :], w[:, :], whi[:, :].bitcast(F32), ALU.subtract).then_inc(lo_s, 1)
            nc.vector.tensor_tensor(lo[:, :], x[:, :], hi[:, :].bitcast(F32), ALU.subtract).then_inc(lo_s, 1)


def load_indices(nc, t, r):
    with Phase(nc, "idx") as f:
        loaded = f.sem("loaded")
        block = f.ctx.enter_context(nc.Block())

        @block.sync
        def _(sp):
            sp.dma_start(r.src[:, :], t["src_col"]).then_inc(loaded, 16)
            sp.dma_start(r.dst[:, :], t["dst_col"]).then_inc(loaded, 16)
            sp.wait_ge(loaded, 32)


def kernel(**inputs):
    import numpy as np
    import concourse.bacc as bacc
    from concourse.bass_utils import run_bass_kernel_spmd as launch

    a = {k: np.asarray(v) for k, v in inputs.items()}
    row = lambda v: np.ascontiguousarray(v.reshape(1, -1))
    turn = lambda v: np.ascontiguousarray(v.T)
    src = np.pad(a["src"], (0, EP - E))
    dst = np.pad(a["dst"], (0, EP - E), constant_values=NP - 1)
    head = np.arange(C) // D
    p = np.arange(P)
    arrays = {
        "x": np.pad(a["x"], ((0, NP + 2 * BL * P - N), (0, 0))),
        "src_col": turn(src.reshape(T, P)),
        "dst_col": turn(dst.reshape(T, P)),
        "dst_row": row(dst),
        "dst_ext": np.pad(row(dst), ((0, 0), (1, 1)), constant_values=-1),
        "last": np.ascontiguousarray(dst.reshape(NW, T // GT // NW, GT * P)[:, :, -1]),
        "eaT": np.concatenate([turn(np.pad(a["edge_attr_3"], ((0, EP - E), (0, 0)))), np.ones((1, EP), np.float32)]),
        "ew": np.concatenate([turn(a["L0_gnn_edge_W"]), row(a["L0_gnn_edge_b"])]),
        "w": a["L0_gnn_W"], "wT": turn(a["L0_gnn_W"]),
        "a_col": np.stack([a["L0_gnn_a_dst"].reshape(-1), a["L0_gnn_a_src"].reshape(-1)], 1),
        "bias": row(a["L0_gnn_bias"]),
        "wqkvT": turn(a["L0_mix_Wqkv"]), "w1T": turn(a["L0_mix_W1"]), "w2T": turn(a["L0_mix_W2"]),
        "b1_col": turn(a["L0_mix_b1"].reshape(KC, P)),
        "g1": row(a["L0_mix_ln1_g"]), "be1": row(a["L0_mix_ln1_b"]),
        "g1_col": turn(a["L0_mix_ln1_g"].reshape(KC, P)), "be1_col": turn(a["L0_mix_ln1_b"].reshape(KC, P)),
        "g2": row(a["L0_mix_ln2_g"]), "be2": row(a["L0_mix_ln2_b"]), "b2": row(a["L0_mix_b2"]),
        "wr": a["L0_ffn_Wr"], "br": row(a["L0_ffn_br"]),
        "ffn_w1": a["L0_ffn_W1"].reshape(XP * C, FF), "ffn_w2": a["L0_ffn_W2"].reshape(XP * FF, C),
        "ffn_b1": np.ascontiguousarray(a["L0_ffn_b1"].reshape(XP, FF // P, P).transpose(0, 2, 1)).reshape(XP * P, FF // P),
        "ffn_b2": a["L0_ffn_b2"], "ffn_g": row(a["L0_ffn_gamma"]), "ffn_be": row(a["L0_ffn_beta"]),
        "c_ident": np.eye(P, dtype=np.float32),
        "c_jrow": np.tile(p.astype(np.float32), (P, 1)),
        "c_jcol": p.astype(np.float32)[:, None],
        "c_headsel": (head.reshape(KC, P).T[:, :, None] == np.arange(H)).astype(np.float32).reshape(P, KC * H),
        "c_headmask": (p[:, None] // D == p[None, :] // D).astype(np.float32),
        "c_valid": (p[:, None] + P * np.arange(NW)[None, :] < N).astype(np.float32),
        "c_sidx": np.tile(np.arange(STEPS, dtype=np.float32), (P, 1)),
    }
    k = T // GT // NW
    arrays["c_gcol"] = 1.0 + np.arange(NW * k, dtype=np.float32).reshape(NW, k)
    scratch = {"d_xn": [NP, C], "d_h": [NP, C], "d_as": [NP, H], "d_q": [P, NW * C], "d_x1": [NP, C], "d_xb": [NP, C],
               "d_xfT": [P, KC, NP]}

    in_parts = {"d_hw": [NP, 2 * (C + H)], "d_ea": [3 * EF, EP], "d_ew": [3 * EF, C]}

    nc = bacc.Bacc("TRN2", target_bir_lowering=False, num_devices=1)
    feed, aps = {}, {}
    for name, v in arrays.items():
        v = np.ascontiguousarray(v)
        feed[f"in_{name}"] = v
        aps[name] = nc.dram_tensor(f"in_{name}", v.shape, mybir.dt.from_np(v.dtype), kind="ExternalInput").ap()
    for name, shape in scratch.items():
        aps[name] = nc.dram_tensor(name, shape, F32).ap()
    for name, shape in in_parts.items():
        aps[name] = nc.dram_tensor(name, shape, F32).ap()
    aps["d_start"] = nc.dram_tensor("d_start", [T // GT], I32).ap()
    aps["out"] = nc.dram_tensor("out", [NP, C], F32, kind="ExternalOutput").ap()
    aps["src_col"] = aps["src_col"].bitcast(U32)
    gps_layer(nc, aps)
    return launch(nc, [feed], core_ids=[0]).results[0]["out"][:N]
```
